# Optimizing a Trainium2 kernel written in Bass

```python
import numpy as np
import jax
import jax.numpy as jnp

def _softmax(x, axis=-1):
    return jax.nn.softmax(x, axis=axis)

def _gelu(x):
    return jax.nn.gelu(x, approximate=True)

def _silu(x):
    return jax.nn.silu(x)

def _sigmoid(x):
    return jax.nn.sigmoid(x)

def _layernorm(x, axis=-1, eps=1e-05):
    m = jnp.mean(x, axis=axis, keepdims=True)
    v = jnp.var(x, axis=axis, keepdims=True)
    return (x - m) / jnp.sqrt(v + eps)

def _scatter_add(tgt, idx, src, axis=0):
    return tgt.at[idx].add(src)

def _segment_sum(src, seg, n):
    return jax.ops.segment_sum(src, seg, n)
kernel_name = 'mk_hybrid_d1_jaxref_r8_871ede'

def setup_inputs(seed: int=0):
    np.random.seed(seed)
    _w = jnp.asarray

    def _L0_attn_a_setup():
        import jax, jax.numpy as jnp
        import numpy as np
        import math
        N_EMBD = 128
        N_HEAD = 16
        N_LAYER = 12
        key = jax.random.key(seed)
        kx, kw, kb = jax.random.split(key, 3)
        B, T, C = (4, 256, N_EMBD)
        x = jax.random.normal(kx, (B, T, C), dtype=jnp.float32)
        bound = 1.0 / math.sqrt(C)
        W = jax.random.uniform(kw, (3 * C, C), minval=-bound, maxval=bound, dtype=jnp.float32)
        W = W * (1.0 / math.sqrt(N_LAYER * 2))
        b = jax.random.uniform(kb, (3 * C,), minval=-bound, maxval=bound, dtype=jnp.float32)
        return {'x': x, 'W': W, 'b': b}
    _L0_attn_a_in = _L0_attn_a_setup()

    def _L0_attn_b_setup():
        import jax, jax.numpy as jnp
        import numpy as np
        B, T, C = (2, 512, 128)
        H, M, CHUNK = (16, 64, 128)
        D = C // H
        DELTA = 1e-06
        key = jax.random.key(seed)
        ks = jax.random.split(key, 4)
        x = jax.random.normal(ks[0], (B, T, C), dtype=jnp.float32)
        Wqkv = jax.random.normal(ks[1], (3 * C, C), dtype=jnp.float32) * 0.02
        bqkv = jnp.zeros((3 * C,), dtype=jnp.float32)
        Wout = jax.random.normal(ks[2], (C, C), dtype=jnp.float32) * 0.02
        bout = jnp.zeros((C,), dtype=jnp.float32)
        proj = jax.random.normal(ks[3], (H, D, M), dtype=jnp.float32) / np.sqrt(D)
        return {'x': x, 'Wqkv': Wqkv, 'bqkv': bqkv, 'Wout': Wout, 'bout': bout, 'proj': proj}
    _L0_attn_b_in = _L0_attn_b_setup()

    def _L0_ffn_setup():
        import jax, jax.numpy as jnp
        import numpy as np
        TOP_K = 2
        NUM_EXPERTS = 8
        key = jax.random.key(seed)
        ks = jax.random.split(key, 8)
        h, d, ds, E = (128, 64, 128, NUM_EXPERTS)
        s = 1.0 / np.sqrt(h)
        return {'x': jax.random.normal(ks[0], (2, 256, h), jnp.float32), 'router': jax.random.normal(ks[1], (h, E), jnp.float32) * s, 'experts_gate': jax.random.normal(ks[2], (E, h, d), jnp.float32) * s, 'experts_up': jax.random.normal(ks[3], (E, h, d), jnp.float32) * s, 'experts_down': jax.random.normal(ks[4], (E, d, h), jnp.float32) * (1.0 / np.sqrt(d)), 'shared_gate': jax.random.normal(ks[5], (h, ds), jnp.float32) * s, 'shared_up': jax.random.normal(ks[6], (h, ds), jnp.float32) * s, 'shared_down': jax.random.normal(ks[7], (ds, h), jnp.float32) * (1.0 / np.sqrt(ds))}
    _L0_ffn_in = _L0_ffn_setup()
    _d = {'L0_attn_a_x': _L0_attn_a_in['x'], 'L0_attn_a_W': _L0_attn_a_in['W'], 'L0_attn_a_b': _L0_attn_a_in['b'], 'L0_attn_b_Wqkv': _L0_attn_b_in['Wqkv'], 'L0_attn_b_bqkv': _L0_attn_b_in['bqkv'], 'L0_attn_b_Wout': _L0_attn_b_in['Wout'], 'L0_attn_b_bout': _L0_attn_b_in['bout'], 'L0_attn_b_proj': _L0_attn_b_in['proj'], 'L0_ffn_router': _L0_ffn_in['router'], 'L0_ffn_experts_gate': _L0_ffn_in['experts_gate'], 'L0_ffn_experts_up': _L0_ffn_in['experts_up'], 'L0_ffn_experts_down': _L0_ffn_in['experts_down'], 'L0_ffn_shared_gate': _L0_ffn_in['shared_gate'], 'L0_ffn_shared_up': _L0_ffn_in['shared_up'], 'L0_ffn_shared_down': _L0_ffn_in['shared_down']}
    _x0 = _d['L0_attn_a_x']
    _d['L0_attn_a_x'] = jax.random.normal(jax.random.fold_in(jax.random.key(seed), 1), (16, 512, 128), dtype=_x0.dtype)
    del _x0
    return _d

def reference(L0_attn_a_x, L0_attn_a_W, L0_attn_a_b, L0_attn_b_Wqkv, L0_attn_b_bqkv, L0_attn_b_Wout, L0_attn_b_bout, L0_attn_b_proj, L0_ffn_router, L0_ffn_experts_gate, L0_ffn_experts_up, L0_ffn_experts_down, L0_ffn_shared_gate, L0_ffn_shared_up, L0_ffn_shared_down):

    def _L0_attn_a_ref(x, W, b):
        import jax, jax.numpy as jnp
        import numpy as np
        import math
        N_EMBD = 128
        N_HEAD = 16
        N_LAYER = 12
        B, T, C = x.shape
        H = N_HEAD
        D = C // H
        qkv = jnp.einsum('btc,oc->bto', x, W) + b
        q, k, v = jnp.split(qkv, 3, axis=-1)
        q = q.reshape(B, T, H, D).transpose(0, 2, 1, 3)
        k = k.reshape(B, T, H, D).transpose(0, 2, 1, 3)
        v = v.reshape(B, T, H, D).transpose(0, 2, 1, 3)
        att = jnp.einsum('bhtd,bhsd->bhts', q, k) / math.sqrt(D)
        causal = jnp.tril(jnp.ones((T, T), dtype=bool))
        att = jnp.where(causal, att, -jnp.inf)
        att = jax.nn.softmax(att, axis=-1)
        y = jnp.einsum('bhts,bhsd->bhtd', att, v)
        return y.transpose(0, 2, 1, 3).reshape(B, T, C)

    def _L0_attn_b_ref(x, Wqkv, bqkv, Wout, bout, proj):
        import jax, jax.numpy as jnp
        import numpy as np
        B, T, C = (2, 512, 128)
        H, M, CHUNK = (16, 64, 128)
        D = C // H
        DELTA = 1e-06
        b, t, c = x.shape
        qkv = x @ Wqkv.T + bqkv
        q, k, v = jnp.split(qkv, 3, axis=-1)

        def to_heads(z):
            return z.reshape(b, t, H, D).transpose(0, 2, 1, 3).astype(jnp.float32)
        q, k, v = (to_heads(q), to_heads(k), to_heads(v))
        nch = t // CHUNK

        def to_chunks(z):
            return z.reshape(b, H, nch, CHUNK, D).transpose(2, 0, 1, 3, 4)
        qc, kc, vc = (to_chunks(q), to_chunks(k), to_chunks(v))
        mask = jnp.tril(jnp.ones((CHUNK, CHUNK), dtype=jnp.float32))

        def step(carry, inp):
            kv_state, k_state = carry
            q_ch, k_ch, v_ch = inp
            qp = jax.nn.relu(jnp.einsum('bhtd,hdm->bhtm', q_ch, proj))
            kp = jax.nn.relu(jnp.einsum('bhtd,hdm->bhtm', k_ch, proj))
            ctx_hist = jnp.einsum('bhtm,bhmd->bhtd', qp, kv_state)
            norm_hist = jnp.einsum('bhtm,bhm->bht', qp, k_state)
            aw = jnp.einsum('bhtm,bhsm->bhts', qp, kp) * mask
            ctx_intra = jnp.einsum('bhts,bhsd->bhtd', aw, v_ch)
            norm_intra = aw.sum(-1)
            out = (ctx_hist + ctx_intra) / (norm_hist + norm_intra + DELTA)[..., None]
            new_kv = kv_state + jnp.einsum('bhtm,bhtd->bhmd', kp, v_ch)
            new_k = k_state + kp.sum(2)
            return ((new_kv, new_k), out)
        carry0 = (jnp.zeros((b, H, M, D), jnp.float32), jnp.zeros((b, H, M), jnp.float32))
        _, outs = jax.lax.scan(step, carry0, (qc, kc, vc))
        out = outs.transpose(1, 2, 0, 3, 4).reshape(b, H, t, D)
        out = out.transpose(0, 2, 1, 3).reshape(b, t, c)
        return out @ Wout.T + bout

    def _L0_ffn_ref(x, router, experts_gate, experts_up, experts_down, shared_gate, shared_up, shared_down):
        import jax, jax.numpy as jnp
        import numpy as np
        TOP_K = 2
        NUM_EXPERTS = 8
        b, s, h = x.shape
        E = router.shape[1]
        shared_act = jax.nn.silu(jnp.einsum('bsh,hd->bsd', x, shared_gate))
        shared_up_out = jnp.einsum('bsh,hd->bsd', x, shared_up)
        shared_out = jnp.einsum('bsd,dh->bsh', shared_act * shared_up_out, shared_down)
        router_probs = jax.nn.softmax(jnp.einsum('bsh,he->bse', x, router), axis=-1)
        topk_probs, topk_idx = jax.lax.top_k(router_probs, TOP_K)
        coef = jnp.sum(jax.nn.one_hot(topk_idx, E, dtype=x.dtype) * topk_probs[..., None], axis=2)
        coef = coef.reshape(b * s, E)
        x_flat = x.reshape(b * s, h)
        gate = jnp.einsum('th,ehd->etd', x_flat, experts_gate)
        up = jnp.einsum('th,ehd->etd', x_flat, experts_up)
        expert_out = jnp.einsum('etd,edh->eth', jax.nn.silu(gate) * up, experts_down)
        routed = jnp.einsum('eth,te->th', expert_out, coef)
        return routed.reshape(b, s, h) + shared_out
    x = L0_attn_a_x
    x = x + _L0_attn_a_ref(_layernorm(x, axis=-1), L0_attn_a_W, L0_attn_a_b)
    x = x + _L0_ffn_ref(_layernorm(x, axis=-1), L0_ffn_router, L0_ffn_experts_gate, L0_ffn_experts_up, L0_ffn_experts_down, L0_ffn_shared_gate, L0_ffn_shared_up, L0_ffn_shared_down)
    x = x + _L0_attn_b_ref(_layernorm(x, axis=-1), L0_attn_b_Wqkv, L0_attn_b_bqkv, L0_attn_b_Wout, L0_attn_b_bout, L0_attn_b_proj)
    x = x + _L0_ffn_ref(_layernorm(x, axis=-1), L0_ffn_router, L0_ffn_experts_gate, L0_ffn_experts_up, L0_ffn_experts_down, L0_ffn_shared_gate, L0_ffn_shared_up, L0_ffn_shared_down)
    return x

_drawn_inputs = setup_inputs


def setup_inputs(seed=0):
    import zlib

    import numpy as np

    out = dict(_drawn_inputs(seed))
    spreads = {'L0_attn_b_bqkv': (0.0, 0.341), 'L0_attn_b_bout': (0.0, 0.1)}
    factors = {'L0_attn_b_Wqkv': 5.532, 'L0_attn_b_proj': 8.0}
    for name, (base, spread) in spreads.items():
        noise = np.random.default_rng([zlib.crc32(name.encode()), seed]).standard_normal(out[name].shape)
        drawn = base * np.exp(spread * noise) if base else spread * noise
        out[name] = jnp.asarray(drawn.astype(out[name].dtype))
    for name, factor in factors.items():
        out[name] = (out[name] * factor).astype(out[name].dtype)
    return out
```

```python
import numpy as np
import concourse.bass as bass
from concourse import mybir
from contextlib import ExitStack

F32 = mybir.dt.float32
BF16 = mybir.dt.bfloat16
ACT = mybir.ActivationFunctionType
ALU = mybir.AluOpType
AX = mybir.AxisListType

NB, T, C = 16, 512, 128
H, D = 16, 8
TILES = T // 128
HL = 8
PARTS = 3
ROWS = PARTS * PARTS * D
KROWS = 96
MROWS = KROWS + PARTS
E, ED = 8, 64
M = 64
EPS = 1e-5
DELTA = 1e-6
SCALE = float(D) ** -0.5
NEG = -1e30
ORDER = [0, 2, 4, 6, 1, 3, 5, 7]


def upto(i, per, const):
    value = i * per + const
    return max(value, 0) if isinstance(i, int) else value


class Common:
    pass


def allocate_common(nc, ctx):
    g = Common()

    def sb(name, shape, dt=F32):
        return ctx.enter_context(nc.sbuf_tensor(name, shape, dt))

    g.passed_sp = ctx.enter_context(nc.semaphore("passed_sp"))
    g.passed_pool = ctx.enter_context(nc.semaphore("passed_pool"))
    g.passed_dve = ctx.enter_context(nc.semaphore("passed_dve"))
    g.x_all = sb("x_all", [128, NB, TILES, C])
    g.ident = sb("ident", [128, 128])
    g.ident_bf = sb("ident_bf", [128, 128], BF16)
    g.mask_neg = sb("mask_neg", [128, 128], BF16)
    g.causal01 = sb("causal01", [128, 128])
    g.pair_mask = sb("pair_mask", [128, 32])
    g.earlier = sb("earlier", [128, E, E])
    g.half_power = sb("half_power", [128, TILES])
    g.weights_t = sb("weights_t", [128, 7, 128])
    g.qk_bias = sb("qk_bias", [128, 4])
    g.row_bias = sb("row_bias", [128, 3, TILES, C])
    g.proj = sb("proj", [KROWS, H, 3 * M], BF16)
    g.w_gate = sb("w_gate", [128, 5, 128])
    g.w_up = sb("w_up", [128, 5, 128])
    g.w_down = sb("w_down", [128, 5, 128])
    g.w_router = sb("w_router", [128, E])
    g.select = sb("select", [KROWS, E, ED], BF16)
    return g


def emit_setup(nc, g, x, a_w, a_b, b_w, b_b, out_w, out_b, proj, router, gate, up, down, s_gate, s_up, s_down):
    with ExitStack() as ctx:
        sb = lambda name, shape, dt=F32: ctx.enter_context(nc.sbuf_tensor(name, shape, dt))
        sem = lambda name: ctx.enter_context(nc.semaphore(name))
        w_rows = sb("w_rows", [128, 7, 128])
        bias_rows = sb("bias_rows", [1, 3, 128])
        ones_row = sb("ones_row", [1, 128])
        pj = sb("pj", [D, H, M])
        pj_left = sb("pj_left", [D, H, M])
        pj_parts = sb("pj_parts", [D, PARTS, H, M], BF16)
        ps_w = [ctx.enter_context(nc.psum_tensor(f"ps_w{n}", [128, 4, 128], F32)) for n in range(3)]
        x_first = sem("x_first")
        weights_in = sem("weights_in")
        ffn_in = sem("ffn_in")
        x_rest = sem("x_rest")
        proj_in = sem("proj_in")
        filled = sem("filled")
        cleared = sem("cleared")
        select_first = sem("select_first")
        select_stacked = sem("select_stacked")
        constants = sem("constants")
        idents = sem("idents")
        ones_set = sem("ones_set")
        transposed = sem("transposed")
        biases_up = sem("biases_up")
        proj_step = sem("proj_step")
        proj_zeroed = sem("proj_zeroed")
        proj_stacked = sem("proj_stacked")
        copied = sem("copied")

        x_v = x.rearrange("b (j p) c -> p b j c", p=128)
        qk = lambda w, part, f: w[128 * part + 64 * f:128 * part + 64 * f + 64]
        with nc.Block() as block:

            @block.sync
            def _(sp):
                for m, (w, part) in enumerate(((a_w, 0), (a_w, 1), (b_w, 0), (b_w, 1))):
                    for f in range(2):
                        sp.dma_start(w_rows[64 * f:64 * f + 64, m, :],
                                     qk(w, part, f).rearrange("(l d) c -> d l c", d=D)).then_inc(weights_in, 16)
                for m, w in ((4, a_w[256:384, :]), (5, b_w[256:384, :]), (6, out_w)):
                    sp.dma_start(w_rows[:, m, :], w).then_inc(weights_in, 16)
                for m, (b, part) in enumerate(((a_b, 0), (a_b, 1), (b_b, 0), (b_b, 1))):
                    for f in range(2):
                        sp.dma_start(g.qk_bias[64 * f:64 * f + 64, m:m + 1],
                                     qk(b, part, f).rearrange("(l d c) -> d l c", d=D, c=1),
                                     allow_slow_non_contiguous=True).then_inc(weights_in, 16)
                for m, b in enumerate((a_b[256:384], b_b[256:384], out_b)):
                    sp.dma_start(bias_rows[:, m, :], b.rearrange("(a n) -> a n", a=1)).then_inc(weights_in, 16)
                sp.dma_start(pj[:, :, :], proj.rearrange("h d m -> d h m")).then_inc(proj_in, 16)
                for q in range(1, 4):
                    sp.dma_start(g.x_all[:, 4 * q:4 * q + 4], x_v[:, 4 * q:4 * q + 4]).then_inc(x_rest, 16)
                sp.wait_ge(proj_step, 5)
                sp.wait_ge(proj_zeroed, 1)
                for i in range(PARTS):
                    for j in range(PARTS):
                        row = PARTS * D * i + D * j
                        sp.dma_start(g.proj[row:row + D, :, M:2 * M], pj_parts[:, j, :, :]).then_inc(proj_stacked, 16)
                sp.wait_ge(select_first, 1)
                for n in range(1, PARTS):
                    sp.dma_start(g.select[E * n:E * n + E, :, :], g.select[0:E, :, :]).then_inc(select_stacked, 16)
                sp.wait_ge(select_stacked, 16 * (PARTS - 1))
                sp.wait_ge(proj_stacked, 16 * PARTS * PARTS)
                sp.wait_ge(x_rest, 48)
                sp.wait_ge(x_first, 16)
                sp.wait_ge(ffn_in, 16 * 7)

            @block.scalar
            def _(act):
                act.dma_start(g.x_all[:, 0:4], x_v[:, 0:4]).then_inc(x_first, 16)
                for dst, w in ((g.w_gate, gate), (g.w_up, up)):
                    act.dma_start(dst[:, 0:4, :].rearrange("c n (e d) -> c (n e) d", e=2),
                                  w.rearrange("e c d -> c e d")).then_inc(ffn_in, 16)
                act.dma_start(g.w_gate[:, 4, :], s_gate).then_inc(ffn_in, 16)
                act.dma_start(g.w_up[:, 4, :], s_up).then_inc(ffn_in, 16)
                act.dma_start(g.w_down[:, 0:4, :], down.rearrange("(n e) d h -> (e d) n h", e=2)).then_inc(ffn_in, 16)
                act.dma_start(g.w_down[:, 4, :], s_down).then_inc(ffn_in, 16)
                act.dma_start(g.w_router[:, :], router).then_inc(ffn_in, 16)
                act.wait_ge(transposed, 7)
                act.activation(g.weights_t[:, 0:4, :], ps_w[0][:, :, :], ACT.Copy).then_inc(copied, 1)
                act.activation(g.weights_t[:, 4:7, :], ps_w[1][:, 0:3, :], ACT.Copy).then_inc(copied, 1)

            @block.gpsimd
            def _(pool):
                pool.memset(g.ident[:, :], 0.0).then_inc(filled, 1)
                pool.memset(g.mask_neg[:, :], 0.0).then_inc(filled, 1)
                pool.memset(g.causal01[:, :], 1.0).then_inc(filled, 1)
                pool.wait_ge(filled, 3)
                pool.affine_select(out=g.ident[:, :], in_=g.ident[:, :], compare_op=ALU.not_equal, fill=1.0,
                                   base=0, pattern=[[-1, 128]], channel_multiplier=1).then_inc(idents, 1)
                pool.affine_select(out=g.mask_neg[:, :], in_=g.mask_neg[:, :], compare_op=ALU.is_ge, fill=NEG,
                                   base=0, pattern=[[-1, 128]], channel_multiplier=1).then_inc(constants, 1)
                pool.affine_select(out=g.causal01[:, :], in_=g.causal01[:, :], compare_op=ALU.is_ge, fill=0.0,
                                   base=0, pattern=[[1, 128]], channel_multiplier=-1).then_inc(constants, 1)
                pool.memset(g.half_power[:, :], -0.5).then_inc(constants, 1)

            @block.vector
            def _(dve):
                dve.memset(ones_row[:, :], 1.0).then_inc(ones_set, 1)
                dve.memset(g.proj[:, :, :].bitcast(F32), 0.0).then_inc(proj_zeroed, 1)
                dve.memset(g.earlier[:, :, :], 0.0).then_inc(cleared, 1)
                dve.memset(g.pair_mask[:, :], 0.0).then_inc(cleared, 1)
                dve.memset(g.select[:, :, :].bitcast(F32), 0.0).then_inc(cleared, 1)
                dve.wait_ge(cleared, 3)
                for e in range(1, E):
                    dve.memset(g.earlier[:, e, 0:e], 1.0).then_inc(constants, 1)
                for r in range(2):
                    dve.memset(g.pair_mask[M * r:M * r + M, 16 * r:16 * r + 16], 1.0).then_inc(constants, 1)
                dve.wait_ge(idents, 1)
                dve.tensor_copy(g.ident_bf[:, :], g.ident[:, :]).then_inc(constants, 1)
                dve.tensor_copy(g.select[0:E, :, :], g.ident[0:E, 0:E].unsqueeze(2).to_broadcast([E, E, ED]))\
                    .then_inc(select_first, 1)
                dve.wait_ge(proj_in, 16)
                dve.tensor_copy(pj_parts[:, 0], pj[:, :, :]).then_inc(proj_step, 1)
                dve.wait_ge(proj_step, 1)
                dve.tensor_tensor(pj_left[:, :, :], pj[:, :, :], pj_parts[:, 0], ALU.subtract).then_inc(proj_step, 1)
                dve.wait_ge(proj_step, 2)
                dve.tensor_copy(pj_parts[:, 1], pj_left[:, :, :]).then_inc(proj_step, 1)
                dve.wait_ge(proj_step, 3)
                dve.tensor_tensor(pj[:, :, :], pj_left[:, :, :], pj_parts[:, 1], ALU.subtract).then_inc(proj_step, 1)
                dve.wait_ge(proj_step, 4)
                dve.tensor_copy(pj_parts[:, 2], pj[:, :, :]).then_inc(proj_step, 1)
                dve.wait_ge(biases_up, 1)
                for m in range(3):
                    dve.tensor_copy(g.row_bias[:, m],
                                    ps_w[2][:, m:m + 1, :].to_broadcast([128, TILES, C])).then_inc(copied, 1)

            @block.tensor
            def _(pe):
                pe.wait_ge(weights_in, 16 * 22)
                pe.wait_ge(idents, 1)
                for m in range(7):
                    pe.transpose(ps_w[m // 4][:, m % 4, :], w_rows[:, m, :], g.ident[:, :]).then_inc(transposed, 1)
                pe.wait_ge(ones_set, 1)
                for m in range(3):
                    last = pe.matmul(ps_w[2][:, m, :], ones_row[:, :], bias_rows[:, m, :], start=True, stop=True)
                last.then_inc(biases_up, 1)


def emit_softmax_attention(nc, g):
    AHEAD = 6
    PP = 5
    PU, PB = 4, 8
    NP = NB * PB
    NU = 2 * NB
    STACK_DMAS = 2 * PARTS * PARTS
    with ExitStack() as ctx:
        sb = lambda name, shape, dt=F32: ctx.enter_context(nc.sbuf_tensor(name, shape, dt))
        ps = lambda name, shape, dt=F32: ctx.enter_context(nc.psum_tensor(name, shape, dt))
        sem = lambda name: ctx.enter_context(nc.semaphore(name))
        q_stack = [sb(f"q_stack{n}", [MROWS, HL, T], BF16) for n in range(4)]
        k_stack = [sb(f"k_stack{n}", [MROWS, HL, T], BF16) for n in range(4)]
        probs = sb("probs", [128, 2, 4, 3 * 512])
        v_aug = [sb(f"v_aug{n}", [128, TILES, H, 32]) for n in range(2)]
        parts = sb("parts", [128, 2, PARTS, T], BF16)
        qk_full = sb("qk_full", [128, 2, T])
        xn = sb("xn", [128, TILES, C])
        xn_t = sb("xn_t", [128, T])
        ln_stats = sb("ln_stats", [128, TILES, 6])
        ln_mv = sb("ln_mv", [128, TILES, 2])
        ln_var = sb("ln_var", [128, TILES])
        ln_rstd = sb("ln_rstd", [128, TILES])
        row_max = sb("row_max", [128, 2, TILES, HL])
        max_left = sb("max_left", [128, TILES, HL])
        max_parts = sb("max_parts", [128, TILES, PARTS, HL], BF16)
        max_rows = sb("max_rows", [PARTS * HL, T], BF16)
        y_cols = sb("y_cols", [128, T])
        y_recip = sb("y_recip", [128, TILES * HL])
        y_norm = sb("y_norm", [128, TILES * HL, D])
        ps_max = [ps(f"ps_max{n}", [128, 512]) for n in range(2)]
        ps_exp = [ps(f"ps_exp{n}", [128, 512]) for n in range(3)]
        ps_pv = ps("ps_pv", [128, 512])
        ps_build = ps("ps_build", [128, 512])
        ps_turn = ps("ps_turn", [128, 512])
        turn_bf = ps_turn[:, :].bitcast(BF16)

        zeroed = sem("a_zeroed")
        ones_set = sem("a_ones_set")
        stats_done = sem("a_stats_done")
        mv_done = sem("a_mv_done")
        var_done = sem("a_var_done")
        rstd_done = sem("a_rstd_done")
        xn_done = sem("a_xn_done")
        xn_turned = sem("a_xn_turned")
        xn_t_done = sem("a_xn_t_done")
        qk_done = sem("a_qk_done")
        qk_full_done = sem("a_qk_full_done")
        left1_done = sem("a_left1_done")
        mid_done = sem("a_mid_done")
        low_done = sem("a_low_done")
        v_done = sem("a_v_done")
        v_aug_done = sem("a_v_aug_done")
        stacked = [sem(f"a_stacked{f}") for f in range(2)]
        rows_scored = sem("a_rows_scored")
        rows_reduced = sem("a_rows_reduced")
        max_step = sem("a_max_step")
        max_turned = sem("a_max_turned")
        max_rows_done = sem("a_max_rows_done")
        max_stacked = [sem(f"a_max_stacked{f}") for f in range(2)]
        cols_scored = sem("a_cols_scored")
        exp_done = sem("a_exp_done")
        masked = sem("a_masked")
        pv_done = sem("a_pv_done")
        y_cols_done = sem("a_y_cols_done")
        y_turned = sem("a_y_turned")
        y_recip_done = sem("a_y_recip_done")
        y_norm_done = sem("a_y_norm_done")
        x_added = sem("a_x_added")

        LOOPS = NP // 16 - 2
        TAIL = 8

        def run(eng, step):
            for s in range(-12, TAIL):
                step(0, s)
            with eng.Fori(0, LOOPS) as i:
                for s in range(TAIL, TAIL + 16):
                    step(i, s)
            for s in range(TAIL, NP - 16 * LOOPS + 3):
                step(LOOPS, s)

        def falls(i, s, every, offset, count):
            if (s - offset) % every:
                return None
            n = (s - offset) // every
            if isinstance(i, int) and not 0 <= i * (16 // every) + n < count:
                return None
            return n

        COLS = {0: 0, 1: 512, 3: 896, 2: 1024}

        with nc.Block() as block:

            @block.sync
            def _(sp):
                sp.wait_ge(zeroed, 8)

                def step(i, s):
                    u = falls(i, s, 4, -1, NU)
                    if u is not None:
                        f = u % 2
                        sp.wait_ge(max_rows_done, upto(i, 4, u + 1))
                        sp.sem_inc(g.passed_sp, 1)
                        sp.dma_start(q_stack[u % 4][KROWS:MROWS, :, :], max_rows[:, :]).then_inc(max_stacked[f], 16)
                    b = falls(i, s, 8, -8, NB)
                    if b is not None:
                        sp.wait_ge(low_done, upto(i, 4, 2 * b + 2))
                        sp.sem_inc(g.passed_sp, 1)
                        for f in range(2):
                            u = 2 * b + f
                            sp.wait_ge(cols_scored, upto(i, PP * 16, PP * PU * (u - 3)))
                            sp.sem_inc(g.passed_sp, 1)
                            sp.wait_ge(stacked[f], upto(i, 2 * 16 * STACK_DMAS, 16 * STACK_DMAS * b))
                            sp.sem_inc(g.passed_sp, 1)
                            for n in range(PARTS):
                                for c in range(PARTS):
                                    row = PARTS * D * n + D * c
                                    sp.dma_start(q_stack[u % 4][row:row + D, :, :],
                                                 parts[64 * f:64 * f + 64, 0, n, :]).then_inc(stacked[f], 16)
                                    row = PARTS * D * c + D * n
                                    sp.dma_start(k_stack[u % 4][row:row + D, :, :],
                                                 parts[64 * f:64 * f + 64, 1, n, :]).then_inc(stacked[f], 16)

                run(sp, step)

            @block.gpsimd
            def _(pool):
                def step(i, s):
                    b = falls(i, s, 8, -12, NB)
                    if b is not None:
                        pool.wait_ge(mv_done, upto(i, 2, b + 1))
                        pool.sem_inc(g.passed_pool, 1)
                        pool.tensor_scalar(ln_var[:, :], ln_mv[:, :, 1], EPS, 1.0, ALU.add, ALU.mult)\
                            .then_inc(var_done, 1)
                        pool.wait_ge(var_done, upto(i, 2, b + 1))
                        pool.sem_inc(g.passed_pool, 1)
                        pool.wait_ge(xn_done, upto(i, 2, b))
                        pool.sem_inc(g.passed_pool, 1)
                        pool.tensor_tensor(ln_rstd[:, :], ln_var[:, :], g.half_power[:, :], ALU.pow)\
                            .then_inc(rstd_done, 1)
                    for n in range(2):
                        b = falls(i, s, 8, -10 + n, NB)
                        if b is not None:
                            pool.wait_ge(qk_full_done, upto(i, 8, 4 * b + 2 * n + 2))
                            pool.sem_inc(g.passed_pool, 1)
                            pool.tensor_tensor(qk_full[:, n, :], qk_full[:, n, :], parts[:, n, 0, :], ALU.subtract)\
                                .then_inc(left1_done, 1)
                            pool.wait_ge(mid_done, upto(i, 4, 2 * b + n + 1))
                            pool.sem_inc(g.passed_pool, 1)
                            pool.tensor_tensor(parts[:, n, 2, :], qk_full[:, n, :], parts[:, n, 1, :], ALU.subtract)\
                                .then_inc(low_done, 1)
                    p = falls(i, s, 1, 0, NP)
                    if p is not None:
                        pool.wait_ge(exp_done, upto(i, PP * 16, PP * (p + 1)))
                        pool.sem_inc(g.passed_pool, 1)
                        two = probs[:, p // 2 % 2, 2 * (p % 2):2 * (p % 2) + 2, :]
                        tri = dict(compare_op=ALU.is_ge, fill=0.0, base=0, channel_multiplier=-1)
                        d012 = two.rearrange("p h (n c) -> p (h n) c", c=512)[:, :, 0:128]
                        pool.affine_select(out=d012, in_=d012, pattern=[[0, 6], [1, 128]], **tri)\
                            .then_inc(masked, 1)
                        d3 = two[:, :, 896:1024]
                        pool.affine_select(out=d3, in_=d3, pattern=[[0, 2], [1, 128]], **tri).then_inc(masked, 1)
                    u = falls(i, s, 4, 6, NU)
                    if u is not None:
                        pool.wait_ge(y_norm_done, upto(i, 4, u + 1))
                        pool.sem_inc(g.passed_pool, 1)
                        b = u // 2
                        tile = x_slot(g, i, b)[:, :, 64 * (u % 2):64 * (u % 2) + 64]
                        pool.tensor_tensor(tile, tile, y_norm[:, :, :].rearrange("p (j h) d -> p j (h d)", j=TILES),
                                           ALU.add).then_inc(x_added, 1)

                run(pool, step)

            @block.scalar
            def _(act):
                def step(i, s):
                    b = falls(i, s, 8, -11, NB)
                    if b is not None:
                        act.wait_ge(xn_turned, upto(i, 2, b + 1))
                        act.wait_ge(v_done, upto(i, 2, b))
                        act.activation(xn_t[:, :], ps_build[:, :], ACT.Copy).then_inc(xn_t_done, 1)
                    for n in range(2):
                        b = falls(i, s, 8, -10 + n, NB)
                        if b is not None:
                            act.wait_ge(qk_done, upto(i, 4, 2 * b + n + 1))
                            act.wait_ge(low_done, upto(i, 4, 2 * b))
                            for f in range(2):
                                act.wait_ge(stacked[f], upto(i, 2 * 16 * STACK_DMAS, 16 * STACK_DMAS * b))
                            act.activation(qk_full[:, n, :], ps_build[:, :], ACT.Identity,
                                           bias=g.qk_bias[:, n:n + 1]).then_inc(qk_full_done, 1)
                            act.activation(parts[:, n, 0, :], ps_build[:, :], ACT.Identity,
                                           bias=g.qk_bias[:, n:n + 1]).then_inc(qk_full_done, 1)
                    u = falls(i, s, 4, 5, NU)
                    if u is not None:
                        act.wait_ge(pv_done, upto(i, 8, 2 * u + 2))
                        act.wait_ge(y_turned, upto(i, 4, u))
                        act.activation(y_cols[:, :], ps_pv[:, :], ACT.Copy).then_inc(y_cols_done, 1)
                    p = falls(i, s, 1, 0, NP)
                    if p is not None:
                        quad = p // 2
                        if p % 2 == 0:
                            act.wait_ge(pv_done, upto(i, 8, quad - 1))
                        row = probs[:, quad % 2]
                        for n in range(PP):
                            act.wait_ge(cols_scored, upto(i, PP * 16, PP * p + n + 1))
                            slot = 2 * (p % 2) + n // 2
                            if n == PP - 1:
                                dst = row[:, 2 * (p % 2):2 * (p % 2) + 2, 1024:1280]
                                src = ps_exp[2][:, :].rearrange("p (h t) -> p h t", h=2)
                            else:
                                dst = row[:, slot, 512 * (n % 2):512 * (n % 2) + 512]
                                src = ps_exp[n % 2][:, :]
                            act.activation(dst, src, ACT.Exp, scale=SCALE).then_inc(exp_done, 1)
                    for n in range(2):
                        b = falls(i, s, 8, -10 + n, NB)
                        if b is not None:
                            act.wait_ge(left1_done, upto(i, 4, 2 * b + n + 1))
                            act.activation(parts[:, n, 1, :], qk_full[:, n, :], ACT.Copy).then_inc(mid_done, 1)
                    u = falls(i, s, 4, -2, NU)
                    if u is not None:
                        act.wait_ge(max_turned, upto(i, 4, u + 1))
                        act.wait_ge(max_stacked[(u - 1) % 2], upto(i, 32, 16 * ((u + 1) // 2)))
                        act.activation(max_rows[:, :], turn_bf[0:PARTS * HL, 0:512], ACT.Copy)\
                            .then_inc(max_rows_done, 1)

                run(act, step)

            @block.vector
            def _(dve):
                for n in range(4):
                    dve.memset(q_stack[n][64:KROWS, :, :].bitcast(F32), 0.0).then_inc(zeroed, 1)
                    dve.memset(k_stack[n][64:KROWS, :, :].bitcast(F32), 0.0).then_inc(zeroed, 1)
                    dve.memset(k_stack[n][KROWS:MROWS, :, :], 1.0).then_inc(ones_set, 1)
                for n in range(2):
                    dve.memset(v_aug[n][:, :, :, :], 0.0).then_inc(zeroed, 1)
                dve.wait_ge(zeroed, 10)
                for n in range(2):
                    for r in range(2):
                        pairs = v_aug[n][:, :, :, :].rearrange("p j (q r) w -> p (j q) r w", r=2)
                        dve.memset(pairs[:, :, r, 16 * r + D:16 * r + D + 1], 1.0).then_inc(ones_set, 1)

                def step(i, s):
                    b = falls(i, s, 8, -12, NB)
                    if b is not None:
                        emit_ln_stats(dve, g, i, b, ln_stats, ln_mv, stats_done, mv_done)
                    b = falls(i, s, 8, -6, NB)
                    if b is not None:
                        dve.wait_ge(v_done, upto(i, 2, b + 1))
                        dve.wait_ge(pv_done, upto(i, 8, 4 * (b - 1)))
                        src = ps_build[:, :].rearrange("p (n r d) -> p n r d", r=2, d=D)
                        bias = g.row_bias[:, 0].rearrange("p j (q r d) -> p (j q) r d", r=2, d=D)
                        pairs = v_aug[b % 2][:, :, :, :].rearrange("p j (q r) w -> p (j q) r w", r=2)
                        for r in range(2):
                            dve.tensor_tensor(pairs[:, :, r, 16 * r:16 * r + D], src[:, :, r, :], bias[:, :, r, :],
                                              ALU.add).then_inc(v_aug_done, 1)
                    u = falls(i, s, 4, 6, NU)
                    if u is not None:
                        dve.wait_ge(y_turned, upto(i, 4, u + 1))
                        heads = ps_turn[:, :].rearrange("p (n w) -> p n w", w=16)
                        dve.wait_ge(y_norm_done, upto(i, 4, u))
                        dve.reciprocal(y_recip[:, :], heads[:, :, D]).then_inc(y_recip_done, 1)
                        dve.wait_ge(y_recip_done, upto(i, 4, u + 1))
                        dve.wait_ge(x_added, upto(i, 4, u))
                        dve.tensor_tensor(y_norm[:, :, :], heads[:, :, 0:D],
                                          y_recip[:, :].unsqueeze(2).to_broadcast([128, TILES * HL, D]),
                                          ALU.mult).then_inc(y_norm_done, 1)
                    p = falls(i, s, 1, -AHEAD, NP)
                    if p is not None:
                        k, u = p % 4, p // 4
                        if k == 0:
                            dve.wait_ge(max_step, upto(i, 16, 4 * (u - 1)))
                        for n in range(PP):
                            dve.wait_ge(rows_scored, upto(i, PP * 16, PP * p + n + 1))
                            bank = ps_max[(p + n) % 2]
                            if n == PP - 1:
                                hl = ORDER[2 * k]
                                dve.tensor_reduce(row_max[:, u % 2, 1, hl:hl + 3:2],
                                                  bank[:, :].rearrange("p (h s) -> p h s", h=2), axis=AX.X, op=ALU.max)\
                                    .then_inc(rows_reduced, 2)
                                continue
                            hl = ORDER[2 * k + n // 2]
                            if n % 2 == 0:
                                dve.tensor_reduce(row_max[:, u % 2, 3, hl:hl + 1], bank[:, :], axis=AX.X, op=ALU.max)\
                                    .then_inc(rows_reduced, 2)
                            else:
                                dve.tensor_reduce(row_max[:, u % 2, 2, hl:hl + 1], bank[:, 0:384], axis=AX.X,
                                                  op=ALU.max).then_inc(rows_reduced, 1)
                                dve.tensor_reduce(row_max[:, u % 2, 0, hl:hl + 1], bank[:, 384:512], axis=AX.X,
                                                  op=ALU.max).then_inc(rows_reduced, 1)
                        if k == 3:
                            dve.wait_ge(rows_reduced, upto(i, 2 * PP * 16, 2 * PP * (p + 1)))
                            dve.wait_ge(max_turned, upto(i, 4, u))
                            top = row_max[:, u % 2]
                            cut = lambda n: max_parts[:, :, n, :]
                            dve.tensor_scalar(cut(0), top, -1.0, None, ALU.mult).then_inc(max_step, 1)
                            dve.wait_ge(max_step, upto(i, 16, 4 * u + 1))
                            dve.scalar_tensor_tensor(out=max_left[:, :, :], in0=top, scalar=-1.0, in1=cut(0),
                                                     op0=ALU.mult, op1=ALU.subtract).then_inc(max_step, 1)
                            dve.wait_ge(max_step, upto(i, 16, 4 * u + 2))
                            dve.tensor_copy(cut(1), max_left[:, :, :]).then_inc(max_step, 1)
                            dve.wait_ge(max_step, upto(i, 16, 4 * u + 3))
                            dve.tensor_tensor(cut(2), max_left[:, :, :], cut(1), ALU.subtract).then_inc(max_step, 1)
                    b = falls(i, s, 8, -12, NB)
                    if b is not None:
                        dve.wait_ge(xn_turned, upto(i, 2, b))
                        emit_ln_apply(dve, g, i, b, xn, ln_mv, ln_rstd, rstd_done, xn_done)

                run(dve, step)

            @block.tensor
            def _(pe):
                pe.wait_ge(ones_set, 8)

                def step(i, s):
                    b = falls(i, s, 8, -11, NB)
                    if b is not None:
                        pe.wait_ge(xn_done, upto(i, 2, b + 1))
                        pe.wait_ge(v_aug_done, upto(i, 4, 2 * b))
                        for j in range(TILES):
                            last = pe.transpose(ps_build[:, 128 * j:128 * j + 128], xn[:, j, :], g.ident[:, :])
                        last.then_inc(xn_turned, 1)
                    b = falls(i, s, 8, -6, NB)
                    if b is not None:
                        pe.wait_ge(qk_full_done, upto(i, 8, 4 * b + 4))
                        for j in range(TILES):
                            last = pe.matmul(ps_build[:, 128 * j:128 * j + 128], xn_t[:, 128 * j:128 * j + 128],
                                             g.weights_t[:, 4, :], start=True, stop=True)
                        last.then_inc(v_done, 1)
                    p = falls(i, s, 1, -AHEAD, NP)
                    if p is not None:
                        k, u = p % 4, p // 4
                        qs, ks = q_stack[u % 4], k_stack[u % 4]
                        if k == 0:
                            pe.wait_ge(stacked[u % 2], upto(i, 2 * 16 * STACK_DMAS, 16 * STACK_DMAS * (u // 2 + 1)))

                        def rows(bank, col, hl, j):
                            pe.matmul(bank[:, col:col + 128 * (j + 1)], qs[0:KROWS, hl, 128 * j:128 * j + 128],
                                      ks[0:KROWS, hl, 0:128 * (j + 1)], start=True, stop=False)
                            return pe.matmul(bank[:, col + 128 * j:col + 128 * (j + 1)], g.ident_bf[:, :],
                                             g.mask_neg[:, :], start=False, stop=True)

                        for n in range(PP):
                            bank = ps_max[(p + n) % 2]
                            pe.wait_ge(rows_reduced, upto(i, 2 * PP * 16, 2 * (PP * p + n - 1)))
                            if n == PP - 1:
                                rows(bank, 0, ORDER[2 * k], 1)
                                last = rows(bank, 256, ORDER[2 * k + 1], 1)
                            elif n % 2 == 0:
                                last = rows(bank, 0, ORDER[2 * k + n // 2], 3)
                            else:
                                rows(bank, 0, ORDER[2 * k + n // 2], 2)
                                last = rows(bank, 384, ORDER[2 * k + n // 2], 0)
                            last.then_inc(rows_scored, 1)
                    p = falls(i, s, 1, 0, NP)
                    if p is not None:
                        k, u = p % 4, p // 4
                        qs, ks = q_stack[u % 4], k_stack[u % 4]
                        if k == 0:
                            pe.wait_ge(max_stacked[u % 2], upto(i, 32, 16 * (u // 2 + 1)))

                        def cols(bank, col, hl, j):
                            return pe.matmul(bank[:, col:col + T - 128 * j], ks[0:MROWS, hl, 128 * j:128 * j + 128],
                                             qs[0:MROWS, hl, 128 * j:T], start=True, stop=True)

                        for n in range(PP):
                            before = PP * p + {0: -2, 1: -1, 2: 1, 3: 2, 4: 0}[n]
                            pe.wait_ge(exp_done, upto(i, PP * 16, before))
                            if n == PP - 1:
                                cols(ps_exp[2], 0, ORDER[2 * k], 2)
                                last = cols(ps_exp[2], 256, ORDER[2 * k + 1], 2)
                            elif n % 2 == 0:
                                last = cols(ps_exp[0], 0, ORDER[2 * k + n // 2], 0)
                            else:
                                cols(ps_exp[1], 0, ORDER[2 * k + n // 2], 1)
                                last = cols(ps_exp[1], 384, ORDER[2 * k + n // 2], 3)
                            last.then_inc(cols_scored, 1)
                    u = falls(i, s, 4, -2, NU)
                    if u is not None:
                        pe.wait_ge(max_step, upto(i, 16, 4 * u + 4))
                        pe.wait_ge(y_norm_done, upto(i, 4, u - 1))
                        for j in range(TILES):
                            last = pe.transpose(turn_bf[0:PARTS * HL, 128 * j:128 * j + 128],
                                                max_parts[:, j].rearrange("p n h -> p (n h)"), g.ident_bf[:, :])
                        last.then_inc(max_turned, 1)
                    for n in range(2):
                        b = falls(i, s, 8, -11 + n, NB)
                        if b is not None:
                            if n == 0:
                                pe.wait_ge(xn_t_done, upto(i, 2, b + 1))
                            else:
                                pe.wait_ge(qk_full_done, upto(i, 8, 4 * b + 2))
                            pe.matmul(ps_build[:, :], g.weights_t[:, n, :], xn_t[:, :], start=True, stop=True)\
                                .then_inc(qk_done, 1)
                    quad = falls(i, s, 2, 2, NP // 2)
                    if quad is not None:
                        b, r, f = quad // 4, quad % 2, quad // 2 % 2
                        pe.wait_ge(masked, upto(i, 32, 4 * quad + 4))
                        pe.wait_ge(v_aug_done, upto(i, 4, 2 * b + 2))
                        if r == 0:
                            pe.wait_ge(y_cols_done, upto(i, 4, quad // 2))
                        for j in range(TILES):
                            for c in range(4):
                                last = pe.matmul(ps_pv[32 * c:32 * c + 32, 128 * j:T],
                                                 v_aug[b % 2][:, j, HL * f + 2 * c + r, :],
                                                 probs[:, quad % 2, c, COLS[j]:COLS[j] + T - 128 * j],
                                                 start=(r == 0 and j == 0), stop=(r == 1 and j == TILES - 1),
                                                 skip_group_check=True)
                        last.then_inc(pv_done, 1)
                    u = falls(i, s, 4, 5, NU)
                    if u is not None:
                        pe.wait_ge(y_cols_done, upto(i, 4, u + 1))
                        if not (isinstance(i, int) and 4 * i + u + 1 >= NU):
                            pe.wait_ge(max_rows_done, upto(i, 4, u + 2))
                        for j in range(TILES):
                            last = pe.transpose(ps_turn[:, 128 * j:128 * j + 128], y_cols[:, 128 * j:128 * j + 128],
                                                g.ident[:, :])
                        last.then_inc(y_turned, 1)

                run(pe, step)


def emit_ffn(nc, g, tag):
    CH = 5
    PR = 4
    with ExitStack() as ctx:
        sb = lambda name, shape, dt=F32: ctx.enter_context(nc.sbuf_tensor(f"f{tag}_{name}", shape, dt))
        ps = lambda name, shape, dt=F32: ctx.enter_context(nc.psum_tensor(f"f{tag}_{name}", shape, dt))
        sem = lambda name: ctx.enter_context(nc.semaphore(f"f{tag}_{name}"))
        xn = sb("xn", [128, TILES, C])
        xn_t = sb("xn_t", [128, 2, T])
        ln_stats = sb("ln_stats", [128, TILES, 6])
        ln_mv = sb("ln_mv", [128, TILES, 2])
        ln_var = sb("ln_var", [128, TILES])
        ln_rstd = sb("ln_rstd", [128, TILES])
        silu = sb("silu", [128, 2, T])
        gated = sb("gated", [128, 2, T])
        hidden = sb("hidden", [128, CH, T])
        top = sb("top", [128, TILES])
        shifted = sb("shifted", [128, TILES, E])
        exps = sb("exps", [128, TILES, E])
        total = sb("total", [128, TILES])
        inv_total = sb("inv_total", [128, TILES])
        prob = sb("prob", [128, TILES, E])
        above = sb("above", [128, TILES, E, E])
        equal = sb("equal", [128, TILES, E, E])
        ties = sb("ties", [128, TILES, E, E])
        rank = sb("rank", [128, TILES, E])
        coef = sb("coef", [128, TILES, E])
        coef_left = sb("coef_left", [128, TILES, E])
        coef_parts = sb("coef_parts", [128, TILES, PARTS, E], BF16)
        coef_rows = sb("coef_rows", [KROWS, T], BF16)
        ps_gate = [ps(f"ps_gate{n}", [128, T]) for n in range(2)]
        ps_up = [ps(f"ps_up{n}", [128, T]) for n in range(2)]
        ps_coef = [ps(f"ps_coef{n}", [128, T]) for n in range(2)]
        ps_out = ps("ps_out", [128, T])
        ps_small = ps("ps_small", [128, T])
        small_bf = ps_small[:, :].bitcast(BF16)

        zeroed = sem("zeroed")
        stats_done = sem("stats_done")
        mv_done = sem("mv_done")
        var_done = sem("var_done")
        rstd_done = sem("rstd_done")
        xn_done = sem("xn_done")
        xn_turned = sem("xn_turned")
        xn_t_done = sem("xn_t_done")
        gate_done = sem("gate_done")
        up_done = sem("up_done")
        silu_done = sem("silu_done")
        gated_done = sem("gated_done")
        weighted = sem("weighted")
        spread = sem("spread")
        out_done = sem("out_done")
        x_added = sem("x_added")
        logits_done = sem("logits_done")
        top_done = sem("top_done")
        shifted_done = sem("shifted_done")
        exps_done = sem("exps_done")
        route = sem("route")
        ROUTE = 13
        coef_turned = sem("coef_turned")
        coef_rows_done = sem("coef_rows_done")

        LOOPS = NB // 2 - 2

        def run(eng, batch):
            for e in range(-2, 2):
                batch(0, e)
            with eng.Fori(0, LOOPS) as i:
                for e in range(2, 4):
                    batch(i, e)
            for e in range(2, NB - 2 * LOOPS + 1):
                batch(LOOPS, e)

        def live(i, e):
            return not isinstance(i, int) or 0 <= 2 * i + e < NB

        with nc.Block() as block:

            @block.gpsimd
            def _(pool):
                def batch(i, e):
                    if live(i, e + 2):
                        pool.wait_ge(mv_done, upto(i, 2, e + 3))
                        pool.sem_inc(g.passed_pool, 1)
                        pool.tensor_scalar(ln_var[:, :], ln_mv[:, :, 1], EPS, 1.0, ALU.add, ALU.mult)\
                            .then_inc(var_done, 1)
                        pool.wait_ge(var_done, upto(i, 2, e + 3))
                        pool.sem_inc(g.passed_pool, 1)
                        pool.wait_ge(xn_done, upto(i, 2, e + 2))
                        pool.sem_inc(g.passed_pool, 1)
                        pool.tensor_tensor(ln_rstd[:, :], ln_var[:, :], g.half_power[:, :], ALU.pow)\
                            .then_inc(rstd_done, 1)

                run(pool, batch)

            @block.scalar
            def _(act):
                def batch(i, e):
                    for n in range(CH):
                        if n == 1 and live(i, e + 1):
                            act.wait_ge(xn_turned, upto(i, 2, e + 2))
                            act.wait_ge(up_done, upto(i, 2 * CH, CH * e))
                            act.activation(xn_t[:, (e + 1) % 2, :], ps_small[:, :], ACT.Copy).then_inc(xn_t_done, 1)
                        if live(i, e):
                            act.wait_ge(gate_done, upto(i, 2 * CH, CH * e + n + 1))
                            act.wait_ge(gated_done, upto(i, 2 * CH, CH * e + n - 1))
                            act.activation(silu[:, (e + n) % 2, :], ps_gate[(e + n) % 2][:, :], ACT.Silu)\
                                .then_inc(silu_done, 1)
                        if n == 2 and live(i, e + 1):
                            act.wait_ge(shifted_done, upto(i, 2, e + 2))
                            act.activation(exps[:, :, :], shifted[:, :, :], ACT.Exp).then_inc(exps_done, 1)
                        if n == CH - 1 and live(i, e + 1):
                            act.wait_ge(coef_turned, upto(i, 2, e + 2))
                            act.wait_ge(spread, upto(i, 2 * PR, PR * (e + 1)))
                            act.activation(coef_rows[0:PARTS * E, :], small_bf[0:PARTS * E, 0:T], ACT.Copy)\
                                .then_inc(coef_rows_done, 1)

                run(act, batch)

            @block.vector
            def _(dve):
                dve.memset(coef_rows[:, :].bitcast(F32), 0.0).then_inc(zeroed, 1)

                def route_step(i, e, k, ins):
                    ins.then_inc(route, 1)
                    dve.wait_ge(route, upto(i, 2 * ROUTE, ROUTE * e + k))

                def batch(i, e):
                    for n in range(CH):
                        if n == 2 and live(i, e - 1):
                            dve.wait_ge(out_done, upto(i, 2, e))
                            tile = x_slot(g, i, e - 1)
                            dve.tensor_tensor(tile, tile, ps_out[:, :].rearrange("p (j c) -> p j c", j=TILES), ALU.add)\
                                .then_inc(x_added, 1)
                        if n == 2 and live(i, e + 1):
                            dve.wait_ge(logits_done, upto(i, 2, e + 2))
                            logits = ps_small[:, 0:TILES * E].rearrange("p (j e) -> p j e", e=E)
                            dve.tensor_reduce(top[:, :], logits, axis=AX.X, op=ALU.max).then_inc(top_done, 1)
                            dve.wait_ge(top_done, upto(i, 2, e + 2))
                            dve.wait_ge(exps_done, upto(i, 2, e + 1))
                            dve.tensor_tensor(shifted[:, :, :], logits, top[:, :].unsqueeze(2).to_broadcast([128, TILES, E]),
                                              ALU.subtract).then_inc(shifted_done, 1)
                        if live(i, e):
                            par = (e + n) % 2
                            dve.wait_ge(silu_done, upto(i, 2 * CH, CH * e + n + 1))
                            dve.wait_ge(up_done, upto(i, 2 * CH, CH * e + n + 1))
                            dve.wait_ge(out_done, upto(i, 2, e))
                            last = n == CH - 1
                            dst = hidden[:, n, :] if last else gated[:, par, :]
                            if not last:
                                dve.wait_ge(weighted, upto(i, 2 * PR, PR * e + n - 1))
                            dve.tensor_tensor(dst, ps_up[par][:, :], silu[:, par, :], ALU.mult).then_inc(gated_done, 1)
                            if not last:
                                dve.wait_ge(gated_done, upto(i, 2 * CH, CH * e + n + 1))
                                dve.wait_ge(spread, upto(i, 2 * PR, PR * e + n + 1))
                                dve.tensor_tensor(hidden[:, n, :], ps_coef[n % 2][:, :], gated[:, par, :], ALU.mult)\
                                    .then_inc(weighted, 1)
                        if n == 2 and live(i, e + 1):
                            f = e + 1
                            dve.wait_ge(exps_done, upto(i, 2, f + 1))
                            dve.wait_ge(coef_turned, upto(i, 2, f))
                            each = prob[:, :, :].unsqueeze(3).to_broadcast([128, TILES, E, E])
                            other = prob[:, :, :].unsqueeze(2).to_broadcast([128, TILES, E, E])
                            route_step(i, f, 1, dve.tensor_reduce(total[:, :], exps[:, :, :], axis=AX.X, op=ALU.add))
                            route_step(i, f, 2, dve.reciprocal(inv_total[:, :], total[:, :]))
                            route_step(i, f, 3, dve.tensor_tensor(
                                prob[:, :, :], exps[:, :, :], inv_total[:, :].unsqueeze(2).to_broadcast([128, TILES, E]),
                                ALU.mult))
                            route_step(i, f, 4, dve.tensor_tensor(above[:, :, :, :], other, each, ALU.is_gt))
                            route_step(i, f, 5, dve.tensor_tensor(equal[:, :, :, :], other, each, ALU.is_equal))
                            route_step(i, f, 6, dve.tensor_tensor(
                                ties[:, :, :, :].rearrange("p j e f -> p j (e f)"),
                                equal[:, :, :, :].rearrange("p j e f -> p j (e f)"),
                                g.earlier[:, :, :].rearrange("p e f -> p (e f)").unsqueeze(1)
                                .to_broadcast([128, TILES, E * E]), ALU.mult))
                            route_step(i, f, 7, dve.tensor_tensor(above[:, :, :, :], above[:, :, :, :], ties[:, :, :, :],
                                                                  ALU.add))
                            route_step(i, f, 8, dve.tensor_reduce(rank[:, :, :], above[:, :, :, :], axis=AX.X, op=ALU.add))
                            route_step(i, f, 9, dve.scalar_tensor_tensor(
                                out=coef[:, :, :], in0=rank[:, :, :], scalar=1.5, in1=prob[:, :, :],
                                op0=ALU.is_lt, op1=ALU.mult))
                            cut = lambda k: coef_parts[:, :, k, :]
                            route_step(i, f, 10, dve.tensor_copy(cut(0), coef[:, :, :]))
                            route_step(i, f, 11, dve.tensor_tensor(coef_left[:, :, :], coef[:, :, :], cut(0), ALU.subtract))
                            route_step(i, f, 12, dve.tensor_copy(cut(1), coef_left[:, :, :]))
                            dve.tensor_tensor(cut(2), coef_left[:, :, :], cut(1), ALU.subtract).then_inc(route, 1)
                        if n == 3 and live(i, e + 2):
                            emit_ln_stats(dve, g, i, e + 2, ln_stats, ln_mv, stats_done, mv_done)
                        if n == 4 and live(i, e + 2):
                            dve.wait_ge(xn_turned, upto(i, 2, e + 2))
                            emit_ln_apply(dve, g, i, e + 2, xn, ln_mv, ln_rstd, rstd_done, xn_done)

                run(dve, batch)

            @block.tensor
            def _(pe):
                pe.wait_ge(zeroed, 1)

                def down(i, e, n):
                    if n == CH - 1:
                        pe.wait_ge(gated_done, upto(i, 2 * CH, CH * e + CH))
                    else:
                        pe.wait_ge(weighted, upto(i, 2 * PR, PR * e + n + 1))
                    if n == 0:
                        pe.wait_ge(x_added, upto(i, 2, e))
                    for j in range(TILES):
                        last = pe.matmul(ps_out[:, 128 * j:128 * j + 128], hidden[:, n, 128 * j:128 * j + 128],
                                         g.w_down[:, n, :], start=(n == 0 and j == 0), stop=(n == CH - 1),
                                         skip_group_check=True)
                    if n == CH - 1:
                        last.then_inc(out_done, 1)

                def batch(i, e):
                    for n in range(CH):
                        if live(i, e):
                            par = (e + n) % 2
                            xt = xn_t[:, e % 2, :]
                            if n == 0:
                                pe.wait_ge(xn_t_done, upto(i, 2, e + 1))
                            pe.wait_ge(silu_done, upto(i, 2 * CH, CH * e + n - 1))
                            pe.matmul(ps_gate[par][:, :], g.w_gate[:, n, :], xt, start=True, stop=True)\
                                .then_inc(gate_done, 1)
                            pe.wait_ge(gated_done, upto(i, 2 * CH, CH * e + n - 1))
                            pe.matmul(ps_up[par][:, :], g.w_up[:, n, :], xt, start=True, stop=True)\
                                .then_inc(up_done, 1)
                            if n < PR:
                                if n == 0:
                                    pe.wait_ge(coef_rows_done, upto(i, 2, e + 1))
                                pe.wait_ge(weighted, upto(i, 2 * PR, PR * e + n - 1))
                                pe.matmul(ps_coef[n % 2][:, :],
                                          g.select[:, 2 * n:2 * n + 2, :].rearrange("p e d -> p (e d)"),
                                          coef_rows[:, :], start=True, stop=True).then_inc(spread, 1)
                        if n < 2 and live(i, e - 1):
                            down(i, e - 1, n + 3)
                        if n >= 2 and live(i, e):
                            down(i, e, n - 2)
                        if n == 0 and live(i, e + 1):
                            pe.wait_ge(xn_done, upto(i, 2, e + 2))
                            pe.wait_ge(coef_rows_done, upto(i, 2, e + 1))
                            for j in range(TILES):
                                last = pe.transpose(ps_small[:, 128 * j:128 * j + 128], xn[:, j, :], g.ident[:, :])
                            last.then_inc(xn_turned, 1)
                        if n == 1 and live(i, e + 1):
                            pe.wait_ge(xn_t_done, upto(i, 2, e + 2))
                            for j in range(TILES):
                                last = pe.matmul(ps_small[:, E * j:E * j + E],
                                                 xn_t[:, (e + 1) % 2, 128 * j:128 * j + 128], g.w_router[:, :],
                                                 start=True, stop=True)
                            last.then_inc(logits_done, 1)
                        if n == CH - 1 and live(i, e + 1):
                            pe.wait_ge(route, upto(i, 2 * ROUTE, ROUTE * (e + 2)))
                            for j in range(TILES):
                                last = pe.transpose(small_bf[0:PARTS * E, 128 * j:128 * j + 128],
                                                    coef_parts[:, j].rearrange("p n e -> p (n e)"), g.ident_bf[:, :])
                            last.then_inc(coef_turned, 1)

                run(pe, batch)


def emit_linear_attention(nc, g):
    PU = 4
    NU = 2 * NB
    KEY_TOK, KEY_FEAT, QUERY = range(3)
    OTHERS = [(KEY_TOK, j) for j in range(TILES - 1)] + [(QUERY, c) for c in range(PU)]
    TILE_OF = [t for k in range(HL) for t in OTHERS[k:k + 1] + [(KEY_FEAT, k)]]
    FEATS = len(TILE_OF)
    STACK_DMAS = 2 * PARTS * PARTS
    with ExitStack() as ctx:
        sb = lambda name, shape, dt=F32: ctx.enter_context(nc.sbuf_tensor(f"l_{name}", shape, dt))
        ps = lambda name, shape, dt=F32: ctx.enter_context(nc.psum_tensor(f"l_{name}", shape, dt))
        sem = lambda name: ctx.enter_context(nc.semaphore(f"l_{name}"))
        q_stack = [sb(f"q_stack{n}", [KROWS, HL, T], BF16) for n in range(2)]
        k_stack = [sb(f"k_stack{n}", [KROWS, HL, T], BF16) for n in range(2)]
        key_tok = sb("key_tok", [128, 2, TILES - 1, HL * M])
        key_feat = sb("key_feat", [128, HL, T])
        query_feat = sb("query_feat", [128, 2, PU, T])
        attn = sb("attn", [128, HL, TILES, 128])
        v_aug = [sb(f"v_aug{n}", [128, TILES, H // 2, 64]) for n in range(2)]
        parts = sb("parts", [128, 2, PARTS, T], BF16)
        qk_full = sb("qk_full", [128, 2, T])
        xn = sb("xn", [128, TILES, C])
        xn_t = sb("xn_t", [128, T])
        ln_stats = sb("ln_stats", [128, TILES, 6])
        ln_mv = sb("ln_mv", [128, TILES, 2])
        ln_var = sb("ln_var", [128, TILES])
        ln_rstd = sb("ln_rstd", [128, TILES])
        state_cols = sb("state_cols", [128, 128])
        state = sb("state", [128, TILES - 1, PU * 32])
        y_cols = sb("y_cols", [128, T])
        y_sum = sb("y_sum", [128, TILES * HL])
        y_recip = sb("y_recip", [128, TILES * HL])
        y_norm = sb("y_norm", [128, TILES, C])
        y_t = sb("y_t", [128, T])
        y_out = sb("y_out", [128, TILES, C])
        ps_feat = [ps(f"ps_feat{n}", [128, T]) for n in range(2)]
        ps_attn = [ps(f"ps_attn{n}", [128, T]) for n in range(2)]
        ps_pv = ps("ps_pv", [128, T])
        ps_state = ps("ps_state", [128, T])
        ps_turn = ps("ps_turn", [128, T])
        ps_build = ps("ps_build", [128, T])

        zeroed = sem("zeroed")
        ones_set = sem("ones_set")
        stats_done = sem("stats_done")
        mv_done = sem("mv_done")
        var_done = sem("var_done")
        rstd_done = sem("rstd_done")
        xn_done = sem("xn_done")
        xn_turned = sem("xn_turned")
        xn_t_done = sem("xn_t_done")
        qk_done = sem("qk_done")
        qk_full_done = sem("qk_full_done")
        left1_done = sem("left1_done")
        mid_done = sem("mid_done")
        low_done = sem("low_done")
        v_done = sem("v_done")
        v_aug_done = sem("v_aug_done")
        stacked = [sem(f"stacked{f}") for f in range(2)]
        feat_done = sem("feat_done")
        feat_out = sem("feat_out")
        scored = sem("scored")
        attn_done = sem("attn_done")
        within_done = sem("within_done")
        hist_done = sem("hist_done")
        summed = sem("summed")
        state_cols_done = sem("state_cols_done")
        state_turned = sem("state_turned")
        state_done = sem("state_done")
        y_cols_done = sem("y_cols_done")
        y_turned = sem("y_turned")
        y_sum_done = sem("y_sum_done")
        y_recip_done = sem("y_recip_done")
        y_norm_done = sem("y_norm_done")
        y_norm_turned = sem("y_norm_turned")
        y_t_done = sem("y_t_done")
        projected = sem("projected")
        biased = sem("biased")
        x_added = sem("x_added")

        FIRST, BODY, LOOPS = -4, 8, 5

        def run(eng, step):
            for s in range(FIRST, BODY):
                step(0, s)
            with eng.Fori(0, LOOPS) as i:
                for s in range(BODY, BODY + 4):
                    step(i, s)
            for s in range(BODY, NU - 4 * LOOPS + 2):
                step(LOOPS, s)

        def unit(i, s):
            return s if not isinstance(i, int) or 0 <= 4 * i + s < NU else None

        def batch(i, s2):
            return s2 // 2 if s2 % 2 == 0 and (not isinstance(i, int) or 0 <= 2 * i + s2 // 2 < NB) else None

        with nc.Block() as block:

            @block.sync
            def _(sp):
                sp.wait_ge(zeroed, 4)

                def step(i, s):
                    b = batch(i, s + 3)
                    if b is not None:
                        sp.wait_ge(low_done, upto(i, 4, 2 * b + 2))
                        sp.sem_inc(g.passed_sp, 1)
                        for f in range(2):
                            u = 2 * b + f
                            sp.wait_ge(feat_done, upto(i, 4 * FEATS, FEATS * (u - 1)))
                            sp.sem_inc(g.passed_sp, 1)
                            sp.wait_ge(stacked[f], upto(i, 2 * 16 * STACK_DMAS, 16 * STACK_DMAS * b))
                            sp.sem_inc(g.passed_sp, 1)
                            for n in range(PARTS):
                                for c in range(PARTS):
                                    row = PARTS * D * n + D * c
                                    for m, stack in enumerate((q_stack, k_stack)):
                                        sp.dma_start(stack[u % 2][row:row + D, :, :],
                                                     parts[64 * f:64 * f + 64, m, n, :]).then_inc(stacked[f], 16)

                run(sp, step)

            @block.gpsimd
            def _(pool):
                def step(i, s):
                    for k in range(8):
                        b = batch(i, s + 4)
                        if k == 4 and b is not None:
                            pool.wait_ge(mv_done, upto(i, 2, b + 1))
                            pool.sem_inc(g.passed_pool, 1)
                            pool.tensor_scalar(ln_var[:, :], ln_mv[:, :, 1], EPS, 1.0, ALU.add, ALU.mult)\
                                .then_inc(var_done, 1)
                            pool.wait_ge(var_done, upto(i, 2, b + 1))
                            pool.sem_inc(g.passed_pool, 1)
                            pool.wait_ge(xn_done, upto(i, 2, b))
                            pool.sem_inc(g.passed_pool, 1)
                            pool.tensor_tensor(ln_rstd[:, :], ln_var[:, :], g.half_power[:, :], ALU.pow)\
                                .then_inc(rstd_done, 1)
                        b = batch(i, s + 3)
                        if k in (2, 3) and b is not None:
                            n = k - 2
                            pool.wait_ge(qk_full_done, upto(i, 8, 4 * b + 2 * n + 2))
                            pool.sem_inc(g.passed_pool, 1)
                            pool.tensor_tensor(qk_full[:, n, :], qk_full[:, n, :], parts[:, n, 0, :], ALU.subtract)\
                                .then_inc(left1_done, 1)
                            pool.wait_ge(mid_done, upto(i, 4, 2 * b + n + 1))
                            pool.sem_inc(g.passed_pool, 1)
                            pool.tensor_tensor(parts[:, n, 2, :], qk_full[:, n, :], parts[:, n, 1, :], ALU.subtract)\
                                .then_inc(low_done, 1)
                        b = batch(i, s - 3)
                        if k == 6 and b is not None:
                            pool.wait_ge(biased, upto(i, 2, b + 1))
                            pool.sem_inc(g.passed_pool, 1)
                            tile = x_slot(g, i, b)
                            pool.tensor_tensor(tile, tile, y_out[:, :, :], ALU.add).then_inc(x_added, 1)

                run(pool, step)

            @block.scalar
            def _(act):
                def step(i, s):
                    for k in range(8):
                        b = batch(i, s + 3)
                        if k in (2, 3) and b is not None:
                            n = k - 2
                            act.wait_ge(qk_done, upto(i, 4, 2 * b + n + 1))
                            act.wait_ge(low_done, upto(i, 4, 2 * b))
                            for f in range(2):
                                act.wait_ge(stacked[f], upto(i, 2 * 16 * STACK_DMAS, 16 * STACK_DMAS * b))
                            act.activation(qk_full[:, n, :], ps_build[:, :], ACT.Identity,
                                           bias=g.qk_bias[:, 2 + n:3 + n]).then_inc(qk_full_done, 1)
                            act.activation(parts[:, n, 0, :], ps_build[:, :], ACT.Identity,
                                           bias=g.qk_bias[:, 2 + n:3 + n]).then_inc(qk_full_done, 1)
                        b = batch(i, s - 3)
                        if k == 5 and b is not None:
                            act.wait_ge(y_norm_turned, upto(i, 2, b + 1))
                            act.wait_ge(projected, upto(i, 2, b))
                            act.activation(y_t[:, :], ps_build[:, :], ACT.Copy).then_inc(y_t_done, 1)
                        u = unit(i, s - 1)
                        if k == 3 and u is not None:
                            act.wait_ge(hist_done, upto(i, 4, u + 1))
                            act.wait_ge(y_turned, upto(i, 4, u))
                            act.activation(y_cols[:, :], ps_pv[:, :], ACT.Copy).then_inc(y_cols_done, 1)
                        u = unit(i, s)
                        if k in (3, 4, 5) and u is not None:
                            j = k - 3
                            act.wait_ge(summed, upto(i, 12, 3 * u + j + 1))
                            act.wait_ge(state_turned, upto(i, 12, 3 * u + j))
                            act.activation(state_cols[:, :], ps_state[:, 0:128], ACT.Copy).then_inc(state_cols_done, 1)
                        u = unit(i, s + 1)
                        if u is not None:
                            for n in range(2 * k, min(2 * k + 2, FEATS)):
                                kind, m = TILE_OF[n]
                                src = ps_feat[(u + n) % 2]
                                if kind == KEY_TOK:
                                    dst = key_tok[:, u % 2, m, :]
                                    act.wait_ge(summed, upto(i, 12, 3 * (u - 1)))
                                elif kind == KEY_FEAT:
                                    dst = key_feat[:, ORDER[m], :]
                                    act.wait_ge(scored, upto(i, 32, HL * (u - 1) + m + 1))
                                else:
                                    dst = query_feat[:, u % 2, m, :]
                                    act.wait_ge(hist_done, upto(i, 4, u - 1))
                                act.wait_ge(feat_done, upto(i, 4 * FEATS, FEATS * u + n + 1))
                                act.activation(dst, src[:, :], ACT.Relu).then_inc(feat_out, 1)
                        b = batch(i, s + 3)
                        if k == 0 and b is not None:
                            act.wait_ge(xn_turned, upto(i, 2, b + 1))
                            act.wait_ge(v_done, upto(i, 2, b))
                            act.activation(xn_t[:, :], ps_build[:, :], ACT.Copy).then_inc(xn_t_done, 1)
                        if k in (3, 4) and b is not None:
                            n = k - 3
                            act.wait_ge(left1_done, upto(i, 4, 2 * b + n + 1))
                            act.activation(parts[:, n, 1, :], qk_full[:, n, :], ACT.Copy).then_inc(mid_done, 1)

                run(act, step)

            @block.vector
            def _(dve):
                for n in range(2):
                    dve.memset(q_stack[n][64:KROWS, :, :].bitcast(F32), 0.0).then_inc(zeroed, 1)
                    dve.memset(k_stack[n][64:KROWS, :, :].bitcast(F32), 0.0).then_inc(zeroed, 1)
                for n in range(2):
                    dve.memset(v_aug[n][:, :, :, :], 0.0).then_inc(zeroed, 1)
                dve.wait_ge(zeroed, 6)
                for n in range(2):
                    for r in range(2):
                        at = 32 - 16 * r
                        dve.memset(v_aug[n][:, :, :, at + D:at + D + 1], 1.0).then_inc(ones_set, 1)

                def step(i, s):
                    for k in range(8):
                        b = batch(i, s + 2)
                        if k == 4 and b is not None:
                            dve.wait_ge(v_done, upto(i, 2, b + 1))
                            dve.wait_ge(hist_done, upto(i, 4, 2 * (b - 1)))
                            src = ps_build[:, :].rearrange("p (n r d) -> p n r d", r=2, d=D)
                            bias = g.row_bias[:, 1].rearrange("p j (q r d) -> p (j q) r d", r=2, d=D)
                            pairs = v_aug[b % 2][:, :, :, :].rearrange("p j q w -> p (j q) w")
                            for r in range(2):
                                at = 32 - 16 * r
                                dve.tensor_tensor(pairs[:, :, at:at + D], src[:, :, r, :], bias[:, :, r, :],
                                                  ALU.add).then_inc(v_aug_done, 1)
                        u = unit(i, s - 2)
                        if k == 0 and u is not None:
                            dve.wait_ge(y_turned, upto(i, 4, u + 1))
                            heads = ps_turn[:, :].rearrange("p (n w) -> p n w", w=16)
                            dve.wait_ge(y_norm_done, upto(i, 4, u))
                            dve.tensor_scalar(y_sum[:, :], heads[:, :, D], DELTA, None, ALU.add).then_inc(y_sum_done, 1)
                            dve.wait_ge(y_sum_done, upto(i, 4, u + 1))
                            dve.reciprocal(y_recip[:, :], y_sum[:, :]).then_inc(y_recip_done, 1)
                            dve.wait_ge(y_recip_done, upto(i, 4, u + 1))
                            dve.wait_ge(y_norm_turned, upto(i, 2, u // 2))
                            f = u % 2
                            dve.tensor_tensor(y_norm[:, :, 64 * f:64 * f + 64].rearrange("p j (h d) -> p j h d", d=D),
                                              ps_turn[:, :].rearrange("p (j h w) -> p j h w", j=TILES, w=16)[:, :, :, 0:D],
                                              y_recip[:, :].rearrange("p (j h) -> p j h", j=TILES).unsqueeze(3)
                                              .to_broadcast([128, TILES, HL, D]), ALU.mult).then_inc(y_norm_done, 1)
                        b = batch(i, s - 3)
                        if k == 7 and b is not None:
                            dve.wait_ge(projected, upto(i, 2, b + 1))
                            dve.wait_ge(x_added, upto(i, 2, b))
                            dve.tensor_tensor(y_out[:, :, :], ps_build[:, :].rearrange("p (j c) -> p j c", j=TILES),
                                              g.row_bias[:, 2], ALU.add).then_inc(biased, 1)
                        u = unit(i, s)
                        if u is not None:
                            hl = ORDER[k]
                            dve.wait_ge(scored, upto(i, 32, HL * u + k + 1))
                            dve.wait_ge(within_done, upto(i, 8, 2 * (u - 1) + k // 4 + 1))
                            dve.tensor_tensor(attn[:, hl, :, :], ps_attn[k % 2][:, :].rearrange("p (j t) -> p j t", j=TILES),
                                              g.causal01[:, :].unsqueeze(1).to_broadcast([128, TILES, 128]),
                                              ALU.mult).then_inc(attn_done, 1)
                        if k in (4, 5, 6) and u is not None:
                            j = k - 4
                            dve.wait_ge(state_turned, upto(i, 12, 3 * u + j + 1))
                            dve.wait_ge(hist_done, upto(i, 4, u))
                            for r in range(2):
                                dve.tensor_tensor(state[:, j, :].rearrange("p (q w) -> p q w", q=PU)[:, :, 16 * r:16 * r + 16],
                                                  ps_turn[:, 0:128].rearrange("p (q w) -> p q w", q=PU)
                                                  [:, :, 16 - 16 * r:32 - 16 * r],
                                                  g.pair_mask[:, 16 * r:16 * r + 16].unsqueeze(1)
                                                  .to_broadcast([128, PU, 16]), ALU.mult).then_inc(state_done, 1)
                        b = batch(i, s + 4)
                        if k == 3 and b is not None:
                            emit_ln_stats(dve, g, i, b, ln_stats, ln_mv, stats_done, mv_done)
                        if k == 6 and b is not None:
                            dve.wait_ge(xn_turned, upto(i, 2, b))
                            emit_ln_apply(dve, g, i, b, xn, ln_mv, ln_rstd, rstd_done, xn_done)

                run(dve, step)

            @block.tensor
            def _(pe):
                pe.wait_ge(ones_set, 4)

                def features(i, u, n):
                    bank, f = ps_feat[(u + n) % 2], u % 2
                    ks, qs = k_stack[u % 2], q_stack[u % 2]
                    if n == 0:
                        pe.wait_ge(stacked[f], upto(i, 2 * 16 * STACK_DMAS, 16 * STACK_DMAS * (u // 2 + 1)))
                    pe.wait_ge(feat_out, upto(i, 4 * FEATS, FEATS * u + n - 1))
                    kind, m = TILE_OF[n]
                    if kind == KEY_TOK:
                        for hl in range(HL):
                            last = pe.matmul(bank[:, M * hl:M * hl + M], ks[:, hl, 128 * m:128 * m + 128],
                                             g.proj[:, HL * f + hl, M:2 * M], start=True, stop=True)
                    elif kind == KEY_FEAT:
                        hl = ORDER[m]
                        at = M * (1 - hl % 2)
                        last = pe.matmul(bank[:, :], g.proj[:, HL * f + hl, at:at + 2 * M], ks[:, hl, :],
                                         start=True, stop=True)
                    else:
                        for r in range(2):
                            hl = 2 * m + r
                            last = pe.matmul(bank[M * r:M * r + M, :], g.proj[:, HL * f + hl, M:2 * M], qs[:, hl, :],
                                             start=True, stop=True)
                    last.then_inc(feat_done, 1)

                def within(i, u, r):
                    f = u % 2
                    pe.wait_ge(attn_done, upto(i, 32, HL * u + 4 * r + 4))
                    if r == 0:
                        pe.wait_ge(y_cols_done, upto(i, 4, u))
                        pe.wait_ge(v_aug_done, upto(i, 4, 2 * (u // 2) + 2))
                    for j in range(TILES):
                        for c in range(PU):
                            last = pe.matmul(ps_pv[32 * c:32 * c + 32, 128 * j:128 * j + 128],
                                             v_aug[u // 2 % 2][:, j, PU * f + c, 32 - 32 * r:64 - 32 * r], attn[:, 2 * c + r, j, :],
                                             start=(r == 0 and j == 0), stop=False, skip_group_check=True)
                    last.then_inc(within_done, 1)

                def sums(i, u, j):
                    pe.wait_ge(state_cols_done, upto(i, 12, 3 * u + j))
                    if j == 0:
                        pe.wait_ge(v_aug_done, upto(i, 4, 2 * (u // 2) + 2))
                    for c in range(PU):
                        last = pe.matmul(ps_state[32 * c:32 * c + 32, 0:128],
                                         v_aug[u // 2 % 2][:, j, PU * (u % 2) + c, 16:48],
                                         key_tok[:, u % 2, j, 128 * c:128 * c + 128],
                                         start=(j == 0), stop=(j == TILES - 2), skip_group_check=True)
                    last.then_inc(summed, 1)

                def step(i, s):
                    for k in range(8):
                        b = batch(i, s + 3)
                        if k == 0 and b is not None:
                            pe.wait_ge(xn_done, upto(i, 2, b + 1))
                            pe.wait_ge(v_aug_done, upto(i, 4, 2 * b))
                            for j in range(TILES):
                                last = pe.transpose(ps_build[:, 128 * j:128 * j + 128], xn[:, j, :], g.ident[:, :])
                            last.then_inc(xn_turned, 1)
                        nxt = unit(i, s + 1)
                        if nxt is not None:
                            features(i, nxt, 2 * k)
                        u = unit(i, s)
                        if u is not None:
                            hl = ORDER[k]
                            if k == 0:
                                pe.wait_ge(feat_out, upto(i, 4 * FEATS, FEATS * (u + 1)))
                            pe.wait_ge(attn_done, upto(i, 32, HL * u + k - 1))
                            for j in range(TILES):
                                last = pe.matmul(ps_attn[k % 2][:, 128 * j:128 * j + 128],
                                                 key_feat[:, hl, 128 * j:128 * j + 128],
                                                 query_feat[:, u % 2, hl // 2, 128 * j:128 * j + 128],
                                                 start=True, stop=True)
                            last.then_inc(scored, 1)
                        if nxt is not None and 2 * k + 1 < FEATS:
                            features(i, nxt, 2 * k + 1)
                        v = unit(i, s - 1)
                        if k == 1 and v is not None:
                            within(i, v, 1)
                        if k == 2 and v is not None:
                            pe.wait_ge(state_done, upto(i, 24, 6 * v + 6))
                            for j in range(1, TILES):
                                for c in range(PU):
                                    last = pe.matmul(ps_pv[32 * c:32 * c + 32, 128 * j:128 * j + 128],
                                                     state[:, j - 1, 32 * c:32 * c + 32],
                                                     query_feat[:, v % 2, c, 128 * j:128 * j + 128],
                                                     start=False, stop=(j == TILES - 1), skip_group_check=True)
                            last.then_inc(hist_done, 1)
                        if k == 2 and u is not None:
                            sums(i, u, 0)
                        if k in (3, 4, 5) and u is not None:
                            j = k - 3
                            if j < 2:
                                sums(i, u, j + 1)
                            pe.wait_ge(state_cols_done, upto(i, 12, 3 * u + j + 1))
                            pe.wait_ge(state_done, upto(i, 24, 2 * (3 * u + j)))
                            pe.wait_ge(y_norm_done, upto(i, 4, u - 1))
                            pe.transpose(ps_turn[:, 0:128], state_cols[:, :], g.ident[:, :]).then_inc(state_turned, 1)
                        if k == 6 and u is not None:
                            within(i, u, 0)
                        if k == 7 and v is not None:
                            pe.wait_ge(y_cols_done, upto(i, 4, v + 1))
                            if u is not None:
                                pe.wait_ge(state_done, upto(i, 24, 6 * u + 6))
                            pe.wait_ge(y_norm_done, upto(i, 4, v))
                            for j in range(TILES):
                                last = pe.transpose(ps_turn[:, 128 * j:128 * j + 128], y_cols[:, 128 * j:128 * j + 128],
                                                    g.ident[:, :])
                            last.then_inc(y_turned, 1)
                        if k in (1, 2) and b is not None:
                            if k == 1:
                                pe.wait_ge(xn_t_done, upto(i, 2, b + 1))
                            else:
                                pe.wait_ge(qk_full_done, upto(i, 8, 4 * b + 2))
                            pe.matmul(ps_build[:, :], g.weights_t[:, 1 + k, :], xn_t[:, :], start=True, stop=True)\
                                .then_inc(qk_done, 1)
                        w = batch(i, s + 2)
                        if k == 3 and w is not None:
                            pe.wait_ge(qk_full_done, upto(i, 8, 4 * w + 4))
                            pe.wait_ge(biased, upto(i, 2, w - 2))
                            for j in range(TILES):
                                last = pe.matmul(ps_build[:, 128 * j:128 * j + 128], xn_t[:, 128 * j:128 * j + 128],
                                                 g.weights_t[:, 5, :], start=True, stop=True)
                            last.then_inc(v_done, 1)
                        o = batch(i, s - 3)
                        if k == 4 and o is not None:
                            pe.wait_ge(y_norm_done, upto(i, 4, 2 * o + 2))
                            if not (isinstance(i, int) and 2 * i + o + 3 >= NB):
                                pe.wait_ge(qk_full_done, upto(i, 8, 4 * (o + 3) + 4))
                            for j in range(TILES):
                                last = pe.transpose(ps_build[:, 128 * j:128 * j + 128], y_norm[:, j, :], g.ident[:, :])
                            last.then_inc(y_norm_turned, 1)
                        if k == 6 and o is not None:
                            pe.wait_ge(y_t_done, upto(i, 2, o + 1))
                            for j in range(TILES):
                                last = pe.matmul(ps_build[:, 128 * j:128 * j + 128], y_t[:, 128 * j:128 * j + 128],
                                                 g.weights_t[:, 6, :], start=True, stop=True)
                            last.then_inc(projected, 1)

                run(pe, step)


def x_slot(g, i, b):
    if isinstance(i, int):
        return g.x_all[:, 2 * i + b]
    return g.x_all[:, bass.ds(i * 2 + b, 1)].rearrange("p a j c -> p (a j) c")


def emit_ln_stats(dve, g, i, b, stats, mv, stats_done, mv_done):
    tile = x_slot(g, i, b)
    for j in range(TILES):
        last = dve.bn_stats(stats[:, j, :], tile[:, j, :])
    last.then_inc(stats_done, 1)
    dve.wait_ge(stats_done, upto(i, 2, b + 1))
    dve.sem_inc(g.passed_dve, 1)
    for j in range(TILES):
        last = dve.bn_aggr(mv[:, j, :], stats[:, j, :])
    last.then_inc(mv_done, 1)


def emit_ln_apply(dve, g, i, b, xn, mv, rstd, rstd_done, xn_done):
    tile = x_slot(g, i, b)
    dve.wait_ge(rstd_done, upto(i, 2, b + 1))
    for j in range(TILES):
        last = dve.tensor_scalar(xn[:, j, :], tile[:, j, :], mv[:, j, 0:1], rstd[:, j:j + 1],
                                 ALU.subtract, ALU.mult)
    last.then_inc(xn_done, 1)


def emit_store(nc, g, out):
    out_v = out.rearrange("b (j p) c -> p b j c", p=128)
    with nc.semaphore("out_stored") as out_stored, nc.Block() as block:

        @block.sync
        def _(sp):
            for q in range(4):
                sp.dma_start(out_v[:, 4 * q:4 * q + 4], g.x_all[:, 4 * q:4 * q + 4]).then_inc(out_stored, 16)
            sp.wait_ge(out_stored, 64)


def hybrid_kernel(nc, x, a_w, a_b, b_w, b_b, out_w, out_b, proj, router, gate, up, down, s_gate, s_up, s_down, out,
                  layers="afbf"):
    with ExitStack() as ctx:
        g = allocate_common(nc, ctx)
        emit_setup(nc, g, x, a_w, a_b, b_w, b_b, out_w, out_b, proj, router, gate, up, down, s_gate, s_up, s_down)
        for n, layer in enumerate(layers):
            if layer == "a":
                emit_softmax_attention(nc, g)
            elif layer == "f":
                emit_ffn(nc, g, n)
            else:
                emit_linear_attention(nc, g)
        emit_store(nc, g, out)


_INS = ['L0_attn_a_x', 'L0_attn_a_W', 'L0_attn_a_b', 'L0_attn_b_Wqkv', 'L0_attn_b_bqkv', 'L0_attn_b_Wout',
        'L0_attn_b_bout', 'L0_attn_b_proj', 'L0_ffn_router', 'L0_ffn_experts_gate', 'L0_ffn_experts_up',
        'L0_ffn_experts_down', 'L0_ffn_shared_gate', 'L0_ffn_shared_up', 'L0_ffn_shared_down']
_OUT_SHAPE = (NB, T, C)


def kernel(**inputs):
    import concourse.bacc as bacc
    from concourse.bass_utils import run_bass_kernel_spmd

    nc = bacc.Bacc("TRN2", target_bir_lowering=False, num_devices=1)
    arrays, args = {}, []
    for name in _INS:
        a = np.ascontiguousarray(inputs[name])
        arrays[f"in_{name}"] = a
        args.append(nc.dram_tensor(f"in_{name}", a.shape, mybir.dt.from_np(a.dtype), kind="ExternalInput").ap())
    args.append(nc.dram_tensor("out_x", _OUT_SHAPE, F32, kind="ExternalOutput").ap())
    hybrid_kernel(nc, *args)
    r = run_bass_kernel_spmd(nc, [arrays], core_ids=[0])
    return r.results[0]["out_x"]
```

```python
import numpy as np
import concourse.bass as bass
from concourse import mybir
from contextlib import ExitStack

F32 = mybir.dt.float32
BF16 = mybir.dt.bfloat16
ACT = mybir.ActivationFunctionType
ALU = mybir.AluOpType
AX = mybir.AxisListType

NB, T, C = 16, 512, 128
H, D = 16, 8
TILES = T // 128
HL = 8
PARTS = 3
ROWS = PARTS * PARTS * D
KROWS = 96
MROWS = KROWS + PARTS
E, ED = 8, 64
M = 64
EPS = 1e-5
DELTA = 1e-6
SCALE = float(D) ** -0.5
NEG = -1e30
ORDER = [0, 2, 4, 6, 1, 3, 5, 7]


def upto(i, per, const):
    value = i * per + const
    return max(value, 0) if isinstance(i, int) else value


class Common:
    pass


def allocate_common(nc, ctx):
    g = Common()

    def sb(name, shape, dt=F32):
        return ctx.enter_context(nc.sbuf_tensor(name, shape, dt))

    g.passed_sp = ctx.enter_context(nc.semaphore("passed_sp"))
    g.passed_pool = ctx.enter_context(nc.semaphore("passed_pool"))
    g.passed_dve = ctx.enter_context(nc.semaphore("passed_dve"))
    g.x_all = sb("x_all", [128, NB, TILES, C])
    g.ident = sb("ident", [128, 128])
    g.ident_bf = sb("ident_bf", [128, 128], BF16)
    g.mask_neg = sb("mask_neg", [128, 128], BF16)
    g.causal01 = sb("causal01", [128, 128])
    g.pair_mask = sb("pair_mask", [128, 32])
    g.earlier = sb("earlier", [128, E, E])
    g.half_power = sb("half_power", [128, TILES])
    g.weights_t = sb("weights_t", [128, 7, 128])
    g.qk_bias = sb("qk_bias", [128, 4])
    g.row_bias = sb("row_bias", [128, 3, TILES, C])
    g.proj = sb("proj", [KROWS, H, 3 * M], BF16)
    g.w_gate = sb("w_gate", [128, 5, 128])
    g.w_up = sb("w_up", [128, 5, 128])
    g.w_down = sb("w_down", [128, 5, 128])
    g.w_router = sb("w_router", [128, E])
    g.select = sb("select", [KROWS, E, ED], BF16)
    return g


def emit_setup(nc, g, x, a_w, a_b, b_w, b_b, out_w, out_b, proj, router, gate, up, down, s_gate, s_up, s_down):
    with ExitStack() as ctx:
        sb = lambda name, shape, dt=F32: ctx.enter_context(nc.sbuf_tensor(name, shape, dt))
        sem = lambda name: ctx.enter_context(nc.semaphore(name))
        w_rows = sb("w_rows", [128, 7, 128])
        bias_rows = sb("bias_rows", [1, 3, 128])
        ones_row = sb("ones_row", [1, 128])
        pj = sb("pj", [D, H, M])
        pj_left = sb("pj_left", [D, H, M])
        pj_parts = sb("pj_parts", [D, PARTS, H, M], BF16)
        ps_w = [ctx.enter_context(nc.psum_tensor(f"ps_w{n}", [128, 4, 128], F32)) for n in range(3)]
        x_first = sem("x_first")
        weights_in = sem("weights_in")
        ffn_in = sem("ffn_in")
        x_rest = sem("x_rest")
        proj_in = sem("proj_in")
        filled = sem("filled")
        cleared = sem("cleared")
        select_first = sem("select_first")
        select_stacked = sem("select_stacked")
        constants = sem("constants")
        idents = sem("idents")
        ones_set = sem("ones_set")
        transposed = sem("transposed")
        biases_up = sem("biases_up")
        proj_step = sem("proj_step")
        proj_zeroed = sem("proj_zeroed")
        proj_stacked = sem("proj_stacked")
        copied = sem("copied")

        x_v = x.rearrange("b (j p) c -> p b j c", p=128)
        qk = lambda w, part, f: w[128 * part + 64 * f:128 * part + 64 * f + 64]
        with nc.Block() as block:

            @block.sync
            def _(sp):
                for m, (w, part) in enumerate(((a_w, 0), (a_w, 1), (b_w, 0), (b_w, 1))):
                    for f in range(2):
                        sp.dma_start(w_rows[64 * f:64 * f + 64, m, :],
                                     qk(w, part, f).rearrange("(l d) c -> d l c", d=D)).then_inc(weights_in, 16)
                for m, w in ((4, a_w[256:384, :]), (5, b_w[256:384, :]), (6, out_w)):
                    sp.dma_start(w_rows[:, m, :], w).then_inc(weights_in, 16)
                for m, (b, part) in enumerate(((a_b, 0), (a_b, 1), (b_b, 0), (b_b, 1))):
                    for f in range(2):
                        sp.dma_start(g.qk_bias[64 * f:64 * f + 64, m:m + 1],
                                     qk(b, part, f).rearrange("(l d c) -> d l c", d=D, c=1),
                                     allow_slow_non_contiguous=True).then_inc(weights_in, 16)
                for m, b in enumerate((a_b[256:384], b_b[256:384], out_b)):
                    sp.dma_start(bias_rows[:, m, :], b.rearrange("(a n) -> a n", a=1)).then_inc(weights_in, 16)
                sp.dma_start(pj[:, :, :], proj.rearrange("h d m -> d h m")).then_inc(proj_in, 16)
                for q in range(1, 4):
                    sp.dma_start(g.x_all[:, 4 * q:4 * q + 4], x_v[:, 4 * q:4 * q + 4]).then_inc(x_rest, 16)
                sp.wait_ge(proj_step, 5)
                sp.wait_ge(proj_zeroed, 1)
                for i in range(PARTS):
                    for j in range(PARTS):
                        row = PARTS * D * i + D * j
                        sp.dma_start(g.proj[row:row + D, :, M:2 * M], pj_parts[:, j, :, :]).then_inc(proj_stacked, 16)
                sp.wait_ge(select_first, 1)
                for n in range(1, PARTS):
                    sp.dma_start(g.select[E * n:E * n + E, :, :], g.select[0:E, :, :]).then_inc(select_stacked, 16)
                sp.wait_ge(select_stacked, 16 * (PARTS - 1))
                sp.wait_ge(proj_stacked, 16 * PARTS * PARTS)
                sp.wait_ge(x_rest, 48)
                sp.wait_ge(x_first, 16)
                sp.wait_ge(ffn_in, 16 * 7)

            @block.scalar
            def _(act):
                act.dma_start(g.x_all[:, 0:4], x_v[:, 0:4]).then_inc(x_first, 16)
                for dst, w in ((g.w_gate, gate), (g.w_up, up)):
                    act.dma_start(dst[:, 0:4, :].rearrange("c n (e d) -> c (n e) d", e=2),
                                  w.rearrange("e c d -> c e d")).then_inc(ffn_in, 16)
                act.dma_start(g.w_gate[:, 4, :], s_gate).then_inc(ffn_in, 16)
                act.dma_start(g.w_up[:, 4, :], s_up).then_inc(ffn_in, 16)
                act.dma_start(g.w_down[:, 0:4, :], down.rearrange("(n e) d h -> (e d) n h", e=2)).then_inc(ffn_in, 16)
                act.dma_start(g.w_down[:, 4, :], s_down).then_inc(ffn_in, 16)
                act.dma_start(g.w_router[:, :], router).then_inc(ffn_in, 16)
                act.wait_ge(transposed, 7)
                act.activation(g.weights_t[:, 0:4, :], ps_w[0][:, :, :], ACT.Copy).then_inc(copied, 1)
                act.activation(g.weights_t[:, 4:7, :], ps_w[1][:, 0:3, :], ACT.Copy).then_inc(copied, 1)

            @block.gpsimd
            def _(pool):
                pool.memset(g.ident[:, :], 0.0).then_inc(filled, 1)
                pool.memset(g.mask_neg[:, :], 0.0).then_inc(filled, 1)
                pool.memset(g.causal01[:, :], 1.0).then_inc(filled, 1)
                pool.wait_ge(filled, 3)
                pool.affine_select(out=g.ident[:, :], in_=g.ident[:, :], compare_op=ALU.not_equal, fill=1.0,
                                   base=0, pattern=[[-1, 128]], channel_multiplier=1).then_inc(idents, 1)
                pool.affine_select(out=g.mask_neg[:, :], in_=g.mask_neg[:, :], compare_op=ALU.is_ge, fill=NEG,
                                   base=0, pattern=[[-1, 128]], channel_multiplier=1).then_inc(constants, 1)
                pool.affine_select(out=g.causal01[:, :], in_=g.causal01[:, :], compare_op=ALU.is_ge, fill=0.0,
                                   base=0, pattern=[[1, 128]], channel_multiplier=-1).then_inc(constants, 1)
                pool.memset(g.half_power[:, :], -0.5).then_inc(constants, 1)

            @block.vector
            def _(dve):
                dve.memset(ones_row[:, :], 1.0).then_inc(ones_set, 1)
                dve.memset(g.proj[:, :, :].bitcast(F32), 0.0).then_inc(proj_zeroed, 1)
                dve.memset(g.earlier[:, :, :], 0.0).then_inc(cleared, 1)
                dve.memset(g.pair_mask[:, :], 0.0).then_inc(cleared, 1)
                dve.memset(g.select[:, :, :].bitcast(F32), 0.0).then_inc(cleared, 1)
                dve.wait_ge(cleared, 3)
                for e in range(1, E):
                    dve.memset(g.earlier[:, e, 0:e], 1.0).then_inc(constants, 1)
                for r in range(2):
                    dve.memset(g.pair_mask[M * r:M * r + M, 16 * r:16 * r + 16], 1.0).then_inc(constants, 1)
                dve.wait_ge(idents, 1)
                dve.tensor_copy(g.ident_bf[:, :], g.ident[:, :]).then_inc(constants, 1)
                dve.tensor_copy(g.select[0:E, :, :], g.ident[0:E, 0:E].unsqueeze(2).to_broadcast([E, E, ED]))\
                    .then_inc(select_first, 1)
                dve.wait_ge(proj_in, 16)
                dve.tensor_copy(pj_parts[:, 0], pj[:, :, :]).then_inc(proj_step, 1)
                dve.wait_ge(proj_step, 1)
                dve.tensor_tensor(pj_left[:, :, :], pj[:, :, :], pj_parts[:, 0], ALU.subtract).then_inc(proj_step, 1)
                dve.wait_ge(proj_step, 2)
                dve.tensor_copy(pj_parts[:, 1], pj_left[:, :, :]).then_inc(proj_step, 1)
                dve.wait_ge(proj_step, 3)
                dve.tensor_tensor(pj[:, :, :], pj_left[:, :, :], pj_parts[:, 1], ALU.subtract).then_inc(proj_step, 1)
                dve.wait_ge(proj_step, 4)
                dve.tensor_copy(pj_parts[:, 2], pj[:, :, :]).then_inc(proj_step, 1)
                dve.wait_ge(biases_up, 1)
                for m in range(3):
                    dve.tensor_copy(g.row_bias[:, m],
                                    ps_w[2][:, m:m + 1, :].to_broadcast([128, TILES, C])).then_inc(copied, 1)

            @block.tensor
            def _(pe):
                pe.wait_ge(weights_in, 16 * 22)
                pe.wait_ge(idents, 1)
                for m in range(7):
                    pe.transpose(ps_w[m // 4][:, m % 4, :], w_rows[:, m, :], g.ident[:, :]).then_inc(transposed, 1)
                pe.wait_ge(ones_set, 1)
                for m in range(3):
                    last = pe.matmul(ps_w[2][:, m, :], ones_row[:, :], bias_rows[:, m, :], start=True, stop=True)
                last.then_inc(biases_up, 1)


def emit_softmax_attention(nc, g):
    AHEAD = 6
    PP = 5
    PU, PB = 4, 8
    NP = NB * PB
    NU = 2 * NB
    STACK_DMAS = 2 * PARTS * PARTS
    with ExitStack() as ctx:
        sb = lambda name, shape, dt=F32: ctx.enter_context(nc.sbuf_tensor(name, shape, dt))
        ps = lambda name, shape, dt=F32: ctx.enter_context(nc.psum_tensor(name, shape, dt))
        sem = lambda name: ctx.enter_context(nc.semaphore(name))
        q_stack = [sb(f"q_stack{n}", [MROWS, HL, T], BF16) for n in range(4)]
        k_stack = [sb(f"k_stack{n}", [MROWS, HL, T], BF16) for n in range(4)]
        probs = sb("probs", [128, 2, 4, 3 * 512])
        v_aug = [sb(f"v_aug{n}", [128, TILES, H, 32]) for n in range(2)]
        parts = sb("parts", [128, 2, PARTS, T], BF16)
        qk_full = sb("qk_full", [128, 2, T])
        xn = sb("xn", [128, TILES, C])
        xn_t = sb("xn_t", [128, T])
        ln_stats = sb("ln_stats", [128, TILES, 6])
        ln_mv = sb("ln_mv", [128, TILES, 2])
        ln_var = sb("ln_var", [128, TILES])
        ln_rstd = sb("ln_rstd", [128, TILES])
        row_max = sb("row_max", [128, 2, TILES, HL])
        max_left = sb("max_left", [128, TILES, HL])
        max_parts = sb("max_parts", [128, TILES, PARTS, HL], BF16)
        max_rows = sb("max_rows", [PARTS * HL, T], BF16)
        y_cols = sb("y_cols", [128, T])
        y_recip = sb("y_recip", [128, TILES * HL])
        y_norm = sb("y_norm", [128, TILES * HL, D])
        ps_max = [ps(f"ps_max{n}", [128, 512]) for n in range(2)]
        ps_exp = [ps(f"ps_exp{n}", [128, 512]) for n in range(3)]
        ps_pv = ps("ps_pv", [128, 512])
        ps_build = ps("ps_build", [128, 512])
        ps_turn = ps("ps_turn", [128, 512])
        turn_bf = ps_turn[:, :].bitcast(BF16)

        zeroed = sem("a_zeroed")
        ones_set = sem("a_ones_set")
        stats_done = sem("a_stats_done")
        mv_done = sem("a_mv_done")
        var_done = sem("a_var_done")
        rstd_done = sem("a_rstd_done")
        xn_done = sem("a_xn_done")
        xn_turned = sem("a_xn_turned")
        xn_t_done = sem("a_xn_t_done")
        qk_done = sem("a_qk_done")
        qk_full_done = sem("a_qk_full_done")
        left1_done = sem("a_left1_done")
        mid_done = sem("a_mid_done")
        low_done = sem("a_low_done")
        v_done = sem("a_v_done")
        v_aug_done = sem("a_v_aug_done")
        stacked = [sem(f"a_stacked{f}") for f in range(2)]
        rows_scored = sem("a_rows_scored")
        rows_reduced = sem("a_rows_reduced")
        max_step = sem("a_max_step")
        max_turned = sem("a_max_turned")
        max_rows_done = sem("a_max_rows_done")
        max_stacked = [sem(f"a_max_stacked{f}") for f in range(2)]
        cols_scored = sem("a_cols_scored")
        exp_done = sem("a_exp_done")
        masked = sem("a_masked")
        pv_done = sem("a_pv_done")
        y_cols_done = sem("a_y_cols_done")
        y_turned = sem("a_y_turned")
        y_recip_done = sem("a_y_recip_done")
        y_norm_done = sem("a_y_norm_done")
        x_added = sem("a_x_added")

        LOOPS = NP // 16 - 2
        TAIL = 8

        def run(eng, step):
            for s in range(-15, TAIL):
                step(0, s)
            with eng.Fori(0, LOOPS) as i:
                for s in range(TAIL, TAIL + 16):
                    step(i, s)
            for s in range(TAIL, NP - 16 * LOOPS + 4):
                step(LOOPS, s)

        def falls(i, s, every, offset, count):
            if (s - offset) % every:
                return None
            n = (s - offset) // every
            if isinstance(i, int) and not 0 <= i * (16 // every) + n < count:
                return None
            return n

        COLS = {0: 0, 1: 512, 3: 896, 2: 1024}

        with nc.Block() as block:

            @block.sync
            def _(sp):
                sp.wait_ge(zeroed, 8)

                def step(i, s):
                    for f in range(2):
                        b = falls(i, s, 8, -11 + 2 * f, NB)
                        if b is None:
                            continue
                        u = 2 * b + f
                        sp.wait_ge(low_done, upto(i, 4, 2 * b + 1))
                        sp.sem_inc(g.passed_sp, 1)
                        sp.wait_ge(cols_scored, upto(i, PP * 16, PP * PU * (u - 3)))
                        sp.sem_inc(g.passed_sp, 1)
                        sp.wait_ge(stacked[f], upto(i, 2 * 16 * STACK_DMAS, 16 * STACK_DMAS * b))
                        sp.sem_inc(g.passed_sp, 1)
                        for n in range(PARTS):
                            for c in range(PARTS):
                                row = PARTS * D * n + D * c
                                sp.dma_start(q_stack[u % 4][row:row + D, :, :],
                                             parts[64 * f:64 * f + 64, 0, n, :]).then_inc(stacked[f], 16)
                        sp.wait_ge(low_done, upto(i, 4, 2 * b + 2))
                        sp.sem_inc(g.passed_sp, 1)
                        for n in range(PARTS):
                            for c in range(PARTS):
                                row = PARTS * D * c + D * n
                                sp.dma_start(k_stack[u % 4][row:row + D, :, :],
                                             parts[64 * f:64 * f + 64, 1, n, :]).then_inc(stacked[f], 16)

                run(sp, step)

            @block.gpsimd
            def _(pool):
                def step(i, s):
                    b = falls(i, s, 8, -14, NB)
                    if b is not None:
                        pool.wait_ge(mv_done, upto(i, 2, b + 1))
                        pool.sem_inc(g.passed_pool, 1)
                        pool.tensor_scalar(ln_var[:, :], ln_mv[:, :, 1], EPS, 1.0, ALU.add, ALU.mult)\
                            .then_inc(var_done, 1)
                        pool.wait_ge(var_done, upto(i, 2, b + 1))
                        pool.sem_inc(g.passed_pool, 1)
                        pool.wait_ge(xn_done, upto(i, 2, b))
                        pool.sem_inc(g.passed_pool, 1)
                        pool.tensor_tensor(ln_rstd[:, :], ln_var[:, :], g.half_power[:, :], ALU.pow)\
                            .then_inc(rstd_done, 1)
                    for n in range(2):
                        b = falls(i, s, 8, -12 + n, NB)
                        if b is not None:
                            pool.wait_ge(qk_full_done, upto(i, 8, 4 * b + 2 * n + 2))
                            pool.sem_inc(g.passed_pool, 1)
                            pool.tensor_tensor(qk_full[:, n, :], qk_full[:, n, :], parts[:, n, 0, :], ALU.subtract)\
                                .then_inc(left1_done, 1)
                    p = falls(i, s, 1, 0, NP)
                    if p is not None:
                        pool.wait_ge(exp_done, upto(i, PP * 16, PP * (p + 1)))
                        pool.sem_inc(g.passed_pool, 1)
                        two = probs[:, p // 2 % 2, 2 * (p % 2):2 * (p % 2) + 2, :]
                        tri = dict(compare_op=ALU.is_ge, fill=0.0, base=0, channel_multiplier=-1)
                        d012 = two.rearrange("p h (n c) -> p (h n) c", c=512)[:, :, 0:128]
                        pool.affine_select(out=d012, in_=d012, pattern=[[0, 6], [1, 128]], **tri)\
                            .then_inc(masked, 1)
                        d3 = two[:, :, 896:1024]
                        pool.affine_select(out=d3, in_=d3, pattern=[[0, 2], [1, 128]], **tri).then_inc(masked, 1)
                    for n in range(2):
                        b = falls(i, s, 8, -12 + n, NB)
                        if b is not None:
                            pool.wait_ge(mid_done, upto(i, 4, 2 * b + n + 1))
                            pool.sem_inc(g.passed_pool, 1)
                            pool.tensor_tensor(parts[:, n, 2, :], qk_full[:, n, :], parts[:, n, 1, :], ALU.subtract)\
                                .then_inc(low_done, 1)
                    u = falls(i, s, 4, 6, NU)
                    if u is not None:
                        pool.wait_ge(y_norm_done, upto(i, 4, u + 1))
                        pool.sem_inc(g.passed_pool, 1)
                        b = u // 2
                        tile = x_slot(g, i, b)[:, :, 64 * (u % 2):64 * (u % 2) + 64]
                        pool.tensor_tensor(tile, tile, y_norm[:, :, :].rearrange("p (j h) d -> p j (h d)", j=TILES),
                                           ALU.add).then_inc(x_added, 1)

                run(pool, step)

            @block.scalar
            def _(act):
                def step(i, s):
                    p = falls(i, s, 1, 0, NP)
                    for n in range(PP):
                        if p is not None:
                            quad = p // 2
                            if n == 0 and p % 2 == 0:
                                act.wait_ge(pv_done, upto(i, 8, quad - 1))
                            row = probs[:, quad % 2]
                            act.wait_ge(cols_scored, upto(i, PP * 16, PP * p + n + 1))
                            slot = 2 * (p % 2) + n // 2
                            if n == PP - 1:
                                dst = row[:, 2 * (p % 2):2 * (p % 2) + 2, 1024:1280]
                                src = ps_exp[2][:, :].rearrange("p (h t) -> p h t", h=2)
                            else:
                                dst = row[:, slot, 512 * (n % 2):512 * (n % 2) + 512]
                                src = ps_exp[n % 2][:, :]
                            act.activation(dst, src, ACT.Exp, scale=SCALE).then_inc(exp_done, 1)
                        u = falls(i, s, 4, -1, NU)
                        if n == 0 and u is not None:
                            act.wait_ge(max_rows_done, upto(i, 4, u + 1))
                            act.dma_start(q_stack[u % 4][KROWS:MROWS, :, :], max_rows[:, :])\
                                .then_inc(max_stacked[u % 2], 16)
                        b = falls(i, s, 8, -13, NB)
                        if n == 1 and b is not None:
                            act.wait_ge(xn_turned, upto(i, 2, b + 1))
                            act.wait_ge(v_done, upto(i, 2, b))
                            act.activation(xn_t[:, :], ps_build[:, :], ACT.Copy).then_inc(xn_t_done, 1)
                        for m in range(2):
                            b = falls(i, s, 8, -12 + m, NB)
                            if n == 0 and b is not None:
                                act.wait_ge(qk_done, upto(i, 4, 2 * b + m + 1))
                                act.wait_ge(low_done, upto(i, 4, 2 * b))
                                for f in range(2):
                                    act.wait_ge(stacked[f], upto(i, 2 * 16 * STACK_DMAS, 16 * STACK_DMAS * b))
                                act.activation(parts[:, m, 0, :], ps_build[:, :], ACT.Identity,
                                               bias=g.qk_bias[:, m:m + 1]).then_inc(qk_full_done, 1)
                            if n == 2 and b is not None:
                                act.activation(qk_full[:, m, :], ps_build[:, :], ACT.Identity,
                                               bias=g.qk_bias[:, m:m + 1]).then_inc(qk_full_done, 1)
                    u = falls(i, s, 4, 5, NU)
                    if u is not None:
                        act.wait_ge(pv_done, upto(i, 8, 2 * u + 2))
                        act.wait_ge(y_turned, upto(i, 4, u))
                        act.activation(y_cols[:, :], ps_pv[:, :], ACT.Copy).then_inc(y_cols_done, 1)
                    for n in range(2):
                        b = falls(i, s, 8, -12 + n, NB)
                        if b is not None:
                            act.wait_ge(left1_done, upto(i, 4, 2 * b + n + 1))
                            act.activation(parts[:, n, 1, :], qk_full[:, n, :], ACT.Copy).then_inc(mid_done, 1)
                    u = falls(i, s, 4, -2, NU)
                    if u is not None:
                        act.wait_ge(max_turned, upto(i, 4, u + 1))
                        act.wait_ge(max_stacked[(u - 1) % 2], upto(i, 32, 16 * ((u + 1) // 2)))
                        act.activation(max_rows[:, :], turn_bf[0:PARTS * HL, 0:512], ACT.Copy)\
                            .then_inc(max_rows_done, 1)

                run(act, step)

            @block.vector
            def _(dve):
                for n in range(4):
                    dve.memset(q_stack[n][64:KROWS, :, :].bitcast(F32), 0.0).then_inc(zeroed, 1)
                    dve.memset(k_stack[n][64:KROWS, :, :].bitcast(F32), 0.0).then_inc(zeroed, 1)
                    dve.memset(k_stack[n][KROWS:MROWS, :, :], 1.0).then_inc(ones_set, 1)
                for n in range(2):
                    dve.memset(v_aug[n][:, :, :, :], 0.0).then_inc(zeroed, 1)
                dve.wait_ge(zeroed, 10)
                for n in range(2):
                    for r in range(2):
                        pairs = v_aug[n][:, :, :, :].rearrange("p j (q r) w -> p (j q) r w", r=2)
                        dve.memset(pairs[:, :, r, 16 * r + D:16 * r + D + 1], 1.0).then_inc(ones_set, 1)

                def normalise(i, u):
                    dve.wait_ge(y_turned, upto(i, 4, u + 1))
                    heads = ps_turn[:, :].rearrange("p (n w) -> p n w", w=16)
                    dve.wait_ge(y_norm_done, upto(i, 4, u))
                    dve.reciprocal(y_recip[:, :], heads[:, :, D]).then_inc(y_recip_done, 1)
                    dve.wait_ge(y_recip_done, upto(i, 4, u + 1))
                    dve.wait_ge(x_added, upto(i, 4, u))
                    dve.tensor_tensor(y_norm[:, :, :], heads[:, :, 0:D],
                                      y_recip[:, :].unsqueeze(2).to_broadcast([128, TILES * HL, D]),
                                      ALU.mult).then_inc(y_norm_done, 1)

                def reduce_tile(i, p, n):
                    k, u = p % 4, p // 4
                    if k == 0 and n == 0:
                        dve.wait_ge(max_step, upto(i, 16, 4 * (u - 1)))
                    dve.wait_ge(rows_scored, upto(i, PP * 16, PP * p + n + 1))
                    bank = ps_max[(p + n) % 2]
                    if n == PP - 1:
                        hl = ORDER[2 * k]
                        dve.tensor_reduce(row_max[:, u % 2, 1, hl:hl + 3:2],
                                          bank[:, :].rearrange("p (h s) -> p h s", h=2), axis=AX.X, op=ALU.max)\
                            .then_inc(rows_reduced, 2)
                        return
                    hl = ORDER[2 * k + n // 2]
                    if n % 2 == 0:
                        dve.tensor_reduce(row_max[:, u % 2, 3, hl:hl + 1], bank[:, :], axis=AX.X, op=ALU.max)\
                            .then_inc(rows_reduced, 2)
                    else:
                        dve.tensor_reduce(row_max[:, u % 2, 2, hl:hl + 1], bank[:, 0:384], axis=AX.X,
                                          op=ALU.max).then_inc(rows_reduced, 1)
                        dve.tensor_reduce(row_max[:, u % 2, 0, hl:hl + 1], bank[:, 384:512], axis=AX.X,
                                          op=ALU.max).then_inc(rows_reduced, 1)

                def cut_maxima(i, u, n):
                    top = row_max[:, u % 2]
                    cut = lambda m: max_parts[:, :, m, :]
                    if n == 0:
                        dve.wait_ge(rows_reduced, upto(i, 2 * PP * 16, 2 * PP * PU * (u + 1)))
                        dve.wait_ge(max_turned, upto(i, 4, u))
                        dve.tensor_scalar(cut(0), top, -1.0, None, ALU.mult).then_inc(max_step, 1)
                    elif n == 1:
                        dve.wait_ge(max_step, upto(i, 16, 4 * u + 1))
                        dve.scalar_tensor_tensor(out=max_left[:, :, :], in0=top, scalar=-1.0, in1=cut(0),
                                                 op0=ALU.mult, op1=ALU.subtract).then_inc(max_step, 1)
                    elif n == 2:
                        dve.wait_ge(max_step, upto(i, 16, 4 * u + 2))
                        dve.tensor_copy(cut(1), max_left[:, :, :]).then_inc(max_step, 1)
                    else:
                        dve.wait_ge(max_step, upto(i, 16, 4 * u + 3))
                        dve.tensor_tensor(cut(2), max_left[:, :, :], cut(1), ALU.subtract).then_inc(max_step, 1)

                def step(i, s):
                    p = falls(i, s, 1, -AHEAD, NP)
                    for n in range(PP):
                        if p is not None:
                            reduce_tile(i, p, n)
                        u = falls(i, s, 4, -2, NU)
                        if u is not None and n < 4:
                            cut_maxima(i, u, n)
                        b = falls(i, s, 8, -15, NB)
                        if b is not None and n < TILES:
                            last = dve.bn_stats(ln_stats[:, n, :], x_slot(g, i, b)[:, n, :])
                            if n == TILES - 1:
                                last.then_inc(stats_done, 1)
                        elif b is not None:
                            dve.wait_ge(stats_done, upto(i, 2, b + 1))
                            dve.sem_inc(g.passed_dve, 1)
                            for j in range(TILES):
                                last = dve.bn_aggr(ln_mv[:, j, :], ln_stats[:, j, :])
                            last.then_inc(mv_done, 1)
                        b = falls(i, s, 8, -14, NB)
                        if b is not None and n > 0:
                            j = n - 1
                            if j == 0:
                                dve.wait_ge(rstd_done, upto(i, 2, b + 1))
                                dve.wait_ge(xn_turned, upto(i, 2, b))
                            last = dve.tensor_scalar(xn[:, j, :], x_slot(g, i, b)[:, j, :], ln_mv[:, j, 0:1],
                                                     ln_rstd[:, j:j + 1], ALU.subtract, ALU.mult)
                            if j == TILES - 1:
                                last.then_inc(xn_done, 1)
                        b = falls(i, s, 8, -6, NB)
                        if b is not None and n == 2:
                            dve.wait_ge(v_done, upto(i, 2, b + 1))
                            dve.wait_ge(pv_done, upto(i, 8, 4 * (b - 1)))
                            src = ps_build[:, :].rearrange("p (n r d) -> p n r d", r=2, d=D)
                            bias = g.row_bias[:, 0].rearrange("p j (q r d) -> p (j q) r d", r=2, d=D)
                            pairs = v_aug[b % 2][:, :, :, :].rearrange("p j (q r) w -> p (j q) r w", r=2)
                            for r in range(2):
                                dve.tensor_tensor(pairs[:, :, r, 16 * r:16 * r + D], src[:, :, r, :], bias[:, :, r, :],
                                                  ALU.add).then_inc(v_aug_done, 1)
                        u = falls(i, s, 4, 6, NU)
                        if u is not None and n == 2:
                            normalise(i, u)

                run(dve, step)

            @block.tensor
            def _(pe):
                pe.wait_ge(ones_set, 8)

                def rows(qs, ks, bank, col, hl, j):
                    pe.matmul(bank[:, col:col + 128 * (j + 1)], qs[0:KROWS, hl, 128 * j:128 * j + 128],
                              ks[0:KROWS, hl, 0:128 * (j + 1)], start=True, stop=False)
                    return pe.matmul(bank[:, col + 128 * j:col + 128 * (j + 1)], g.ident_bf[:, :],
                                     g.mask_neg[:, :], start=False, stop=True)

                def rows_tile(i, p, n):
                    k, u = p % 4, p // 4
                    qs, ks = q_stack[u % 4], k_stack[u % 4]
                    if k == 0 and n == 0:
                        pe.wait_ge(stacked[u % 2], upto(i, 2 * 16 * STACK_DMAS, 16 * STACK_DMAS * (u // 2 + 1)))
                    bank = ps_max[(p + n) % 2]
                    pe.wait_ge(rows_reduced, upto(i, 2 * PP * 16, 2 * (PP * p + n - 1)))
                    if n == PP - 1:
                        rows(qs, ks, bank, 0, ORDER[2 * k], 1)
                        last = rows(qs, ks, bank, 256, ORDER[2 * k + 1], 1)
                    elif n % 2 == 0:
                        last = rows(qs, ks, bank, 0, ORDER[2 * k + n // 2], 3)
                    else:
                        rows(qs, ks, bank, 0, ORDER[2 * k + n // 2], 2)
                        last = rows(qs, ks, bank, 384, ORDER[2 * k + n // 2], 0)
                    last.then_inc(rows_scored, 1)

                def cols(qs, ks, bank, col, hl, j):
                    return pe.matmul(bank[:, col:col + T - 128 * j], ks[0:MROWS, hl, 128 * j:128 * j + 128],
                                     qs[0:MROWS, hl, 128 * j:T], start=True, stop=True)

                def cols_tile(i, p, n):
                    k, u = p % 4, p // 4
                    qs, ks = q_stack[u % 4], k_stack[u % 4]
                    if k == 0 and n == 0:
                        pe.wait_ge(max_stacked[u % 2], upto(i, 32, 16 * (u // 2 + 1)))
                    pe.wait_ge(exp_done, upto(i, PP * 16, PP * p + {0: -2, 1: -1, 2: 1, 3: 2, 4: 0}[n]))
                    if n == PP - 1:
                        cols(qs, ks, ps_exp[2], 0, ORDER[2 * k], 2)
                        last = cols(qs, ks, ps_exp[2], 256, ORDER[2 * k + 1], 2)
                    elif n % 2 == 0:
                        last = cols(qs, ks, ps_exp[0], 0, ORDER[2 * k + n // 2], 0)
                    else:
                        cols(qs, ks, ps_exp[1], 0, ORDER[2 * k + n // 2], 1)
                        last = cols(qs, ks, ps_exp[1], 384, ORDER[2 * k + n // 2], 3)
                    last.then_inc(cols_scored, 1)

                def times_values(i, quad, j):
                    b, r, f = quad // 4, quad % 2, quad // 2 % 2
                    if j == 0:
                        pe.wait_ge(masked, upto(i, 32, 4 * quad + 4))
                        pe.wait_ge(v_aug_done, upto(i, 4, 2 * b + 2))
                        if r == 0:
                            pe.wait_ge(y_cols_done, upto(i, 4, quad // 2))
                    for c in range(4):
                        last = pe.matmul(ps_pv[32 * c:32 * c + 32, 128 * j:T],
                                         v_aug[b % 2][:, j, HL * f + 2 * c + r, :],
                                         probs[:, quad % 2, c, COLS[j]:COLS[j] + T - 128 * j],
                                         start=(r == 0 and j == 0), stop=(r == 1 and j == TILES - 1),
                                         skip_group_check=True)
                    if j == TILES - 1:
                        last.then_inc(pv_done, 1)

                def step(i, s):
                    later, now = falls(i, s, 1, -AHEAD, NP), falls(i, s, 1, 0, NP)
                    for n in range(PP):
                        if later is not None:
                            rows_tile(i, later, n)
                        if now is not None:
                            cols_tile(i, now, n)
                        b = falls(i, s, 8, -6, NB)
                        if n == 0 and b is not None:
                            pe.wait_ge(qk_full_done, upto(i, 8, 4 * b + 4))
                            for j in range(TILES):
                                last = pe.matmul(ps_build[:, 128 * j:128 * j + 128], xn_t[:, 128 * j:128 * j + 128],
                                                 g.weights_t[:, 4, :], start=True, stop=True)
                            last.then_inc(v_done, 1)
                        b = falls(i, s, 8, -13, NB)
                        if n == 1 and b is not None:
                            pe.wait_ge(xn_done, upto(i, 2, b + 1))
                            pe.wait_ge(v_aug_done, upto(i, 4, 2 * b))
                            for j in range(TILES):
                                last = pe.transpose(ps_build[:, 128 * j:128 * j + 128], xn[:, j, :], g.ident[:, :])
                            last.then_inc(xn_turned, 1)
                        u = falls(i, s, 4, 6, NU)
                        if n == 0 and u is not None:
                            pe.wait_ge(y_cols_done, upto(i, 4, u + 1))
                            if not (isinstance(i, int) and 4 * i + u + 1 >= NU):
                                pe.wait_ge(max_rows_done, upto(i, 4, u + 2))
                            for j in range(TILES):
                                last = pe.transpose(ps_turn[:, 128 * j:128 * j + 128], y_cols[:, 128 * j:128 * j + 128],
                                                    g.ident[:, :])
                            last.then_inc(y_turned, 1)
                        quad = falls(i, s - (s % 2), 2, 2, NP // 2)
                        if quad is not None and n >= PP - 2:
                            times_values(i, quad, 2 * (s % 2) + n - (PP - 2))
                    u = falls(i, s, 4, -2, NU)
                    if u is not None:
                        pe.wait_ge(max_step, upto(i, 16, 4 * u + 4))
                        pe.wait_ge(y_norm_done, upto(i, 4, u - 1))
                        for j in range(TILES):
                            last = pe.transpose(turn_bf[0:PARTS * HL, 128 * j:128 * j + 128],
                                                max_parts[:, j].rearrange("p n h -> p (n h)"), g.ident_bf[:, :])
                        last.then_inc(max_turned, 1)
                    for n in range(2):
                        b = falls(i, s, 8, -13 + n, NB)
                        if b is not None:
                            if n == 0:
                                pe.wait_ge(xn_t_done, upto(i, 2, b + 1))
                            else:
                                pe.wait_ge(qk_full_done, upto(i, 8, 4 * b + 2))
                            pe.matmul(ps_build[:, :], g.weights_t[:, n, :], xn_t[:, :], start=True, stop=True)\
                                .then_inc(qk_done, 1)

                run(pe, step)


def emit_ffn(nc, g, tag):
    CH = 5
    PR = 4
    with ExitStack() as ctx:
        sb = lambda name, shape, dt=F32: ctx.enter_context(nc.sbuf_tensor(f"f{tag}_{name}", shape, dt))
        ps = lambda name, shape, dt=F32: ctx.enter_context(nc.psum_tensor(f"f{tag}_{name}", shape, dt))
        sem = lambda name: ctx.enter_context(nc.semaphore(f"f{tag}_{name}"))
        xn = sb("xn", [128, TILES, C])
        xn_t = sb("xn_t", [128, 2, T])
        ln_stats = sb("ln_stats", [128, TILES, 6])
        ln_mv = sb("ln_mv", [128, TILES, 2])
        ln_var = sb("ln_var", [128, TILES])
        ln_rstd = sb("ln_rstd", [128, TILES])
        silu = sb("silu", [128, 2, T])
        gated = sb("gated", [128, 2, T])
        hidden = sb("hidden", [128, CH, T])
        top = sb("top", [128, TILES])
        shifted = sb("shifted", [128, TILES, E])
        exps = sb("exps", [128, TILES, E])
        total = sb("total", [128, TILES])
        inv_total = sb("inv_total", [128, TILES])
        prob = sb("prob", [128, TILES, E])
        above = sb("above", [128, TILES, E, E])
        equal = sb("equal", [128, TILES, E, E])
        ties = sb("ties", [128, TILES, E, E])
        rank = sb("rank", [128, TILES, E])
        coef = sb("coef", [128, TILES, E])
        coef_left = sb("coef_left", [128, TILES, E])
        coef_parts = sb("coef_parts", [128, TILES, PARTS, E], BF16)
        coef_rows = sb("coef_rows", [KROWS, T], BF16)
        ps_gate = [ps(f"ps_gate{n}", [128, T]) for n in range(2)]
        ps_up = [ps(f"ps_up{n}", [128, T]) for n in range(2)]
        ps_coef = [ps(f"ps_coef{n}", [128, T]) for n in range(2)]
        ps_out = ps("ps_out", [128, T])
        ps_small = ps("ps_small", [128, T])
        small_bf = ps_small[:, :].bitcast(BF16)

        zeroed = sem("zeroed")
        stats_done = sem("stats_done")
        mv_done = sem("mv_done")
        var_done = sem("var_done")
        rstd_done = sem("rstd_done")
        xn_done = sem("xn_done")
        xn_turned = sem("xn_turned")
        xn_t_done = sem("xn_t_done")
        gate_done = sem("gate_done")
        up_done = sem("up_done")
        silu_done = sem("silu_done")
        gated_done = sem("gated_done")
        weighted = sem("weighted")
        spread = sem("spread")
        down_done = sem("down_done")
        x_added = sem("x_added")
        logits_done = sem("logits_done")
        top_done = sem("top_done")
        shifted_done = sem("shifted_done")
        exps_done = sem("exps_done")
        route = sem("route")
        ROUTE = 13
        coef_turned = sem("coef_turned")
        coef_rows_done = sem("coef_rows_done")

        LOOPS = NB // 2 - 2

        def run(eng, batch):
            for e in range(-2, 2):
                batch(0, e)
            with eng.Fori(0, LOOPS) as i:
                for e in range(2, 4):
                    batch(i, e)
            for e in range(2, NB - 2 * LOOPS + 1):
                batch(LOOPS, e)

        def live(i, e):
            return not isinstance(i, int) or 0 <= 2 * i + e < NB

        with nc.Block() as block:

            @block.gpsimd
            def _(pool):
                def batch(i, e):
                    if live(i, e + 2):
                        pool.wait_ge(mv_done, upto(i, 2, e + 3))
                        pool.sem_inc(g.passed_pool, 1)
                        pool.tensor_scalar(ln_var[:, :], ln_mv[:, :, 1], EPS, 1.0, ALU.add, ALU.mult)\
                            .then_inc(var_done, 1)
                        pool.wait_ge(var_done, upto(i, 2, e + 3))
                        pool.sem_inc(g.passed_pool, 1)
                        pool.wait_ge(xn_done, upto(i, 2, e + 2))
                        pool.sem_inc(g.passed_pool, 1)
                        pool.tensor_tensor(ln_rstd[:, :], ln_var[:, :], g.half_power[:, :], ALU.pow)\
                            .then_inc(rstd_done, 1)

                run(pool, batch)

            @block.scalar
            def _(act):
                def batch(i, e):
                    for n in range(CH):
                        if n == 1 and live(i, e + 1):
                            act.wait_ge(xn_turned, upto(i, 2, e + 2))
                            act.wait_ge(up_done, upto(i, 2 * CH, CH * e))
                            act.activation(xn_t[:, (e + 1) % 2, :], ps_small[:, :], ACT.Copy).then_inc(xn_t_done, 1)
                        if live(i, e):
                            act.wait_ge(gate_done, upto(i, 2 * CH, CH * e + n + 1))
                            act.wait_ge(gated_done, upto(i, 2 * CH, CH * e + n - 1))
                            act.activation(silu[:, (e + n) % 2, :], ps_gate[(e + n) % 2][:, :], ACT.Silu)\
                                .then_inc(silu_done, 1)
                        if n == 2 and live(i, e + 1):
                            act.wait_ge(shifted_done, upto(i, 2, e + 2))
                            act.activation(exps[:, :, :], shifted[:, :, :], ACT.Exp).then_inc(exps_done, 1)
                        if n == 0 and live(i, e):
                            act.wait_ge(coef_turned, upto(i, 2, e + 1))
                            act.wait_ge(spread, upto(i, 2 * PR, PR * e))
                            act.activation(coef_rows[0:PARTS * E, :], small_bf[0:PARTS * E, 0:T], ACT.Copy)\
                                .then_inc(coef_rows_done, 1)

                run(act, batch)

            @block.vector
            def _(dve):
                dve.memset(coef_rows[:, :].bitcast(F32), 0.0).then_inc(zeroed, 1)

                def route_step(i, e, k):
                    each = prob[:, :, :].unsqueeze(3).to_broadcast([128, TILES, E, E])
                    other = prob[:, :, :].unsqueeze(2).to_broadcast([128, TILES, E, E])
                    cut = lambda k: coef_parts[:, :, k, :]
                    if k == 0:
                        dve.wait_ge(exps_done, upto(i, 2, e + 1))
                        ins = dve.tensor_reduce(total[:, :], exps[:, :, :], axis=AX.X, op=ALU.add)
                    else:
                        dve.wait_ge(route, upto(i, 2 * ROUTE, ROUTE * e + k))
                    if k == 1:
                        ins = dve.reciprocal(inv_total[:, :], total[:, :])
                    if k == 2:
                        ins = dve.tensor_tensor(prob[:, :, :], exps[:, :, :],
                                                inv_total[:, :].unsqueeze(2).to_broadcast([128, TILES, E]), ALU.mult)
                    if k == 3:
                        ins = dve.tensor_tensor(equal[:, :, :, :], other, each, ALU.is_equal)
                    if k == 4:
                        ins = dve.tensor_tensor(ties[:, :, :, :].rearrange("p j e f -> p j (e f)"),
                                                equal[:, :, :, :].rearrange("p j e f -> p j (e f)"),
                                                g.earlier[:, :, :].rearrange("p e f -> p (e f)").unsqueeze(1)
                                                .to_broadcast([128, TILES, E * E]), ALU.mult)
                    if k == 5:
                        ins = dve.tensor_tensor(above[:, :, :, :], other, each, ALU.is_gt)
                    if k == 6:
                        ins = dve.tensor_tensor(above[:, :, :, :], above[:, :, :, :], ties[:, :, :, :], ALU.add)
                    if k == 7:
                        ins = dve.tensor_reduce(rank[:, :, :], above[:, :, :, :], axis=AX.X, op=ALU.add)
                    if k == 8:
                        ins = dve.scalar_tensor_tensor(out=coef[:, :, :], in0=rank[:, :, :], scalar=1.5,
                                                       in1=prob[:, :, :], op0=ALU.is_lt, op1=ALU.mult)
                    if k == 9:
                        dve.wait_ge(coef_turned, upto(i, 2, e))
                        ins = dve.tensor_copy(cut(0), coef[:, :, :])
                    if k == 10:
                        ins = dve.tensor_tensor(coef_left[:, :, :], coef[:, :, :], cut(0), ALU.subtract)
                    if k == 11:
                        ins = dve.tensor_copy(cut(1), coef_left[:, :, :])
                    if k == 12:
                        ins = dve.tensor_tensor(cut(2), coef_left[:, :, :], cut(1), ALU.subtract)
                    ins.then_inc(route, 1)

                ROUTE_BEFORE = {3: (2, 3), 4: (7, 8, 9, 10, 11, 12)}
                ROUTE_AFTER = {2: (0, 1), 3: (4, 5, 6)}

                def batch(i, e):
                    for n in range(CH):
                        if n == 2 and live(i, e - 1):
                            dve.wait_ge(down_done, upto(i, 2 * CH, CH * e))
                            tile = x_slot(g, i, e - 1)
                            dve.tensor_tensor(tile, tile, ps_out[:, :].rearrange("p (j c) -> p j c", j=TILES), ALU.add)\
                                .then_inc(x_added, 1)
                        if n == 2 and live(i, e + 1):
                            dve.wait_ge(logits_done, upto(i, 2, e + 2))
                            logits = ps_small[:, 0:TILES * E].rearrange("p (j e) -> p j e", e=E)
                            dve.tensor_reduce(top[:, :], logits, axis=AX.X, op=ALU.max).then_inc(top_done, 1)
                            dve.wait_ge(top_done, upto(i, 2, e + 2))
                            dve.wait_ge(exps_done, upto(i, 2, e + 1))
                            dve.tensor_tensor(shifted[:, :, :], logits, top[:, :].unsqueeze(2).to_broadcast([128, TILES, E]),
                                              ALU.subtract).then_inc(shifted_done, 1)
                        last = n == CH - 1
                        par = (e + n) % 2
                        if live(i, e):
                            dve.wait_ge(silu_done, upto(i, 2 * CH, CH * e + n + 1))
                            dve.wait_ge(up_done, upto(i, 2 * CH, CH * e + n + 1))
                            dst = hidden[:, n, :] if last else gated[:, par, :]
                            if last:
                                dve.wait_ge(down_done, upto(i, 2 * CH, CH * e))
                            else:
                                dve.wait_ge(weighted, upto(i, 2 * PR, PR * e + n - 1))
                            dve.tensor_tensor(dst, ps_up[par][:, :], silu[:, par, :], ALU.mult).then_inc(gated_done, 1)
                        if live(i, e + 1):
                            for k in ROUTE_BEFORE.get(n, ()):
                                route_step(i, e + 1, k)
                        if live(i, e) and not last:
                            dve.wait_ge(gated_done, upto(i, 2 * CH, CH * e + n + 1))
                            dve.wait_ge(spread, upto(i, 2 * PR, PR * e + n + 1))
                            dve.wait_ge(down_done, upto(i, 2 * CH, CH * (e - 1) + n + 1))
                            dve.tensor_tensor(hidden[:, n, :], ps_coef[n % 2][:, :], gated[:, par, :], ALU.mult)\
                                .then_inc(weighted, 1)
                        if live(i, e + 1):
                            for k in ROUTE_AFTER.get(n, ()):
                                route_step(i, e + 1, k)
                        if n == 0 and live(i, e + 2):
                            emit_ln_stats(dve, g, i, e + 2, ln_stats, ln_mv, stats_done, mv_done)
                        if n == 1 and live(i, e + 2):
                            dve.wait_ge(xn_turned, upto(i, 2, e + 2))
                            emit_ln_apply(dve, g, i, e + 2, xn, ln_mv, ln_rstd, rstd_done, xn_done)

                run(dve, batch)

            @block.tensor
            def _(pe):
                pe.wait_ge(zeroed, 1)

                def down(i, e, n):
                    if n == CH - 1:
                        pe.wait_ge(gated_done, upto(i, 2 * CH, CH * e + CH))
                    else:
                        pe.wait_ge(weighted, upto(i, 2 * PR, PR * e + n + 1))
                    if n == 0:
                        pe.wait_ge(x_added, upto(i, 2, e))
                    for j in range(TILES):
                        last = pe.matmul(ps_out[:, 128 * j:128 * j + 128], hidden[:, n, 128 * j:128 * j + 128],
                                         g.w_down[:, n, :], start=(n == 0 and j == 0), stop=(n == CH - 1),
                                         skip_group_check=True)
                    last.then_inc(down_done, 1)

                def batch(i, e):
                    for n in range(CH):
                        if live(i, e):
                            par = (e + n) % 2
                            xt = xn_t[:, e % 2, :]
                            if n == 0:
                                pe.wait_ge(xn_t_done, upto(i, 2, e + 1))
                            pe.wait_ge(silu_done, upto(i, 2 * CH, CH * e + n - 1))
                            pe.matmul(ps_gate[par][:, :], g.w_gate[:, n, :], xt, start=True, stop=True)\
                                .then_inc(gate_done, 1)
                            pe.wait_ge(gated_done, upto(i, 2 * CH, CH * e + n - 1))
                            pe.matmul(ps_up[par][:, :], g.w_up[:, n, :], xt, start=True, stop=True)\
                                .then_inc(up_done, 1)
                            if 0 < n < PR:
                                pe.wait_ge(weighted, upto(i, 2 * PR, PR * e + n - 1))
                                pe.matmul(ps_coef[n % 2][:, :],
                                          g.select[:, 2 * n:2 * n + 2, :].rearrange("p e d -> p (e d)"),
                                          coef_rows[:, :], start=True, stop=True).then_inc(spread, 1)
                        if n == 0 and live(i, e):
                            pe.wait_ge(route, upto(i, 2 * ROUTE, ROUTE * (e + 1)))
                            for j in range(TILES):
                                last = pe.transpose(small_bf[0:PARTS * E, 128 * j:128 * j + 128],
                                                    coef_parts[:, j].rearrange("p n e -> p (n e)"), g.ident_bf[:, :])
                            last.then_inc(coef_turned, 1)
                        if n < 2 and live(i, e - 1):
                            down(i, e - 1, n + 3)
                        if n == 0 and live(i, e):
                            pe.wait_ge(coef_rows_done, upto(i, 2, e + 1))
                            pe.wait_ge(weighted, upto(i, 2 * PR, PR * e - 1))
                            pe.matmul(ps_coef[0][:, :], g.select[:, 0:2, :].rearrange("p e d -> p (e d)"),
                                      coef_rows[:, :], start=True, stop=True).then_inc(spread, 1)
                        if n >= 2 and live(i, e):
                            down(i, e, n - 2)
                        if n == 0 and live(i, e + 1):
                            pe.wait_ge(xn_done, upto(i, 2, e + 2))
                            pe.wait_ge(coef_rows_done, upto(i, 2, e + 1))
                            for j in range(TILES):
                                last = pe.transpose(ps_small[:, 128 * j:128 * j + 128], xn[:, j, :], g.ident[:, :])
                            last.then_inc(xn_turned, 1)
                        if n == 1 and live(i, e + 1):
                            pe.wait_ge(xn_t_done, upto(i, 2, e + 2))
                            for j in range(TILES):
                                last = pe.matmul(ps_small[:, E * j:E * j + E],
                                                 xn_t[:, (e + 1) % 2, 128 * j:128 * j + 128], g.w_router[:, :],
                                                 start=True, stop=True)
                            last.then_inc(logits_done, 1)

                run(pe, batch)


def emit_linear_attention(nc, g):
    PU = 4
    NU = 2 * NB
    KEY_TOK, KEY_FEAT, QUERY = range(3)
    OTHERS = [(KEY_TOK, j) for j in range(TILES - 1)] + [(QUERY, c) for c in range(PU)]
    TILE_OF = [t for k in range(HL) for t in OTHERS[k:k + 1] + [(KEY_FEAT, k)]]
    FEATS = len(TILE_OF)
    STACK_DMAS = 2 * PARTS * PARTS
    with ExitStack() as ctx:
        sb = lambda name, shape, dt=F32: ctx.enter_context(nc.sbuf_tensor(f"l_{name}", shape, dt))
        ps = lambda name, shape, dt=F32: ctx.enter_context(nc.psum_tensor(f"l_{name}", shape, dt))
        sem = lambda name: ctx.enter_context(nc.semaphore(f"l_{name}"))
        q_stack = [sb(f"q_stack{n}", [KROWS, HL, T], BF16) for n in range(2)]
        k_stack = [sb(f"k_stack{n}", [KROWS, HL, T], BF16) for n in range(2)]
        key_tok = sb("key_tok", [128, 2, TILES - 1, HL * M])
        key_feat = sb("key_feat", [128, HL, T])
        query_feat = sb("query_feat", [128, 2, PU, T])
        attn = sb("attn", [128, HL, TILES, 128])
        v_aug = [sb(f"v_aug{n}", [128, TILES, H // 2, 64]) for n in range(2)]
        parts = [sb(f"parts{n}", [128, 2, PARTS, T], BF16) for n in range(2)]
        qk_full = sb("qk_full", [128, 2, T])
        xn = sb("xn", [128, TILES, C])
        xn_t = sb("xn_t", [128, T])
        ln_stats = sb("ln_stats", [128, TILES, 6])
        ln_mv = sb("ln_mv", [128, TILES, 2])
        ln_var = sb("ln_var", [128, TILES])
        ln_rstd = sb("ln_rstd", [128, TILES])
        state_cols = sb("state_cols", [128, 128])
        state = sb("state", [128, TILES - 1, PU * 32])
        y_cols = sb("y_cols", [128, T])
        y_sum = sb("y_sum", [128, TILES * HL])
        y_recip = sb("y_recip", [128, TILES * HL])
        y_norm = sb("y_norm", [128, TILES, C])
        y_t = sb("y_t", [128, T])
        y_out = sb("y_out", [128, TILES, C])
        ps_feat = [ps(f"ps_feat{n}", [128, T]) for n in range(2)]
        ps_attn = [ps(f"ps_attn{n}", [128, T]) for n in range(2)]
        ps_pv = ps("ps_pv", [128, T])
        ps_state = ps("ps_state", [128, T])
        ps_turn = ps("ps_turn", [128, T])
        ps_build = ps("ps_build", [128, T])

        zeroed = sem("zeroed")
        ones_set = sem("ones_set")
        stats_done = sem("stats_done")
        mv_done = sem("mv_done")
        var_done = sem("var_done")
        rstd_done = sem("rstd_done")
        xn_done = sem("xn_done")
        xn_turned = sem("xn_turned")
        xn_t_done = sem("xn_t_done")
        qk_done = sem("qk_done")
        qk_full_done = sem("qk_full_done")
        left1_done = sem("left1_done")
        mid_done = sem("mid_done")
        low_done = sem("low_done")
        v_done = sem("v_done")
        v_aug_done = sem("v_aug_done")
        stacked = [sem(f"stacked{f}") for f in range(2)]
        feat_done = sem("feat_done")
        feat_out = sem("feat_out")
        scored = sem("scored")
        attn_done = sem("attn_done")
        within_done = sem("within_done")
        hist_done = sem("hist_done")
        summed = sem("summed")
        state_cols_done = sem("state_cols_done")
        state_turned = sem("state_turned")
        state_done = sem("state_done")
        y_cols_done = sem("y_cols_done")
        y_turned = sem("y_turned")
        y_sum_done = sem("y_sum_done")
        y_recip_done = sem("y_recip_done")
        y_norm_done = sem("y_norm_done")
        y_norm_turned = sem("y_norm_turned")
        y_t_done = sem("y_t_done")
        projected = sem("projected")
        biased = sem("biased")
        x_added = sem("x_added")

        FIRST, BODY, LOOPS = -4, 8, 5

        def run(eng, step):
            for s in range(FIRST, BODY):
                step(0, s)
            with eng.Fori(0, LOOPS) as i:
                for s in range(BODY, BODY + 4):
                    step(i, s)
            for s in range(BODY, NU - 4 * LOOPS + 2):
                step(LOOPS, s)

        def unit(i, s):
            return s if not isinstance(i, int) or 0 <= 4 * i + s < NU else None

        def batch(i, s2):
            return s2 // 2 if s2 % 2 == 0 and (not isinstance(i, int) or 0 <= 2 * i + s2 // 2 < NB) else None

        with nc.Block() as block:

            @block.sync
            def _(sp):
                sp.wait_ge(zeroed, 4)

                def step(i, s):
                    b = batch(i, s + 3)
                    if b is not None:
                        sp.wait_ge(low_done, upto(i, 4, 2 * b + 2))
                        sp.sem_inc(g.passed_sp, 1)
                        for f in range(2):
                            u = 2 * b + f
                            sp.wait_ge(feat_done, upto(i, 4 * FEATS, FEATS * (u - 1)))
                            sp.sem_inc(g.passed_sp, 1)
                            sp.wait_ge(stacked[f], upto(i, 2 * 16 * STACK_DMAS, 16 * STACK_DMAS * b))
                            sp.sem_inc(g.passed_sp, 1)
                            for n in range(PARTS):
                                for c in range(PARTS):
                                    row = PARTS * D * n + D * c
                                    for m, stack in enumerate((q_stack, k_stack)):
                                        sp.dma_start(stack[u % 2][row:row + D, :, :],
                                                     parts[b % 2][64 * f:64 * f + 64, m, n, :]).then_inc(stacked[f], 16)

                run(sp, step)

            @block.gpsimd
            def _(pool):
                def step(i, s):
                    for k in range(8):
                        b = batch(i, s + 4)
                        if k == 4 and b is not None:
                            pool.wait_ge(mv_done, upto(i, 2, b + 1))
                            pool.sem_inc(g.passed_pool, 1)
                            pool.tensor_scalar(ln_var[:, :], ln_mv[:, :, 1], EPS, 1.0, ALU.add, ALU.mult)\
                                .then_inc(var_done, 1)
                            pool.wait_ge(var_done, upto(i, 2, b + 1))
                            pool.sem_inc(g.passed_pool, 1)
                            pool.wait_ge(xn_done, upto(i, 2, b))
                            pool.sem_inc(g.passed_pool, 1)
                            pool.tensor_tensor(ln_rstd[:, :], ln_var[:, :], g.half_power[:, :], ALU.pow)\
                                .then_inc(rstd_done, 1)
                        b = batch(i, s + 3)
                        if k in (2, 3) and b is not None:
                            n = k - 2
                            pool.wait_ge(qk_full_done, upto(i, 8, 4 * b + 2 * n + 2))
                            pool.sem_inc(g.passed_pool, 1)
                            pool.tensor_tensor(qk_full[:, n, :], qk_full[:, n, :], parts[b % 2][:, n, 0, :], ALU.subtract)\
                                .then_inc(left1_done, 1)
                            pool.wait_ge(mid_done, upto(i, 4, 2 * b + n + 1))
                            pool.sem_inc(g.passed_pool, 1)
                            pool.tensor_tensor(parts[b % 2][:, n, 2, :], qk_full[:, n, :], parts[b % 2][:, n, 1, :], ALU.subtract)\
                                .then_inc(low_done, 1)
                        b = batch(i, s - 3)
                        if k == 6 and b is not None:
                            pool.wait_ge(biased, upto(i, 2, b + 1))
                            pool.sem_inc(g.passed_pool, 1)
                            tile = x_slot(g, i, b)
                            pool.tensor_tensor(tile, tile, y_out[:, :, :], ALU.add).then_inc(x_added, 1)

                run(pool, step)

            @block.scalar
            def _(act):
                def step(i, s):
                    for k in range(8):
                        b = batch(i, s + 3)
                        if k in (2, 3) and b is not None:
                            n = k - 2
                            act.wait_ge(qk_done, upto(i, 4, 2 * b + n + 1))
                            act.wait_ge(low_done, upto(i, 4, 2 * b))
                            for f in range(2):
                                act.wait_ge(stacked[f], upto(i, 2 * 16 * STACK_DMAS, 16 * STACK_DMAS * (b - 1)))
                            act.activation(qk_full[:, n, :], ps_build[:, :], ACT.Identity,
                                           bias=g.qk_bias[:, 2 + n:3 + n]).then_inc(qk_full_done, 1)
                            act.activation(parts[b % 2][:, n, 0, :], ps_build[:, :], ACT.Identity,
                                           bias=g.qk_bias[:, 2 + n:3 + n]).then_inc(qk_full_done, 1)
                        b = batch(i, s - 3)
                        if k == 5 and b is not None:
                            act.wait_ge(y_norm_turned, upto(i, 2, b + 1))
                            act.wait_ge(projected, upto(i, 2, b))
                            act.activation(y_t[:, :], ps_build[:, :], ACT.Copy).then_inc(y_t_done, 1)
                        u = unit(i, s - 1)
                        if k == 3 and u is not None:
                            act.wait_ge(hist_done, upto(i, 4, u + 1))
                            act.wait_ge(y_turned, upto(i, 4, u))
                            act.activation(y_cols[:, :], ps_pv[:, :], ACT.Copy).then_inc(y_cols_done, 1)
                        u = unit(i, s)
                        if k in (3, 4, 5) and u is not None:
                            j = k - 3
                            act.wait_ge(summed, upto(i, 12, 3 * u + j + 1))
                            act.wait_ge(state_turned, upto(i, 12, 3 * u + j))
                            act.activation(state_cols[:, :], ps_state[:, 0:128], ACT.Copy).then_inc(state_cols_done, 1)
                        u = unit(i, s + 1)
                        if u is not None:
                            for n in range(2 * k, min(2 * k + 2, FEATS)):
                                kind, m = TILE_OF[n]
                                src = ps_feat[(u + n) % 2]
                                if kind == KEY_TOK:
                                    dst = key_tok[:, u % 2, m, :]
                                    act.wait_ge(summed, upto(i, 12, 3 * (u - 1)))
                                elif kind == KEY_FEAT:
                                    dst = key_feat[:, ORDER[m], :]
                                    act.wait_ge(scored, upto(i, 32, HL * (u - 1) + m + 1))
                                else:
                                    dst = query_feat[:, u % 2, m, :]
                                    act.wait_ge(hist_done, upto(i, 4, u - 1))
                                act.wait_ge(feat_done, upto(i, 4 * FEATS, FEATS * u + n + 1))
                                act.activation(dst, src[:, :], ACT.Relu).then_inc(feat_out, 1)
                        b = batch(i, s + 3)
                        if k == 0 and b is not None:
                            act.wait_ge(xn_turned, upto(i, 2, b + 1))
                            act.wait_ge(v_done, upto(i, 2, b))
                            act.activation(xn_t[:, :], ps_build[:, :], ACT.Copy).then_inc(xn_t_done, 1)
                        if k in (3, 4) and b is not None:
                            n = k - 3
                            act.wait_ge(left1_done, upto(i, 4, 2 * b + n + 1))
                            act.activation(parts[b % 2][:, n, 1, :], qk_full[:, n, :], ACT.Copy).then_inc(mid_done, 1)

                run(act, step)

            @block.vector
            def _(dve):
                for n in range(2):
                    dve.memset(q_stack[n][64:KROWS, :, :].bitcast(F32), 0.0).then_inc(zeroed, 1)
                    dve.memset(k_stack[n][64:KROWS, :, :].bitcast(F32), 0.0).then_inc(zeroed, 1)
                for n in range(2):
                    dve.memset(v_aug[n][:, :, :, :], 0.0).then_inc(zeroed, 1)
                dve.wait_ge(zeroed, 6)
                for n in range(2):
                    for r in range(2):
                        at = 32 - 16 * r
                        dve.memset(v_aug[n][:, :, :, at + D:at + D + 1], 1.0).then_inc(ones_set, 1)

                def step(i, s):
                    for k in range(8):
                        b = batch(i, s + 2)
                        if k == 4 and b is not None:
                            dve.wait_ge(v_done, upto(i, 2, b + 1))
                            dve.wait_ge(hist_done, upto(i, 4, 2 * (b - 1)))
                            src = ps_build[:, :].rearrange("p (n r d) -> p n r d", r=2, d=D)
                            bias = g.row_bias[:, 1].rearrange("p j (q r d) -> p (j q) r d", r=2, d=D)
                            pairs = v_aug[b % 2][:, :, :, :].rearrange("p j q w -> p (j q) w")
                            for r in range(2):
                                at = 32 - 16 * r
                                dve.tensor_tensor(pairs[:, :, at:at + D], src[:, :, r, :], bias[:, :, r, :],
                                                  ALU.add).then_inc(v_aug_done, 1)
                        u = unit(i, s - 2)
                        if k == 0 and u is not None:
                            dve.wait_ge(y_turned, upto(i, 4, u + 1))
                            heads = ps_turn[:, :].rearrange("p (n w) -> p n w", w=16)
                            dve.wait_ge(y_norm_done, upto(i, 4, u))
                            dve.tensor_scalar(y_sum[:, :], heads[:, :, D], DELTA, None, ALU.add).then_inc(y_sum_done, 1)
                            dve.wait_ge(y_sum_done, upto(i, 4, u + 1))
                            dve.reciprocal(y_recip[:, :], y_sum[:, :]).then_inc(y_recip_done, 1)
                            dve.wait_ge(y_recip_done, upto(i, 4, u + 1))
                            dve.wait_ge(y_norm_turned, upto(i, 2, u // 2))
                            f = u % 2
                            dve.tensor_tensor(y_norm[:, :, 64 * f:64 * f + 64].rearrange("p j (h d) -> p j h d", d=D),
                                              ps_turn[:, :].rearrange("p (j h w) -> p j h w", j=TILES, w=16)[:, :, :, 0:D],
                                              y_recip[:, :].rearrange("p (j h) -> p j h", j=TILES).unsqueeze(3)
                                              .to_broadcast([128, TILES, HL, D]), ALU.mult).then_inc(y_norm_done, 1)
                        b = batch(i, s - 3)
                        if k == 7 and b is not None:
                            dve.wait_ge(projected, upto(i, 2, b + 1))
                            dve.wait_ge(x_added, upto(i, 2, b))
                            dve.tensor_tensor(y_out[:, :, :], ps_build[:, :].rearrange("p (j c) -> p j c", j=TILES),
                                              g.row_bias[:, 2], ALU.add).then_inc(biased, 1)
                        u = unit(i, s)
                        if k in (4, 5, 6) and u is not None:
                            j = k - 4
                            dve.wait_ge(state_turned, upto(i, 12, 3 * u + j + 1))
                            dve.wait_ge(hist_done, upto(i, 4, u))
                            for r in range(2):
                                dve.tensor_tensor(state[:, j, :].rearrange("p (q w) -> p q w", q=PU)[:, :, 16 * r:16 * r + 16],
                                                  ps_turn[:, 128 * j:128 * j + 128].rearrange("p (q w) -> p q w", q=PU)
                                                  [:, :, 16 - 16 * r:32 - 16 * r],
                                                  g.pair_mask[:, 16 * r:16 * r + 16].unsqueeze(1)
                                                  .to_broadcast([128, PU, 16]), ALU.mult).then_inc(state_done, 1)
                        if u is not None:
                            hl = ORDER[k]
                            dve.wait_ge(scored, upto(i, 32, HL * u + k + 1))
                            dve.wait_ge(within_done, upto(i, 8, 2 * (u - 1) + k // 4 + 1))
                            dve.tensor_tensor(attn[:, hl, :, :], ps_attn[k % 2][:, :].rearrange("p (j t) -> p j t", j=TILES),
                                              g.causal01[:, :].unsqueeze(1).to_broadcast([128, TILES, 128]),
                                              ALU.mult).then_inc(attn_done, 1)
                        b = batch(i, s + 4)
                        if k == 3 and b is not None:
                            emit_ln_stats(dve, g, i, b, ln_stats, ln_mv, stats_done, mv_done)
                        if k == 6 and b is not None:
                            dve.wait_ge(xn_turned, upto(i, 2, b))
                            emit_ln_apply(dve, g, i, b, xn, ln_mv, ln_rstd, rstd_done, xn_done)

                run(dve, step)

            @block.tensor
            def _(pe):
                pe.wait_ge(ones_set, 4)

                def features(i, u, n):
                    bank, f = ps_feat[(u + n) % 2], u % 2
                    ks, qs = k_stack[u % 2], q_stack[u % 2]
                    if n == 0:
                        pe.wait_ge(stacked[f], upto(i, 2 * 16 * STACK_DMAS, 16 * STACK_DMAS * (u // 2 + 1)))
                    pe.wait_ge(feat_out, upto(i, 4 * FEATS, FEATS * u + n - 1))
                    kind, m = TILE_OF[n]
                    if kind == KEY_TOK:
                        for hl in range(HL):
                            last = pe.matmul(bank[:, M * hl:M * hl + M], ks[:, hl, 128 * m:128 * m + 128],
                                             g.proj[:, HL * f + hl, M:2 * M], start=True, stop=True)
                    elif kind == KEY_FEAT:
                        hl = ORDER[m]
                        at = M * (1 - hl % 2)
                        last = pe.matmul(bank[:, :], g.proj[:, HL * f + hl, at:at + 2 * M], ks[:, hl, :],
                                         start=True, stop=True)
                    else:
                        for r in range(2):
                            hl = 2 * m + r
                            last = pe.matmul(bank[M * r:M * r + M, :], g.proj[:, HL * f + hl, M:2 * M], qs[:, hl, :],
                                             start=True, stop=True)
                    last.then_inc(feat_done, 1)

                def within(i, u, r):
                    f = u % 2
                    pe.wait_ge(attn_done, upto(i, 32, HL * u + 4 * r + 4))
                    if r == 0:
                        pe.wait_ge(y_cols_done, upto(i, 4, u))
                        pe.wait_ge(v_aug_done, upto(i, 4, 2 * (u // 2) + 2))
                    for j in range(TILES):
                        for c in range(PU):
                            last = pe.matmul(ps_pv[32 * c:32 * c + 32, 128 * j:128 * j + 128],
                                             v_aug[u // 2 % 2][:, j, PU * f + c, 32 - 32 * r:64 - 32 * r], attn[:, 2 * c + r, j, :],
                                             start=(r == 0 and j == 0), stop=False, skip_group_check=True)
                    last.then_inc(within_done, 1)

                def sums(i, u, j):
                    pe.wait_ge(state_cols_done, upto(i, 12, 3 * u + j))
                    if j == 0:
                        pe.wait_ge(v_aug_done, upto(i, 4, 2 * (u // 2) + 2))
                    for c in range(PU):
                        last = pe.matmul(ps_state[32 * c:32 * c + 32, 0:128],
                                         v_aug[u // 2 % 2][:, j, PU * (u % 2) + c, 16:48],
                                         key_tok[:, u % 2, j, 128 * c:128 * c + 128],
                                         start=(j == 0), stop=(j == TILES - 2), skip_group_check=True)
                    last.then_inc(summed, 1)

                def step(i, s):
                    for k in range(8):
                        b = batch(i, s + 3)
                        if k == 0 and b is not None:
                            pe.wait_ge(xn_done, upto(i, 2, b + 1))
                            pe.wait_ge(v_aug_done, upto(i, 4, 2 * b))
                            for j in range(TILES):
                                last = pe.transpose(ps_build[:, 128 * j:128 * j + 128], xn[:, j, :], g.ident[:, :])
                            last.then_inc(xn_turned, 1)
                        nxt = unit(i, s + 1)
                        if nxt is not None:
                            features(i, nxt, 2 * k)
                        u = unit(i, s)
                        if u is not None:
                            hl = ORDER[k]
                            if k == 0:
                                pe.wait_ge(feat_out, upto(i, 4 * FEATS, FEATS * (u + 1)))
                            pe.wait_ge(attn_done, upto(i, 32, HL * u + k - 1))
                            for j in range(TILES):
                                last = pe.matmul(ps_attn[k % 2][:, 128 * j:128 * j + 128],
                                                 key_feat[:, hl, 128 * j:128 * j + 128],
                                                 query_feat[:, u % 2, hl // 2, 128 * j:128 * j + 128],
                                                 start=True, stop=True)
                            last.then_inc(scored, 1)
                        if nxt is not None and 2 * k + 1 < FEATS:
                            features(i, nxt, 2 * k + 1)
                        v = unit(i, s - 1)
                        if k == 1 and v is not None:
                            within(i, v, 1)
                        if k == 2 and v is not None:
                            pe.wait_ge(state_done, upto(i, 24, 6 * v + 6))
                            for j in range(1, TILES):
                                for c in range(PU):
                                    last = pe.matmul(ps_pv[32 * c:32 * c + 32, 128 * j:128 * j + 128],
                                                     state[:, j - 1, 32 * c:32 * c + 32],
                                                     query_feat[:, v % 2, c, 128 * j:128 * j + 128],
                                                     start=False, stop=(j == TILES - 1), skip_group_check=True)
                            last.then_inc(hist_done, 1)
                        if k == 2 and u is not None:
                            sums(i, u, 0)
                        if k in (3, 4, 5) and u is not None:
                            j = k - 3
                            if j < 2:
                                sums(i, u, j + 1)
                            pe.wait_ge(state_cols_done, upto(i, 12, 3 * u + j + 1))
                            pe.wait_ge(state_done, upto(i, 24, 2 * (3 * u + j)))
                            pe.wait_ge(y_norm_done, upto(i, 4, u - 1))
                            pe.transpose(ps_turn[:, 128 * j:128 * j + 128], state_cols[:, :], g.ident[:, :]).then_inc(state_turned, 1)
                        if k == 6 and u is not None:
                            within(i, u, 0)
                        if k == 7 and v is not None:
                            pe.wait_ge(y_cols_done, upto(i, 4, v + 1))
                            if u is not None:
                                pe.wait_ge(state_done, upto(i, 24, 6 * u + 6))
                            pe.wait_ge(y_norm_done, upto(i, 4, v))
                            for j in range(TILES):
                                last = pe.transpose(ps_turn[:, 128 * j:128 * j + 128], y_cols[:, 128 * j:128 * j + 128],
                                                    g.ident[:, :])
                            last.then_inc(y_turned, 1)
                        if k in (1, 2) and b is not None:
                            if k == 1:
                                pe.wait_ge(xn_t_done, upto(i, 2, b + 1))
                            else:
                                pe.wait_ge(qk_full_done, upto(i, 8, 4 * b + 2))
                            pe.matmul(ps_build[:, :], g.weights_t[:, 1 + k, :], xn_t[:, :], start=True, stop=True)\
                                .then_inc(qk_done, 1)
                        w = batch(i, s + 2)
                        if k == 3 and w is not None:
                            pe.wait_ge(qk_full_done, upto(i, 8, 4 * w + 4))
                            pe.wait_ge(biased, upto(i, 2, w - 2))
                            for j in range(TILES):
                                last = pe.matmul(ps_build[:, 128 * j:128 * j + 128], xn_t[:, 128 * j:128 * j + 128],
                                                 g.weights_t[:, 5, :], start=True, stop=True)
                            last.then_inc(v_done, 1)
                        o = batch(i, s - 3)
                        if k == 4 and o is not None:
                            pe.wait_ge(y_norm_done, upto(i, 4, 2 * o + 2))
                            if not (isinstance(i, int) and 2 * i + o + 3 >= NB):
                                pe.wait_ge(qk_full_done, upto(i, 8, 4 * (o + 3) + 4))
                            for j in range(TILES):
                                last = pe.transpose(ps_build[:, 128 * j:128 * j + 128], y_norm[:, j, :], g.ident[:, :])
                            last.then_inc(y_norm_turned, 1)
                        if k == 6 and o is not None:
                            pe.wait_ge(y_t_done, upto(i, 2, o + 1))
                            for j in range(TILES):
                                last = pe.matmul(ps_build[:, 128 * j:128 * j + 128], y_t[:, 128 * j:128 * j + 128],
                                                 g.weights_t[:, 6, :], start=True, stop=True)
                            last.then_inc(projected, 1)

                run(pe, step)


def x_slot(g, i, b):
    if isinstance(i, int):
        return g.x_all[:, 2 * i + b]
    return g.x_all[:, bass.ds(i * 2 + b, 1)].rearrange("p a j c -> p (a j) c")


def emit_ln_stats(dve, g, i, b, stats, mv, stats_done, mv_done):
    tile = x_slot(g, i, b)
    for j in range(TILES):
        last = dve.bn_stats(stats[:, j, :], tile[:, j, :])
    last.then_inc(stats_done, 1)
    dve.wait_ge(stats_done, upto(i, 2, b + 1))
    dve.sem_inc(g.passed_dve, 1)
    for j in range(TILES):
        last = dve.bn_aggr(mv[:, j, :], stats[:, j, :])
    last.then_inc(mv_done, 1)


def emit_ln_apply(dve, g, i, b, xn, mv, rstd, rstd_done, xn_done):
    tile = x_slot(g, i, b)
    dve.wait_ge(rstd_done, upto(i, 2, b + 1))
    for j in range(TILES):
        last = dve.tensor_scalar(xn[:, j, :], tile[:, j, :], mv[:, j, 0:1], rstd[:, j:j + 1],
                                 ALU.subtract, ALU.mult)
    last.then_inc(xn_done, 1)


def emit_store(nc, g, out):
    out_v = out.rearrange("b (j p) c -> p b j c", p=128)
    with nc.semaphore("out_stored") as out_stored, nc.Block() as block:

        @block.sync
        def _(sp):
            for q in range(4):
                sp.dma_start(out_v[:, 4 * q:4 * q + 4], g.x_all[:, 4 * q:4 * q + 4]).then_inc(out_stored, 16)
            sp.wait_ge(out_stored, 64)


def hybrid_kernel(nc, x, a_w, a_b, b_w, b_b, out_w, out_b, proj, router, gate, up, down, s_gate, s_up, s_down, out,
                  layers="afbf"):
    with ExitStack() as ctx:
        g = allocate_common(nc, ctx)
        emit_setup(nc, g, x, a_w, a_b, b_w, b_b, out_w, out_b, proj, router, gate, up, down, s_gate, s_up, s_down)
        for n, layer in enumerate(layers):
            if layer == "a":
                emit_softmax_attention(nc, g)
            elif layer == "f":
                emit_ffn(nc, g, n)
            else:
                emit_linear_attention(nc, g)
        emit_store(nc, g, out)


_INS = ['L0_attn_a_x', 'L0_attn_a_W', 'L0_attn_a_b', 'L0_attn_b_Wqkv', 'L0_attn_b_bqkv', 'L0_attn_b_Wout',
        'L0_attn_b_bout', 'L0_attn_b_proj', 'L0_ffn_router', 'L0_ffn_experts_gate', 'L0_ffn_experts_up',
        'L0_ffn_experts_down', 'L0_ffn_shared_gate', 'L0_ffn_shared_up', 'L0_ffn_shared_down']
_OUT_SHAPE = (NB, T, C)


def kernel(**inputs):
    import concourse.bacc as bacc
    from concourse.bass_utils import run_bass_kernel_spmd

    nc = bacc.Bacc("TRN2", target_bir_lowering=False, num_devices=1)
    arrays, args = {}, []
    for name in _INS:
        a = np.ascontiguousarray(inputs[name])
        arrays[f"in_{name}"] = a
        args.append(nc.dram_tensor(f"in_{name}", a.shape, mybir.dt.from_np(a.dtype), kind="ExternalInput").ap())
    args.append(nc.dram_tensor("out_x", _OUT_SHAPE, F32, kind="ExternalOutput").ap())
    hybrid_kernel(nc, *args)
    r = run_bass_kernel_spmd(nc, [arrays], core_ids=[0])
    return r.results[0]["out_x"]
```

```python
import numpy as np
import concourse.bass as bass
from concourse import mybir
from contextlib import ExitStack

F32 = mybir.dt.float32
BF16 = mybir.dt.bfloat16
ACT = mybir.ActivationFunctionType
ALU = mybir.AluOpType
AX = mybir.AxisListType

NB, T, C = 16, 512, 128
H, D = 16, 8
TILES = T // 128
HL = 8
PARTS = 3
ROWS = PARTS * PARTS * D
KROWS = 96
MROWS = KROWS + PARTS
E, ED = 8, 64
M = 64
EPS = 1e-5
DELTA = 1e-6
SCALE = float(D) ** -0.5
NEG = -1e30
ORDER = [0, 2, 4, 6, 1, 3, 5, 7]


TWO_ONES = float(np.array([0x3F803F80], np.uint32).view(np.float32)[0])


def upto(i, per, const):
    value = i * per + const
    return max(value, 0) if isinstance(i, int) else value


class Common:
    pass


def allocate_common(nc, ctx):
    g = Common()

    def sb(name, shape, dt=F32):
        return ctx.enter_context(nc.sbuf_tensor(name, shape, dt))

    g.passed_sp = ctx.enter_context(nc.semaphore("passed_sp"))
    g.passed_pool = ctx.enter_context(nc.semaphore("passed_pool"))
    g.passed_dve = ctx.enter_context(nc.semaphore("passed_dve"))
    g.x_all = sb("x_all", [128, NB, TILES, C])
    g.ident = sb("ident", [128, 128])
    g.ident_bf = sb("ident_bf", [128, 128], BF16)
    g.mask_neg = sb("mask_neg", [128, 128], BF16)
    g.causal01 = sb("causal01", [128, 128])
    g.pair_mask = sb("pair_mask", [128, 32])
    g.earlier = sb("earlier", [128, E, E])
    g.half_power = sb("half_power", [128, TILES])
    g.weights_t = sb("weights_t", [128, 7, 128])
    g.qk_bias = sb("qk_bias", [128, 4])
    g.row_bias = sb("row_bias", [128, 3, C])
    g.proj = sb("proj", [KROWS, H, 3 * M], BF16)
    g.w_gate = sb("w_gate", [128, 5, 128])
    g.w_up = sb("w_up", [128, 5, 128])
    g.w_down = sb("w_down", [128, 5, 128])
    g.w_router = sb("w_router", [128, E])
    g.select = sb("select", [KROWS, E, ED], BF16)
    g.pj_parts = sb("pj_parts", [D, PARTS, H, M], BF16)
    g.q_stack = [sb(f"q_stack{n}", [MROWS, HL, T], BF16) for n in range(2)]
    g.k_stack = [sb(f"k_stack{n}", [MROWS, HL, T], BF16) for n in range(2)]
    g.x_next = ctx.enter_context(nc.semaphore("x_next"))
    g.x_rest = ctx.enter_context(nc.semaphore("x_rest"))
    g.qk_bias_in = ctx.enter_context(nc.semaphore("qk_bias_in"))
    g.ffn_in = ctx.enter_context(nc.semaphore("ffn_in"))
    g.proj_stacked = ctx.enter_context(nc.semaphore("proj_stacked"))
    g.select_stacked = ctx.enter_context(nc.semaphore("select_stacked"))
    return g


def allocate_softmax_inputs(nc, ctx, g):
    sb = lambda name, shape, dt=F32: ctx.enter_context(nc.sbuf_tensor(name, shape, dt))
    a = Common()
    a.q_stack = g.q_stack + [sb(f"q_stack{n}", [MROWS, HL, T], BF16) for n in (2, 3)]
    a.k_stack = g.k_stack + [sb(f"k_stack{n}", [MROWS, HL, T], BF16) for n in (2, 3)]
    a.v_aug = [sb(f"v_aug{n}", [128, TILES, H, 32]) for n in range(2)]
    return a


def clear_stacks(eng, a, n, cleared):
    eng.memset(a.q_stack[n][64:KROWS, :, :].bitcast(F32), 0.0).then_inc(cleared, 1)
    eng.memset(a.k_stack[n][64:KROWS, :, :].bitcast(F32), 0.0).then_inc(cleared, 1)
    eng.wait_ge(cleared, 2)
    eng.memset(a.k_stack[n][KROWS:MROWS, :, :].bitcast(F32), TWO_ONES).then_inc(cleared, 1)
    eng.wait_ge(cleared, 3)


def load_next(sp, g, src):
    for m, (b, part) in enumerate(((src.a_b, 0), (src.a_b, 1), (src.b_b, 0), (src.b_b, 1))):
        for f in range(2):
            at = 128 * part + 64 * f
            sp.dma_start(g.qk_bias[64 * f:64 * f + 64, m:m + 1], b[at:at + 64].rearrange("(l d c) -> d l c", d=D, c=1),
                         allow_slow_non_contiguous=True).then_inc(g.qk_bias_in, 16)
    sp.dma_start(g.x_all[:, 1:4], src.x_v[:, 1:4]).then_inc(g.x_next, 16)


def load_rest(eng, g, src):
    for q in range(1, 4):
        eng.dma_start(g.x_all[:, 4 * q:4 * q + 4], src.x_v[:, 4 * q:4 * q + 4]).then_inc(g.x_rest, 16)
    for dst, w in ((g.w_gate, src.gate), (g.w_up, src.up)):
        eng.dma_start(dst[:, 0:4, :].rearrange("c n (e d) -> c (n e) d", e=2),
                     w.rearrange("e c d -> c e d")).then_inc(g.ffn_in, 16)
    eng.dma_start(g.w_gate[:, 4, :], src.s_gate).then_inc(g.ffn_in, 16)
    eng.dma_start(g.w_up[:, 4, :], src.s_up).then_inc(g.ffn_in, 16)
    eng.dma_start(g.w_down[:, 0:4, :], src.down.rearrange("(n e) d h -> (e d) n h", e=2)).then_inc(g.ffn_in, 16)
    eng.dma_start(g.w_down[:, 4, :], src.s_down).then_inc(g.ffn_in, 16)
    eng.dma_start(g.w_router[:, :], src.router).then_inc(g.ffn_in, 16)
    for i in range(PARTS):
        for j in range(PARTS):
            row = PARTS * D * i + D * j
            eng.dma_start(g.proj[row:row + D, :, M:2 * M], g.pj_parts[:, j, :, :]).then_inc(g.proj_stacked, 16)
    for n in range(1, PARTS):
        eng.dma_start(g.select[E * n:E * n + E, :, :], g.select[0:E, :, :]).then_inc(g.select_stacked, 16)


def emit_setup(nc, g, a, src):
    with ExitStack() as ctx:
        sb = lambda name, shape, dt=F32: ctx.enter_context(nc.sbuf_tensor(name, shape, dt))
        sem = lambda name: ctx.enter_context(nc.semaphore(name))
        w_rows = sb("w_rows", [128, 7, 128])
        bias_rows = sb("bias_rows", [1, 3, 128])
        ones_row = sb("ones_row", [1, 128])
        pj = sb("pj", [D, H, M])
        pj_left = sb("pj_left", [D, H, M])
        pj_parts = g.pj_parts
        ps_w = [ctx.enter_context(nc.psum_tensor(f"ps_w{n}", [128, 4, 128], F32)) for n in range(3)]
        x_first = sem("x_first")
        weights_in = sem("weights_in")
        proj_in = sem("proj_in")
        filled = sem("filled")
        cleared = sem("cleared")
        select_first = sem("select_first")
        constants = sem("constants")
        idents = sem("idents")
        ones_set = sem("ones_set")
        transposed = sem("transposed")
        biases_up = sem("biases_up")
        proj_step = sem("proj_step")
        proj_zeroed = sem("proj_zeroed")
        cleared0 = sem("cleared0")
        cleared2 = sem("cleared2")
        values_cleared = sem("values_cleared")
        value_ones = sem("value_ones")
        copied = sem("copied")

        x_v, a_w, a_b, b_w, b_b, out_w, out_b = src.x_v, src.a_w, src.a_b, src.b_w, src.b_b, src.out_w, src.out_b
        qk = lambda w, part, f: w[128 * part + 64 * f:128 * part + 64 * f + 64]
        with nc.Block() as block:

            @block.sync
            def _(sp):
                for m, (w, part) in enumerate(((a_w, 0), (a_w, 1), (b_w, 0), (b_w, 1))):
                    for f in range(2):
                        sp.dma_start(w_rows[64 * f:64 * f + 64, m, :],
                                     qk(w, part, f).rearrange("(l d) c -> d l c", d=D)).then_inc(weights_in, 16)
                for m, w in ((4, a_w[256:384, :]), (5, b_w[256:384, :]), (6, out_w)):
                    sp.dma_start(w_rows[:, m, :], w).then_inc(weights_in, 16)
                sp.wait_ge(proj_step, 5)
                sp.wait_ge(proj_zeroed, 1)
                sp.wait_ge(select_first, 1)
                sp.wait_ge(x_first, 16)

            @block.scalar
            def _(act):
                act.dma_start(g.x_all[:, 0:1], x_v[:, 0:1]).then_inc(x_first, 16)
                act.dma_start(pj[:, :, :], src.proj.rearrange("h d m -> d h m")).then_inc(proj_in, 16)
                for m, b in enumerate((a_b[256:384], b_b[256:384], out_b)):
                    act.dma_start(bias_rows[:, m, :], b.rearrange("(a n) -> a n", a=1)).then_inc(weights_in, 16)
                act.wait_ge(transposed, 7)
                act.activation(g.weights_t[:, 0:4, :], ps_w[0][:, :, :], ACT.Copy).then_inc(copied, 1)
                act.activation(g.weights_t[:, 4:7, :], ps_w[1][:, 0:3, :], ACT.Copy).then_inc(copied, 1)

            @block.gpsimd
            def _(pool):
                pool.memset(g.ident[:, :], 0.0).then_inc(filled, 1)
                pool.memset(g.mask_neg[:, :], 0.0).then_inc(filled, 1)
                pool.memset(g.causal01[:, :], 1.0).then_inc(filled, 1)
                pool.wait_ge(filled, 3)
                pool.affine_select(out=g.ident[:, :], in_=g.ident[:, :], compare_op=ALU.not_equal, fill=1.0,
                                   base=0, pattern=[[-1, 128]], channel_multiplier=1).then_inc(idents, 1)
                pool.affine_select(out=g.mask_neg[:, :], in_=g.mask_neg[:, :], compare_op=ALU.is_ge, fill=NEG,
                                   base=0, pattern=[[-1, 128]], channel_multiplier=1).then_inc(constants, 1)
                pool.affine_select(out=g.causal01[:, :], in_=g.causal01[:, :], compare_op=ALU.is_ge, fill=0.0,
                                   base=0, pattern=[[1, 128]], channel_multiplier=-1).then_inc(constants, 1)
                pool.memset(g.half_power[:, :], -0.5).then_inc(constants, 1)
                for n in range(2):
                    pool.memset(a.v_aug[n][:, :, :, :], 0.0).then_inc(values_cleared, 1)
                pool.wait_ge(values_cleared, 2)
                for n in range(2):
                    for r in range(2):
                        pairs = a.v_aug[n][:, :, :, :].rearrange("p j (q r) w -> p (j q) r w", r=2)
                        pool.memset(pairs[:, :, r, 16 * r + D:16 * r + D + 1], 1.0).then_inc(value_ones, 1)
                pool.wait_ge(value_ones, 4)
                clear_stacks(pool, a, 2, cleared2)

            @block.vector
            def _(dve):
                dve.memset(ones_row[:, :], 1.0).then_inc(ones_set, 1)
                dve.memset(g.proj[:, :, :].bitcast(F32), 0.0).then_inc(proj_zeroed, 1)
                dve.memset(g.earlier[:, :, :], 0.0).then_inc(cleared, 1)
                dve.memset(g.pair_mask[:, :], 0.0).then_inc(cleared, 1)
                dve.memset(g.select[:, :, :].bitcast(F32), 0.0).then_inc(cleared, 1)
                dve.wait_ge(cleared, 3)
                for e in range(1, E):
                    dve.memset(g.earlier[:, e, 0:e], 1.0).then_inc(constants, 1)
                for r in range(2):
                    dve.memset(g.pair_mask[M * r:M * r + M, 16 * r:16 * r + 16], 1.0).then_inc(constants, 1)
                dve.wait_ge(idents, 1)
                dve.tensor_copy(g.ident_bf[:, :], g.ident[:, :]).then_inc(constants, 1)
                dve.tensor_copy(g.select[0:E, :, :], g.ident[0:E, 0:E].unsqueeze(2).to_broadcast([E, E, ED]))\
                    .then_inc(select_first, 1)
                clear_stacks(dve, a, 0, cleared0)
                dve.wait_ge(proj_in, 16)
                dve.tensor_copy(pj_parts[:, 0], pj[:, :, :]).then_inc(proj_step, 1)
                dve.wait_ge(proj_step, 1)
                dve.tensor_tensor(pj_left[:, :, :], pj[:, :, :], pj_parts[:, 0], ALU.subtract).then_inc(proj_step, 1)
                dve.wait_ge(proj_step, 2)
                dve.tensor_copy(pj_parts[:, 1], pj_left[:, :, :]).then_inc(proj_step, 1)
                dve.wait_ge(proj_step, 3)
                dve.tensor_tensor(pj[:, :, :], pj_left[:, :, :], pj_parts[:, 1], ALU.subtract).then_inc(proj_step, 1)
                dve.wait_ge(proj_step, 4)
                dve.tensor_copy(pj_parts[:, 2], pj[:, :, :]).then_inc(proj_step, 1)
                dve.wait_ge(biases_up, 1)
                for m in range(3):
                    dve.tensor_copy(g.row_bias[:, m, :], ps_w[2][:, m, :]).then_inc(copied, 1)

            @block.tensor
            def _(pe):
                pe.wait_ge(weights_in, 16 * 14)
                pe.wait_ge(idents, 1)
                for m in range(7):
                    pe.transpose(ps_w[m // 4][:, m % 4, :], w_rows[:, m, :], g.ident[:, :]).then_inc(transposed, 1)
                pe.wait_ge(ones_set, 1)
                for m in range(3):
                    last = pe.matmul(ps_w[2][:, m, :], ones_row[:, :], bias_rows[:, m, :], start=True, stop=True)
                last.then_inc(biases_up, 1)


def emit_softmax_attention(nc, g, a, src):
    AHEAD = 6
    PP = 5
    PU, PB = 4, 8
    NP = NB * PB
    NU = 2 * NB
    STACK_DMAS = 2 * PARTS * PARTS
    with ExitStack() as ctx:
        sb = lambda name, shape, dt=F32: ctx.enter_context(nc.sbuf_tensor(name, shape, dt))
        ps = lambda name, shape, dt=F32: ctx.enter_context(nc.psum_tensor(name, shape, dt))
        sem = lambda name: ctx.enter_context(nc.semaphore(name))
        q_stack, k_stack, v_aug = a.q_stack, a.k_stack, a.v_aug
        probs = sb("probs", [128, 2, 4, 3 * 512])
        parts = sb("parts", [128, 2, PARTS, T], BF16)
        qk_full = sb("qk_full", [128, 2, T])
        xn = sb("xn", [128, TILES, C])
        xn_t = sb("xn_t", [128, T])
        ln_stats = sb("ln_stats", [128, TILES, 6])
        ln_mv = sb("ln_mv", [128, TILES, 2])
        ln_var = sb("ln_var", [128, TILES])
        ln_rstd = sb("ln_rstd", [128, TILES])
        row_max = sb("row_max", [128, 2, TILES, HL])
        max_left = sb("max_left", [128, TILES, HL])
        max_parts = sb("max_parts", [128, TILES, PARTS, HL], BF16)
        max_rows = sb("max_rows", [PARTS * HL, T], BF16)
        y_cols = sb("y_cols", [128, T])
        y_recip = sb("y_recip", [128, TILES * HL])
        y_norm = sb("y_norm", [128, TILES * HL, D])
        ps_max = [ps(f"ps_max{n}", [128, 512]) for n in range(3)]
        ps_exp = [ps(f"ps_exp{n}", [128, 512]) for n in range(2)]
        ps_pv = ps("ps_pv", [128, 512])
        ps_build = ps("ps_build", [128, 512])
        ps_turn = ps("ps_turn", [128, 512])
        turn_bf = ps_turn[:, :].bitcast(BF16)

        cleared = {1: sem("a_cleared1"), 3: sem("a_cleared3")}
        stats_done = sem("a_stats_done")
        mv_done = sem("a_mv_done")
        var_done = sem("a_var_done")
        rstd_done = sem("a_rstd_done")
        xn_done = sem("a_xn_done")
        xn_turned = sem("a_xn_turned")
        xn_t_done = sem("a_xn_t_done")
        qk_done = sem("a_qk_done")
        qk_full_done = sem("a_qk_full_done")
        left1_done = sem("a_left1_done")
        mid_done = sem("a_mid_done")
        low_done = sem("a_low_done")
        v_done = sem("a_v_done")
        v_aug_done = sem("a_v_aug_done")
        stacked = [sem(f"a_stacked{f}") for f in range(2)]
        rows_scored = sem("a_rows_scored")
        rows_reduced = sem("a_rows_reduced")
        max_step = sem("a_max_step")
        max_turned = sem("a_max_turned")
        max_rows_done = sem("a_max_rows_done")
        max_stacked = [sem(f"a_max_stacked{f}") for f in range(2)]
        cols_scored = sem("a_cols_scored")
        exp_done = sem("a_exp_done")
        masked = sem("a_masked")
        pv_done = sem("a_pv_done")
        y_cols_done = sem("a_y_cols_done")
        y_turned = sem("a_y_turned")
        y_recip_done = sem("a_y_recip_done")
        y_norm_done = sem("a_y_norm_done")
        x_added = sem("a_x_added")

        LOOPS = NP // 16 - 2
        TAIL = 8

        def run(eng, step):
            for s in range(-17, TAIL):
                step(0, s)
            with eng.Fori(0, LOOPS) as i:
                for s in range(TAIL, TAIL + 16):
                    step(i, s)
            for s in range(TAIL, NP - 16 * LOOPS + 4):
                step(LOOPS, s)

        def falls(i, s, every, offset, count):
            if (s - offset) % every:
                return None
            n = (s - offset) // every
            if isinstance(i, int) and not 0 <= i * (16 // every) + n < count:
                return None
            return n

        COLS = {0: 0, 1: 512, 3: 896, 2: 1024}

        with nc.Block() as block:

            @block.sync
            def _(sp):
                load_next(sp, g, src)

                def step(i, s):
                    for f in range(2):
                        b = falls(i, s, 8, -11 + 2 * f, NB)
                        if b is None:
                            continue
                        u = 2 * b + f
                        if isinstance(i, int) and 4 * i + u in cleared:
                            sp.wait_ge(cleared[u], 3)
                        sp.wait_ge(low_done, upto(i, 4, 2 * b + 1))
                        sp.sem_inc(g.passed_sp, 1)
                        sp.wait_ge(cols_scored, upto(i, PP * 16, PP * PU * (u - 3)))
                        sp.sem_inc(g.passed_sp, 1)
                        sp.wait_ge(stacked[f], upto(i, 2 * 16 * STACK_DMAS, 16 * STACK_DMAS * b))
                        sp.sem_inc(g.passed_sp, 1)
                        for n in range(PARTS):
                            for c in range(PARTS):
                                row = PARTS * D * n + D * c
                                sp.dma_start(q_stack[u % 4][row:row + D, :, :],
                                             parts[64 * f:64 * f + 64, 0, n, :]).then_inc(stacked[f], 16)
                        sp.wait_ge(low_done, upto(i, 4, 2 * b + 2))
                        sp.sem_inc(g.passed_sp, 1)
                        for n in range(PARTS):
                            for c in range(PARTS):
                                row = PARTS * D * c + D * n
                                sp.dma_start(k_stack[u % 4][row:row + D, :, :],
                                             parts[64 * f:64 * f + 64, 1, n, :]).then_inc(stacked[f], 16)
                        if isinstance(i, int) and i == 0 and (b, f) == (0, 1):
                            load_rest(sp, g, src)

                run(sp, step)
                sp.wait_ge(g.x_rest, 16 * 3)
                sp.wait_ge(g.ffn_in, 16 * 7)
                sp.wait_ge(g.proj_stacked, 16 * PARTS * PARTS)
                sp.wait_ge(g.select_stacked, 16 * (PARTS - 1))

            @block.gpsimd
            def _(pool):
                def step(i, s):
                    b = falls(i, s, 8, -16, NB)
                    if b is not None:
                        pool.wait_ge(mv_done, upto(i, 2, b + 1))
                        pool.sem_inc(g.passed_pool, 1)
                        pool.tensor_scalar(ln_var[:, :], ln_mv[:, :, 1], EPS, 1.0, ALU.add, ALU.mult)\
                            .then_inc(var_done, 1)
                        pool.wait_ge(var_done, upto(i, 2, b + 1))
                        pool.sem_inc(g.passed_pool, 1)
                        pool.wait_ge(xn_done, upto(i, 2, b))
                        pool.sem_inc(g.passed_pool, 1)
                        pool.tensor_tensor(ln_rstd[:, :], ln_var[:, :], g.half_power[:, :], ALU.pow)\
                            .then_inc(rstd_done, 1)
                    for n in range(2):
                        b = falls(i, s, 8, -12 + n, NB)
                        if b is not None:
                            pool.wait_ge(qk_full_done, upto(i, 8, 4 * b + 2 * n + 2))
                            pool.sem_inc(g.passed_pool, 1)
                            pool.tensor_tensor(qk_full[:, n, :], qk_full[:, n, :], parts[:, n, 0, :], ALU.subtract)\
                                .then_inc(left1_done, 1)
                    p = falls(i, s, 1, 0, NP)
                    if p is not None:
                        pool.wait_ge(exp_done, upto(i, PP * 16, PP * (p + 1)))
                        pool.sem_inc(g.passed_pool, 1)
                        two = probs[:, p // 2 % 2, 2 * (p % 2):2 * (p % 2) + 2, :]
                        tri = dict(compare_op=ALU.is_ge, fill=0.0, base=0, channel_multiplier=-1)
                        d012 = two.rearrange("p h (n c) -> p (h n) c", c=512)[:, :, 0:128]
                        pool.affine_select(out=d012, in_=d012, pattern=[[0, 6], [1, 128]], **tri)\
                            .then_inc(masked, 1)
                        d3 = two[:, :, 896:1024]
                        pool.affine_select(out=d3, in_=d3, pattern=[[0, 2], [1, 128]], **tri).then_inc(masked, 1)
                    for n in range(2):
                        b = falls(i, s, 8, -12 + n, NB)
                        if b is not None:
                            pool.wait_ge(mid_done, upto(i, 4, 2 * b + n + 1))
                            pool.sem_inc(g.passed_pool, 1)
                            pool.tensor_tensor(parts[:, n, 2, :], qk_full[:, n, :], parts[:, n, 1, :], ALU.subtract)\
                                .then_inc(low_done, 1)
                    u = falls(i, s, 4, 7, NU)
                    if u is not None:
                        pool.wait_ge(y_norm_done, upto(i, 4, u + 1))
                        pool.sem_inc(g.passed_pool, 1)
                        b = u // 2
                        tile = x_slot(g, i, b)[:, :, 64 * (u % 2):64 * (u % 2) + 64]
                        pool.tensor_tensor(tile, tile, y_norm[:, :, :].rearrange("p (j h) d -> p j (h d)", j=TILES),
                                           ALU.add).then_inc(x_added, 1)
                    if isinstance(i, int) and s == -11:
                        pool.wait_ge(low_done, 2)
                        clear_stacks(pool, a, 3, cleared[3])

                run(pool, step)

            @block.scalar
            def _(act):
                act.wait_ge(g.qk_bias_in, 16 * 8)

                def step(i, s):
                    p = falls(i, s, 1, 0, NP)
                    for n in range(PP):
                        if p is not None:
                            quad = p // 2
                            if n == 0 and p % 2 == 0:
                                act.wait_ge(pv_done, upto(i, 8, quad - 1))
                            row = probs[:, quad % 2]
                            act.wait_ge(cols_scored, upto(i, PP * 16, PP * p + n + 1))
                            slot = 2 * (p % 2) + n // 2
                            bank = ps_exp[(p + n) % 2]
                            if n == PP - 1:
                                dst = row[:, 2 * (p % 2):2 * (p % 2) + 2, 1024:1280]
                                src = bank[:, :].rearrange("p (h t) -> p h t", h=2)
                            else:
                                dst = row[:, slot, 512 * (n % 2):512 * (n % 2) + 512]
                                src = bank[:, :]
                            act.activation(dst, src, ACT.Exp, scale=SCALE).then_inc(exp_done, 1)
                        u = falls(i, s, 4, -1, NU)
                        if n == 0 and u is not None:
                            act.wait_ge(max_rows_done, upto(i, 4, u + 1))
                            act.dma_start(q_stack[u % 4][KROWS:MROWS, :, :], max_rows[:, :])\
                                .then_inc(max_stacked[u % 2], 16)
                        b = falls(i, s, 8, -13, NB)
                        if n == 1 and b is not None:
                            act.wait_ge(xn_turned, upto(i, 2, b + 1))
                            act.wait_ge(v_done, upto(i, 2, b))
                            act.activation(xn_t[:, :], ps_build[:, :], ACT.Copy).then_inc(xn_t_done, 1)
                        for m in range(2):
                            b = falls(i, s, 8, -12 + m, NB)
                            if n == 1 and b is not None:
                                act.wait_ge(qk_done, upto(i, 4, 2 * b + m + 1))
                                act.wait_ge(low_done, upto(i, 4, 2 * b))
                                for f in range(2):
                                    act.wait_ge(stacked[f], upto(i, 2 * 16 * STACK_DMAS, 16 * STACK_DMAS * b))
                                act.activation(parts[:, m, 0, :], ps_build[:, :], ACT.Identity,
                                               bias=g.qk_bias[:, m:m + 1]).then_inc(qk_full_done, 1)
                            if n == 2 and b is not None:
                                act.activation(qk_full[:, m, :], ps_build[:, :], ACT.Identity,
                                               bias=g.qk_bias[:, m:m + 1]).then_inc(qk_full_done, 1)
                    u = falls(i, s, 4, 5, NU)
                    if u is not None:
                        act.wait_ge(pv_done, upto(i, 8, 2 * u + 2))
                        act.wait_ge(y_turned, upto(i, 4, u))
                        act.activation(y_cols[:, :], ps_pv[:, :], ACT.Copy).then_inc(y_cols_done, 1)
                    for n in range(2):
                        b = falls(i, s, 8, -12 + n, NB)
                        if b is not None:
                            act.wait_ge(left1_done, upto(i, 4, 2 * b + n + 1))
                            act.activation(parts[:, n, 1, :], qk_full[:, n, :], ACT.Copy).then_inc(mid_done, 1)
                    u = falls(i, s, 4, -2, NU)
                    if u is not None:
                        act.wait_ge(max_turned, upto(i, 4, u + 1))
                        act.wait_ge(max_stacked[(u - 1) % 2], upto(i, 32, 16 * ((u + 1) // 2)))
                        act.activation(max_rows[:, :], turn_bf[0:PARTS * HL, 0:512], ACT.Copy)\
                            .then_inc(max_rows_done, 1)

                run(act, step)

            @block.vector
            def _(dve):
                def normalise(i, u):
                    dve.wait_ge(y_turned, upto(i, 4, u + 1))
                    heads = ps_turn[:, :].rearrange("p (n w) -> p n w", w=16)
                    dve.wait_ge(y_norm_done, upto(i, 4, u))
                    dve.reciprocal(y_recip[:, :], heads[:, :, D]).then_inc(y_recip_done, 1)
                    dve.wait_ge(y_recip_done, upto(i, 4, u + 1))
                    dve.wait_ge(x_added, upto(i, 4, u))
                    dve.tensor_tensor(y_norm[:, :, :], heads[:, :, 0:D],
                                      y_recip[:, :].unsqueeze(2).to_broadcast([128, TILES * HL, D]),
                                      ALU.mult).then_inc(y_norm_done, 1)

                def reduce_tile(i, p, n):
                    k, u = p % 4, p // 4
                    if k == 0 and n == 0:
                        dve.wait_ge(max_step, upto(i, 16, 4 * (u - 1)))
                    dve.wait_ge(rows_scored, upto(i, PP * 16, PP * p + n + 1))
                    bank = ps_max[n % 3]
                    if n == PP - 1:
                        hl = ORDER[2 * k]
                        dve.tensor_reduce(row_max[:, u % 2, 1, hl:hl + 3:2],
                                          bank[:, :].rearrange("p (h s) -> p h s", h=2), axis=AX.X, op=ALU.max)\
                            .then_inc(rows_reduced, 2)
                        return
                    hl = ORDER[2 * k + n // 2]
                    if n % 2 == 0:
                        dve.tensor_reduce(row_max[:, u % 2, 3, hl:hl + 1], bank[:, :], axis=AX.X, op=ALU.max)\
                            .then_inc(rows_reduced, 2)
                    else:
                        dve.tensor_reduce(row_max[:, u % 2, 2, hl:hl + 1], bank[:, 0:384], axis=AX.X,
                                          op=ALU.max).then_inc(rows_reduced, 1)
                        dve.tensor_reduce(row_max[:, u % 2, 0, hl:hl + 1], bank[:, 384:512], axis=AX.X,
                                          op=ALU.max).then_inc(rows_reduced, 1)

                def cut_maxima(i, u, n):
                    top = row_max[:, u % 2]
                    cut = lambda m: max_parts[:, :, m, :]
                    if n == 0:
                        dve.wait_ge(rows_reduced, upto(i, 2 * PP * 16, 2 * PP * PU * (u + 1)))
                        dve.wait_ge(max_turned, upto(i, 4, u))
                        dve.tensor_scalar(cut(0), top, -1.0, None, ALU.mult).then_inc(max_step, 1)
                    elif n == 1:
                        dve.wait_ge(max_step, upto(i, 16, 4 * u + 1))
                        dve.scalar_tensor_tensor(out=max_left[:, :, :], in0=top, scalar=-1.0, in1=cut(0),
                                                 op0=ALU.mult, op1=ALU.subtract).then_inc(max_step, 1)
                    elif n == 2:
                        dve.wait_ge(max_step, upto(i, 16, 4 * u + 2))
                        dve.tensor_copy(cut(1), max_left[:, :, :]).then_inc(max_step, 1)
                    else:
                        dve.wait_ge(max_step, upto(i, 16, 4 * u + 3))
                        dve.tensor_tensor(cut(2), max_left[:, :, :], cut(1), ALU.subtract).then_inc(max_step, 1)

                def step(i, s):
                    p = falls(i, s, 1, -AHEAD, NP)
                    for n in range(PP):
                        if p is not None:
                            reduce_tile(i, p, n)
                        u = falls(i, s, 4, -2, NU)
                        if u is not None and n < 4:
                            cut_maxima(i, u, n)
                        b = falls(i, s, 8, -17, NB)
                        if n == 0 and isinstance(i, int) and i == 0:
                            if b == 1:
                                dve.wait_ge(g.x_next, 16)
                            if b == 2:
                                dve.wait_ge(g.x_rest, 16 * 3)
                        if b is not None and n < TILES:
                            last = dve.bn_stats(ln_stats[:, n, :], x_slot(g, i, b)[:, n, :])
                            if n == TILES - 1:
                                last.then_inc(stats_done, 1)
                        elif b is not None:
                            dve.wait_ge(stats_done, upto(i, 2, b + 1))
                            dve.sem_inc(g.passed_dve, 1)
                            for j in range(TILES):
                                last = dve.bn_aggr(ln_mv[:, j, :], ln_stats[:, j, :])
                            last.then_inc(mv_done, 1)
                        b = falls(i, s, 8, -15, NB)
                        if b is not None and n > 0:
                            j = n - 1
                            if j == 0:
                                dve.wait_ge(rstd_done, upto(i, 2, b + 1))
                                dve.wait_ge(xn_turned, upto(i, 2, b))
                            last = dve.tensor_scalar(xn[:, j, :], x_slot(g, i, b)[:, j, :], ln_mv[:, j, 0:1],
                                                     ln_rstd[:, j:j + 1], ALU.subtract, ALU.mult)
                            if j == TILES - 1:
                                last.then_inc(xn_done, 1)
                        b = falls(i, s, 8, -6, NB)
                        if b is not None and n == 2:
                            dve.wait_ge(v_done, upto(i, 2, b + 1))
                            dve.wait_ge(pv_done, upto(i, 8, 4 * (b - 1)))
                            src = ps_build[:, :].rearrange("p (j q r d) -> p j q r d", j=TILES, r=2, d=D)
                            bias = g.row_bias[:, 0, :].rearrange("p (q r d) -> p q r d", r=2, d=D)
                            pairs = v_aug[b % 2][:, :, :, :].rearrange("p j (q r) w -> p j q r w", r=2)
                            for r in range(2):
                                dve.tensor_tensor(pairs[:, :, :, r, 16 * r:16 * r + D], src[:, :, :, r, :],
                                                  bias[:, :, r, :].unsqueeze(1).to_broadcast([128, TILES, H // 2, D]),
                                                  ALU.add).then_inc(v_aug_done, 1)
                        u = falls(i, s, 4, 7, NU)
                        if u is not None and n == 4:
                            normalise(i, u)
                    if isinstance(i, int) and s == -15:
                        clear_stacks(dve, a, 1, cleared[1])

                run(dve, step)

            @block.tensor
            def _(pe):
                def rows(qs, ks, bank, col, hl, j):
                    pe.matmul(bank[:, col:col + 128 * (j + 1)], qs[0:KROWS, hl, 128 * j:128 * j + 128],
                              ks[0:KROWS, hl, 0:128 * (j + 1)], start=True, stop=False)
                    return pe.matmul(bank[:, col + 128 * j:col + 128 * (j + 1)], g.ident_bf[:, :],
                                     g.mask_neg[:, :], start=False, stop=True)

                def rows_tile(i, p, n):
                    k, u = p % 4, p // 4
                    qs, ks = q_stack[u % 4], k_stack[u % 4]
                    if k == 0 and n == 0:
                        pe.wait_ge(stacked[u % 2], upto(i, 2 * 16 * STACK_DMAS, 16 * STACK_DMAS * (u // 2 + 1)))
                    bank = ps_max[n % 3]
                    pe.wait_ge(rows_reduced, upto(i, 2 * PP * 16, 2 * (PP * p + (-1, 0, -2, 1, 2)[n])))
                    if n == PP - 1:
                        rows(qs, ks, bank, 0, ORDER[2 * k], 1)
                        last = rows(qs, ks, bank, 256, ORDER[2 * k + 1], 1)
                    elif n % 2 == 0:
                        last = rows(qs, ks, bank, 0, ORDER[2 * k + n // 2], 3)
                    else:
                        rows(qs, ks, bank, 0, ORDER[2 * k + n // 2], 2)
                        last = rows(qs, ks, bank, 384, ORDER[2 * k + n // 2], 0)
                    last.then_inc(rows_scored, 1)

                def cols(qs, ks, bank, col, hl, j):
                    return pe.matmul(bank[:, col:col + T - 128 * j], ks[0:MROWS, hl, 128 * j:128 * j + 128],
                                     qs[0:MROWS, hl, 128 * j:T], start=True, stop=True)

                def cols_tile(i, p, n):
                    k, u = p % 4, p // 4
                    qs, ks = q_stack[u % 4], k_stack[u % 4]
                    if k == 0 and n == 0:
                        pe.wait_ge(max_stacked[u % 2], upto(i, 32, 16 * (u // 2 + 1)))
                    pe.wait_ge(exp_done, upto(i, PP * 16, PP * p + n - 1))
                    bank = ps_exp[(p + n) % 2]
                    if n == PP - 1:
                        cols(qs, ks, bank, 0, ORDER[2 * k], 2)
                        last = cols(qs, ks, bank, 256, ORDER[2 * k + 1], 2)
                    elif n % 2 == 0:
                        last = cols(qs, ks, bank, 0, ORDER[2 * k + n // 2], 0)
                    else:
                        cols(qs, ks, bank, 0, ORDER[2 * k + n // 2], 1)
                        last = cols(qs, ks, bank, 384, ORDER[2 * k + n // 2], 3)
                    last.then_inc(cols_scored, 1)

                VALUES_AT = {(0, 2): 0, (0, 4): 3, (1, 2): 1, (1, 4): 2}
                LAST_TILE = 2

                def times_values(i, quad, j):
                    b, r, f = quad // 4, quad % 2, quad // 2 % 2
                    if j == 0:
                        pe.wait_ge(masked, upto(i, 32, 4 * quad + 4))
                        pe.wait_ge(v_aug_done, upto(i, 4, 2 * b + 2))
                        if r == 0:
                            pe.wait_ge(y_cols_done, upto(i, 4, quad // 2))
                    for c in range(4):
                        last = pe.matmul(ps_pv[32 * c:32 * c + 32, 128 * j:T],
                                         v_aug[b % 2][:, j, HL * f + 2 * c + r, :],
                                         probs[:, quad % 2, c, COLS[j]:COLS[j] + T - 128 * j],
                                         start=(r == 0 and j == 0), stop=(r == 1 and j == LAST_TILE),
                                         skip_group_check=True)
                    if j == LAST_TILE:
                        last.then_inc(pv_done, 1)

                def step(i, s):
                    later, now = falls(i, s, 1, -AHEAD, NP), falls(i, s, 1, 0, NP)
                    for n in range(PP):
                        if later is not None:
                            rows_tile(i, later, n)
                        if now is not None:
                            cols_tile(i, now, n)
                        b = falls(i, s, 8, -6, NB)
                        if n == 0 and b is not None:
                            pe.wait_ge(qk_full_done, upto(i, 8, 4 * b + 4))
                            for j in range(TILES):
                                last = pe.matmul(ps_build[:, 128 * j:128 * j + 128], xn_t[:, 128 * j:128 * j + 128],
                                                 g.weights_t[:, 4, :], start=True, stop=True)
                            last.then_inc(v_done, 1)
                        b = falls(i, s, 8, -13, NB)
                        if n == 1 and b is not None:
                            pe.wait_ge(xn_done, upto(i, 2, b + 1))
                            pe.wait_ge(v_aug_done, upto(i, 4, 2 * b))
                            for j in range(TILES):
                                last = pe.transpose(ps_build[:, 128 * j:128 * j + 128], xn[:, j, :], g.ident[:, :])
                            last.then_inc(xn_turned, 1)
                        u = falls(i, s, 4, 7, NU)
                        if n == 3 and u is not None:
                            pe.wait_ge(y_cols_done, upto(i, 4, u + 1))
                            turned = upto(i, 4, u + 3)
                            pe.wait_ge(max_rows_done, min(turned, NU) if isinstance(i, int) else turned)
                            pe.wait_ge(y_norm_done, upto(i, 4, u))
                            for j in range(TILES):
                                last = pe.transpose(ps_turn[:, 128 * j:128 * j + 128], y_cols[:, 128 * j:128 * j + 128],
                                                    g.ident[:, :])
                            last.then_inc(y_turned, 1)
                        quad = falls(i, s - (s % 2), 2, 2, NP // 2)
                        if quad is not None and (s % 2, n) in VALUES_AT:
                            times_values(i, quad, VALUES_AT[s % 2, n])
                    u = falls(i, s, 4, -2, NU)
                    if u is not None:
                        pe.wait_ge(max_step, upto(i, 16, 4 * u + 4))
                        pe.wait_ge(y_norm_done, upto(i, 4, u - 2))
                        for j in range(TILES):
                            last = pe.transpose(turn_bf[0:PARTS * HL, 128 * j:128 * j + 128],
                                                max_parts[:, j].rearrange("p n h -> p (n h)"), g.ident_bf[:, :])
                        last.then_inc(max_turned, 1)
                    for n in range(2):
                        b = falls(i, s, 8, -13 + n, NB)
                        if b is not None:
                            if n == 0:
                                pe.wait_ge(xn_t_done, upto(i, 2, b + 1))
                            else:
                                pe.wait_ge(qk_full_done, upto(i, 8, 4 * b + 2))
                            pe.matmul(ps_build[:, :], g.weights_t[:, n, :], xn_t[:, :], start=True, stop=True)\
                                .then_inc(qk_done, 1)

                run(pe, step)


def allocate_linear_values(nc, ctx):
    return [ctx.enter_context(nc.sbuf_tensor(f"l_v_aug{n}", [128, TILES, H // 2, 64], F32)) for n in range(2)]


def emit_ffn(nc, g, tag, values=None, out=None):
    CH = 5
    PR = 4
    with ExitStack() as ctx:
        sb = lambda name, shape, dt=F32: ctx.enter_context(nc.sbuf_tensor(f"f{tag}_{name}", shape, dt))
        ps = lambda name, shape, dt=F32: ctx.enter_context(nc.psum_tensor(f"f{tag}_{name}", shape, dt))
        sem = lambda name: ctx.enter_context(nc.semaphore(f"f{tag}_{name}"))
        xn = sb("xn", [128, TILES, C])
        xn_t = sb("xn_t", [128, 2, T])
        ln_stats = sb("ln_stats", [128, TILES, 6])
        ln_mv = sb("ln_mv", [128, TILES, 2])
        ln_var = sb("ln_var", [128, TILES])
        ln_rstd = sb("ln_rstd", [128, TILES])
        silu = sb("silu", [128, 2, T])
        gated = sb("gated", [128, 2, T])
        hidden = sb("hidden", [128, CH, T])
        top = sb("top", [128, TILES])
        shifted = sb("shifted", [128, TILES, E])
        exps = sb("exps", [128, TILES, E])
        total = sb("total", [128, TILES])
        inv_total = sb("inv_total", [128, TILES])
        prob = sb("prob", [128, TILES, E])
        above = sb("above", [128, TILES, E, E])
        equal = sb("equal", [128, TILES, E, E])
        ties = sb("ties", [128, TILES, E, E])
        rank = sb("rank", [128, TILES, E])
        coef = sb("coef", [128, TILES, E])
        coef_left = sb("coef_left", [128, TILES, E])
        coef_parts = sb("coef_parts", [128, TILES, PARTS, E], BF16)
        coef_rows = sb("coef_rows", [KROWS, T], BF16)
        ps_gate = [ps(f"ps_gate{n}", [128, T]) for n in range(2)]
        ps_up = [ps(f"ps_up{n}", [128, T]) for n in range(2)]
        ps_coef = [ps(f"ps_coef{n}", [128, T]) for n in range(2)]
        ps_out = ps("ps_out", [128, T])
        ps_small = ps("ps_small", [128, T])
        small_bf = ps_small[:, :].bitcast(BF16)

        zeroed = sem("zeroed")
        values_cleared = sem("values_cleared")
        value_ones = sem("value_ones")
        out_stored = sem("out_stored")
        stats_done = sem("stats_done")
        mv_done = sem("mv_done")
        var_done = sem("var_done")
        rstd_done = sem("rstd_done")
        xn_done = sem("xn_done")
        xn_turned = sem("xn_turned")
        xn_t_done = sem("xn_t_done")
        gate_done = sem("gate_done")
        up_done = sem("up_done")
        silu_done = sem("silu_done")
        gated_done = sem("gated_done")
        weighted = sem("weighted")
        spread = sem("spread")
        down_done = sem("down_done")
        x_added = sem("x_added")
        logits_done = sem("logits_done")
        top_done = sem("top_done")
        shifted_done = sem("shifted_done")
        exps_done = sem("exps_done")
        route = sem("route")
        ROUTE = 13
        coef_turned = sem("coef_turned")
        coef_rows_done = sem("coef_rows_done")

        LOOPS = NB // 2 - 2

        def run(eng, batch):
            for e in range(-2, 2):
                batch(0, e)
            with eng.Fori(0, LOOPS) as i:
                for e in range(2, 4):
                    batch(i, e)
            for e in range(2, NB - 2 * LOOPS + 1):
                batch(LOOPS, e)

        def live(i, e):
            return not isinstance(i, int) or 0 <= 2 * i + e < NB

        with nc.Block() as block:

            @block.sync
            def _(sp):
                if out is not None:
                    out_v = out.rearrange("b (j p) c -> p b j c", p=128)
                    ends = (0, 4, 8, 12, 14, 15, 16)
                    for first, end in zip(ends, ends[1:]):
                        sp.wait_ge(x_added, end)
                        sp.dma_start(out_v[:, first:end], g.x_all[:, first:end]).then_inc(out_stored, 16)
                    sp.wait_ge(out_stored, 16 * (len(ends) - 1))

            @block.gpsimd
            def _(pool):
                def batch(i, e):
                    if live(i, e + 2):
                        pool.wait_ge(mv_done, upto(i, 2, e + 3))
                        pool.sem_inc(g.passed_pool, 1)
                        pool.tensor_scalar(ln_var[:, :], ln_mv[:, :, 1], EPS, 1.0, ALU.add, ALU.mult)\
                            .then_inc(var_done, 1)
                        pool.wait_ge(var_done, upto(i, 2, e + 3))
                        pool.sem_inc(g.passed_pool, 1)
                        pool.wait_ge(xn_done, upto(i, 2, e + 2))
                        pool.sem_inc(g.passed_pool, 1)
                        pool.tensor_tensor(ln_rstd[:, :], ln_var[:, :], g.half_power[:, :], ALU.pow)\
                            .then_inc(rstd_done, 1)

                run(pool, batch)
                if values is not None:
                    for n in range(2):
                        pool.memset(values[n][:, :, :, :], 0.0).then_inc(values_cleared, 1)
                    pool.wait_ge(values_cleared, 2)
                    for n in range(2):
                        for r in range(2):
                            at = 32 - 16 * r
                            pool.memset(values[n][:, :, :, at + D:at + D + 1], 1.0).then_inc(value_ones, 1)

            @block.scalar
            def _(act):
                def batch(i, e):
                    for n in range(CH):
                        if n == 1 and live(i, e + 1):
                            act.wait_ge(xn_turned, upto(i, 2, e + 2))
                            act.wait_ge(up_done, upto(i, 2 * CH, CH * e))
                            act.activation(xn_t[:, (e + 1) % 2, :], ps_small[:, :], ACT.Copy).then_inc(xn_t_done, 1)
                        if live(i, e):
                            act.wait_ge(gate_done, upto(i, 2 * CH, CH * e + n + 1))
                            act.wait_ge(gated_done, upto(i, 2 * CH, CH * e + n - 1))
                            act.activation(silu[:, (e + n) % 2, :], ps_gate[(e + n) % 2][:, :], ACT.Silu)\
                                .then_inc(silu_done, 1)
                        if n == 2 and live(i, e + 1):
                            act.wait_ge(shifted_done, upto(i, 2, e + 2))
                            act.activation(exps[:, :, :], shifted[:, :, :], ACT.Exp).then_inc(exps_done, 1)
                        if n == 0 and live(i, e):
                            act.wait_ge(coef_turned, upto(i, 2, e + 1))
                            act.wait_ge(spread, upto(i, 2 * PR, PR * e))
                            act.activation(coef_rows[0:PARTS * E, :], small_bf[0:PARTS * E, 0:T], ACT.Copy)\
                                .then_inc(coef_rows_done, 1)

                run(act, batch)

            @block.vector
            def _(dve):
                dve.memset(coef_rows[:, :].bitcast(F32), 0.0).then_inc(zeroed, 1)

                def route_step(i, e, k):
                    each = prob[:, :, :].unsqueeze(3).to_broadcast([128, TILES, E, E])
                    other = prob[:, :, :].unsqueeze(2).to_broadcast([128, TILES, E, E])
                    cut = lambda k: coef_parts[:, :, k, :]
                    if k == 0:
                        dve.wait_ge(exps_done, upto(i, 2, e + 1))
                        ins = dve.tensor_reduce(total[:, :], exps[:, :, :], axis=AX.X, op=ALU.add)
                    else:
                        dve.wait_ge(route, upto(i, 2 * ROUTE, ROUTE * e + k))
                    if k == 1:
                        ins = dve.reciprocal(inv_total[:, :], total[:, :])
                    if k == 2:
                        ins = dve.tensor_tensor(prob[:, :, :], exps[:, :, :],
                                                inv_total[:, :].unsqueeze(2).to_broadcast([128, TILES, E]), ALU.mult)
                    if k == 3:
                        ins = dve.tensor_tensor(equal[:, :, :, :], other, each, ALU.is_equal)
                    if k == 4:
                        ins = dve.tensor_tensor(ties[:, :, :, :].rearrange("p j e f -> p j (e f)"),
                                                equal[:, :, :, :].rearrange("p j e f -> p j (e f)"),
                                                g.earlier[:, :, :].rearrange("p e f -> p (e f)").unsqueeze(1)
                                                .to_broadcast([128, TILES, E * E]), ALU.mult)
                    if k == 5:
                        ins = dve.tensor_tensor(above[:, :, :, :], other, each, ALU.is_gt)
                    if k == 6:
                        ins = dve.tensor_tensor(above[:, :, :, :], above[:, :, :, :], ties[:, :, :, :], ALU.add)
                    if k == 7:
                        ins = dve.tensor_reduce(rank[:, :, :], above[:, :, :, :], axis=AX.X, op=ALU.add)
                    if k == 8:
                        ins = dve.scalar_tensor_tensor(out=coef[:, :, :], in0=rank[:, :, :], scalar=1.5,
                                                       in1=prob[:, :, :], op0=ALU.is_lt, op1=ALU.mult)
                    if k == 9:
                        dve.wait_ge(coef_turned, upto(i, 2, e))
                        ins = dve.tensor_copy(cut(0), coef[:, :, :])
                    if k == 10:
                        ins = dve.tensor_tensor(coef_left[:, :, :], coef[:, :, :], cut(0), ALU.subtract)
                    if k == 11:
                        ins = dve.tensor_copy(cut(1), coef_left[:, :, :])
                    if k == 12:
                        ins = dve.tensor_tensor(cut(2), coef_left[:, :, :], cut(1), ALU.subtract)
                    ins.then_inc(route, 1)

                ROUTE_BEFORE = {3: (3,)}
                ROUTE_AFTER = {2: (0, 1, 2), 3: (4, 5, 6), 4: (7, 8, 9, 10, 11, 12)}

                def batch(i, e):
                    for n in range(CH):
                        if n == 2 and live(i, e - 1):
                            dve.wait_ge(down_done, upto(i, 2 * CH, CH * e))
                            tile = x_slot(g, i, e - 1)
                            dve.tensor_tensor(tile, tile, ps_out[:, :].rearrange("p (j c) -> p j c", j=TILES), ALU.add)\
                                .then_inc(x_added, 1)
                        if n == 2 and live(i, e + 1):
                            dve.wait_ge(logits_done, upto(i, 2, e + 2))
                            logits = ps_small[:, 0:TILES * E].rearrange("p (j e) -> p j e", e=E)
                            dve.tensor_reduce(top[:, :], logits, axis=AX.X, op=ALU.max).then_inc(top_done, 1)
                            dve.wait_ge(top_done, upto(i, 2, e + 2))
                            dve.wait_ge(exps_done, upto(i, 2, e + 1))
                            dve.tensor_tensor(shifted[:, :, :], logits,
                                              top[:, :].unsqueeze(2).to_broadcast([128, TILES, E]),
                                              ALU.subtract).then_inc(shifted_done, 1)
                        last = n == CH - 1
                        par = (e + n) % 2
                        if live(i, e):
                            dve.wait_ge(silu_done, upto(i, 2 * CH, CH * e + n + 1))
                            dve.wait_ge(up_done, upto(i, 2 * CH, CH * e + n + 1))
                            dst = hidden[:, n, :] if last else gated[:, par, :]
                            if last:
                                dve.wait_ge(down_done, upto(i, 2 * CH, CH * e))
                            else:
                                dve.wait_ge(weighted, upto(i, 2 * PR, PR * e + n - 1))
                            dve.tensor_tensor(dst, ps_up[par][:, :], silu[:, par, :], ALU.mult).then_inc(gated_done, 1)
                        if live(i, e + 1):
                            for k in ROUTE_BEFORE.get(n, ()):
                                route_step(i, e + 1, k)
                        if live(i, e) and not last:
                            dve.wait_ge(gated_done, upto(i, 2 * CH, CH * e + n + 1))
                            dve.wait_ge(spread, upto(i, 2 * PR, PR * e + n + 1))
                            dve.wait_ge(down_done, upto(i, 2 * CH, CH * (e - 1) + n + 1))
                            dve.tensor_tensor(hidden[:, n, :], ps_coef[n % 2][:, :], gated[:, par, :], ALU.mult)\
                                .then_inc(weighted, 1)
                        if live(i, e + 1):
                            for k in ROUTE_AFTER.get(n, ()):
                                route_step(i, e + 1, k)
                        if n == 0 and live(i, e + 2):
                            emit_ln_stats(dve, g, i, e + 2, ln_stats, ln_mv, stats_done, mv_done)
                        if n == 1 and live(i, e + 2):
                            dve.wait_ge(xn_turned, upto(i, 2, e + 2))
                            emit_ln_apply(dve, g, i, e + 2, xn, ln_mv, ln_rstd, rstd_done, xn_done)

                run(dve, batch)

            @block.tensor
            def _(pe):
                pe.wait_ge(zeroed, 1)

                def down(i, e, n):
                    if n == CH - 1:
                        pe.wait_ge(gated_done, upto(i, 2 * CH, CH * e + CH))
                    else:
                        pe.wait_ge(weighted, upto(i, 2 * PR, PR * e + n + 1))
                    if n == 0:
                        pe.wait_ge(x_added, upto(i, 2, e))
                    for j in range(TILES):
                        last = pe.matmul(ps_out[:, 128 * j:128 * j + 128], hidden[:, n, 128 * j:128 * j + 128],
                                         g.w_down[:, n, :], start=(n == 0 and j == 0), stop=(n == CH - 1),
                                         skip_group_check=True)
                    last.then_inc(down_done, 1)

                def batch(i, e):
                    for n in range(CH):
                        if live(i, e):
                            par = (e + n) % 2
                            xt = xn_t[:, e % 2, :]
                            if n == 0:
                                pe.wait_ge(xn_t_done, upto(i, 2, e + 1))
                            pe.wait_ge(silu_done, upto(i, 2 * CH, CH * e + n - 1))
                            pe.matmul(ps_gate[par][:, :], g.w_gate[:, n, :], xt, start=True, stop=True)\
                                .then_inc(gate_done, 1)
                            pe.wait_ge(gated_done, upto(i, 2 * CH, CH * e + n - 1))
                            pe.matmul(ps_up[par][:, :], g.w_up[:, n, :], xt, start=True, stop=True)\
                                .then_inc(up_done, 1)
                            if 0 < n < PR:
                                pe.wait_ge(weighted, upto(i, 2 * PR, PR * e + n - 1))
                                pe.matmul(ps_coef[n % 2][:, :],
                                          g.select[:, 2 * n:2 * n + 2, :].rearrange("p e d -> p (e d)"),
                                          coef_rows[:, :], start=True, stop=True).then_inc(spread, 1)
                        if n == 0 and live(i, e):
                            pe.wait_ge(route, upto(i, 2 * ROUTE, ROUTE * (e + 1)))
                            for j in range(TILES):
                                last = pe.transpose(small_bf[0:PARTS * E, 128 * j:128 * j + 128],
                                                    coef_parts[:, j].rearrange("p n e -> p (n e)"), g.ident_bf[:, :])
                            last.then_inc(coef_turned, 1)
                        if n < 2 and live(i, e - 1):
                            down(i, e - 1, n + 3)
                        if n == 0 and live(i, e):
                            pe.wait_ge(coef_rows_done, upto(i, 2, e + 1))
                            pe.wait_ge(weighted, upto(i, 2 * PR, PR * e - 1))
                            pe.matmul(ps_coef[0][:, :], g.select[:, 0:2, :].rearrange("p e d -> p (e d)"),
                                      coef_rows[:, :], start=True, stop=True).then_inc(spread, 1)
                        if n >= 2 and live(i, e):
                            down(i, e, n - 2)
                        if n == 0 and live(i, e + 1):
                            pe.wait_ge(xn_done, upto(i, 2, e + 2))
                            pe.wait_ge(coef_rows_done, upto(i, 2, e + 1))
                            for j in range(TILES):
                                last = pe.transpose(ps_small[:, 128 * j:128 * j + 128], xn[:, j, :], g.ident[:, :])
                            last.then_inc(xn_turned, 1)
                        if n == 1 and live(i, e + 1):
                            pe.wait_ge(xn_t_done, upto(i, 2, e + 2))
                            for j in range(TILES):
                                last = pe.matmul(ps_small[:, E * j:E * j + E],
                                                 xn_t[:, (e + 1) % 2, 128 * j:128 * j + 128], g.w_router[:, :],
                                                 start=True, stop=True)
                            last.then_inc(logits_done, 1)

                run(pe, batch)


def emit_linear_attention(nc, g, v_aug):
    PU = 4
    NU = 2 * NB
    KEY_TOK, KEY_FEAT, QUERY = range(3)
    OTHERS = [(KEY_TOK, j) for j in range(TILES - 1)] + [(QUERY, c) for c in range(PU)]
    TILE_OF = [t for k in range(HL) for t in OTHERS[k:k + 1] + [(KEY_FEAT, k)]]
    FEATS = len(TILE_OF)
    STACK_DMAS = PARTS * PARTS
    with ExitStack() as ctx:
        sb = lambda name, shape, dt=F32: ctx.enter_context(nc.sbuf_tensor(f"l_{name}", shape, dt))
        ps = lambda name, shape, dt=F32: ctx.enter_context(nc.psum_tensor(f"l_{name}", shape, dt))
        sem = lambda name: ctx.enter_context(nc.semaphore(f"l_{name}"))
        q_stack, k_stack = g.q_stack, g.k_stack
        key_tok = sb("key_tok", [128, 2, TILES - 1, HL * M])
        key_feat = sb("key_feat", [128, HL, T])
        query_feat = sb("query_feat", [128, 2, PU, T])
        attn = sb("attn", [128, HL, TILES, 128])
        parts = [sb(f"parts{n}", [128, 2, PARTS, T], BF16) for n in range(2)]
        qk_full = sb("qk_full", [128, 2, T])
        xn = sb("xn", [128, TILES, C])
        xn_t = sb("xn_t", [128, T])
        ln_stats = sb("ln_stats", [128, TILES, 6])
        ln_mv = sb("ln_mv", [128, TILES, 2])
        ln_var = sb("ln_var", [128, TILES])
        ln_rstd = sb("ln_rstd", [128, TILES])
        state_cols = sb("state_cols", [128, 128])
        state = sb("state", [128, TILES - 1, PU * 32])
        y_cols = sb("y_cols", [128, T])
        y_sum = sb("y_sum", [128, TILES * HL])
        y_recip = sb("y_recip", [128, TILES * HL])
        y_norm = sb("y_norm", [128, TILES, C])
        y_t = sb("y_t", [128, T])
        y_out = sb("y_out", [128, TILES, C])
        ps_feat = [ps(f"ps_feat{n}", [128, T]) for n in range(2)]
        ps_attn = [ps(f"ps_attn{n}", [128, T]) for n in range(2)]
        ps_pv = ps("ps_pv", [128, T])
        ps_state = ps("ps_state", [128, T])
        ps_turn = ps("ps_turn", [128, T])
        ps_build = ps("ps_build", [128, T])

        stats_done = sem("stats_done")
        mv_done = sem("mv_done")
        var_done = sem("var_done")
        rstd_done = sem("rstd_done")
        xn_done = sem("xn_done")
        xn_turned = sem("xn_turned")
        xn_t_done = sem("xn_t_done")
        qk_done = sem("qk_done")
        qk_full_done = sem("qk_full_done")
        top_done = sem("top_done")
        left1_done = sem("left1_done")
        mid_done = sem("mid_done")
        low_done = sem("low_done")
        v_done = sem("v_done")
        v_aug_done = sem("v_aug_done")
        k_stacked = [sem(f"k_stacked{f}") for f in range(2)]
        q_stacked = [sem(f"q_stacked{f}") for f in range(2)]
        feat_done = sem("feat_done")
        feat_out = sem("feat_out")
        scored = sem("scored")
        attn_done = sem("attn_done")
        within_done = sem("within_done")
        hist_done = sem("hist_done")
        summed = sem("summed")
        state_cols_done = sem("state_cols_done")
        state_turned = sem("state_turned")
        state_done = sem("state_done")
        y_cols_done = sem("y_cols_done")
        y_turned = sem("y_turned")
        y_sum_done = sem("y_sum_done")
        y_recip_done = sem("y_recip_done")
        y_norm_done = sem("y_norm_done")
        y_norm_turned = sem("y_norm_turned")
        y_t_done = sem("y_t_done")
        projected = sem("projected")
        biased = sem("biased")
        x_added = sem("x_added")

        FIRST, BODY, LOOPS = -4, 8, 5

        def run(eng, step):
            for s in range(FIRST, BODY):
                step(0, s)
            with eng.Fori(0, LOOPS) as i:
                for s in range(BODY, BODY + 4):
                    step(i, s)
            for s in range(BODY, NU - 4 * LOOPS + 2):
                step(LOOPS, s)

        def unit(i, s):
            return s if not isinstance(i, int) or 0 <= 4 * i + s < NU else None

        def batch(i, s2):
            return s2 // 2 if s2 % 2 == 0 and (not isinstance(i, int) or 0 <= 2 * i + s2 // 2 < NB) else None

        with nc.Block() as block:

            @block.sync
            def _(sp):
                def step(i, s):
                    b = batch(i, s + 3)
                    if b is not None:
                        sp.wait_ge(low_done, upto(i, 4, 2 * b + 2))
                        sp.sem_inc(g.passed_sp, 1)
                        for f in range(2):
                            u = 2 * b + f
                            sp.wait_ge(feat_done, upto(i, 4 * FEATS, FEATS * (u - 1)))
                            sp.sem_inc(g.passed_sp, 1)
                            sp.wait_ge(k_stacked[f], upto(i, 2 * 16 * STACK_DMAS, 16 * STACK_DMAS * b))
                            sp.sem_inc(g.passed_sp, 1)
                            sp.wait_ge(q_stacked[f], upto(i, 2 * 16 * STACK_DMAS, 16 * STACK_DMAS * b))
                            sp.sem_inc(g.passed_sp, 1)
                            for n in range(PARTS):
                                for c in range(PARTS):
                                    row = PARTS * D * n + D * c
                                    sp.dma_start(k_stack[u % 2][row:row + D, :, :],
                                                 parts[b % 2][64 * f:64 * f + 64, 1, n, :]).then_inc(k_stacked[f], 16)
                            for n in range(PARTS):
                                for c in range(PARTS):
                                    row = PARTS * D * n + D * c
                                    sp.dma_start(q_stack[u % 2][row:row + D, :, :],
                                                 parts[b % 2][64 * f:64 * f + 64, 0, n, :]).then_inc(q_stacked[f], 16)

                run(sp, step)

            @block.gpsimd
            def _(pool):
                def step(i, s):
                    for k in range(8):
                        b = batch(i, s + 4)
                        if k == 1 and b is not None:
                            pool.wait_ge(mv_done, upto(i, 2, b + 1))
                            pool.sem_inc(g.passed_pool, 1)
                            pool.tensor_scalar(ln_var[:, :], ln_mv[:, :, 1], EPS, 1.0, ALU.add, ALU.mult)\
                                .then_inc(var_done, 1)
                            pool.wait_ge(var_done, upto(i, 2, b + 1))
                            pool.sem_inc(g.passed_pool, 1)
                            pool.wait_ge(xn_done, upto(i, 2, b))
                            pool.sem_inc(g.passed_pool, 1)
                            pool.tensor_tensor(ln_rstd[:, :], ln_var[:, :], g.half_power[:, :], ALU.pow)\
                                .then_inc(rstd_done, 1)
                        b = batch(i, s + 3)
                        if k in (2, 3) and b is not None:
                            n = k - 2
                            pool.wait_ge(top_done, upto(i, 4, 2 * b + n + 1))
                            pool.sem_inc(g.passed_pool, 1)
                            pool.tensor_tensor(qk_full[:, n, :], qk_full[:, n, :], parts[b % 2][:, n, 0, :],
                                               ALU.subtract)\
                                .then_inc(left1_done, 1)
                            pool.wait_ge(mid_done, upto(i, 4, 2 * b + n + 1))
                            pool.sem_inc(g.passed_pool, 1)
                            pool.tensor_tensor(parts[b % 2][:, n, 2, :], qk_full[:, n, :], parts[b % 2][:, n, 1, :],
                                               ALU.subtract)\
                                .then_inc(low_done, 1)
                        b = batch(i, s - 3)
                        if k == 6 and b is not None:
                            pool.wait_ge(biased, upto(i, 2, b + 1))
                            pool.sem_inc(g.passed_pool, 1)
                            tile = x_slot(g, i, b)
                            pool.tensor_tensor(tile, tile, y_out[:, :, :], ALU.add).then_inc(x_added, 1)

                run(pool, step)

            @block.scalar
            def _(act):
                def step(i, s):
                    for k in range(8):
                        u = unit(i, s)
                        if k in (3, 4, 5) and u is not None:
                            j = k - 3
                            act.wait_ge(summed, upto(i, 12, 3 * u + j + 1))
                            act.wait_ge(state_turned, upto(i, 12, 3 * u + j))
                            act.activation(state_cols[:, :], ps_state[:, 0:128], ACT.Copy).then_inc(state_cols_done, 1)
                        b = batch(i, s + 3)
                        if k in (2, 3) and b is not None:
                            n = k - 2
                            act.wait_ge(qk_done, upto(i, 4, 2 * b + n + 1))
                            act.wait_ge(low_done, upto(i, 4, 2 * b))
                            act.activation(qk_full[:, n, :], ps_build[:, :], ACT.Identity,
                                           bias=g.qk_bias[:, 2 + n:3 + n]).then_inc(qk_full_done, 1)
                        b = batch(i, s - 3)
                        if k == 5 and b is not None:
                            act.wait_ge(y_norm_turned, upto(i, 2, b + 1))
                            act.wait_ge(projected, upto(i, 2, b))
                            act.activation(y_t[:, :], ps_build[:, :], ACT.Copy).then_inc(y_t_done, 1)
                        u = unit(i, s - 1)
                        if k == 3 and u is not None:
                            act.wait_ge(hist_done, upto(i, 4, u + 1))
                            act.wait_ge(y_turned, upto(i, 4, u))
                            act.activation(y_cols[:, :], ps_pv[:, :], ACT.Copy).then_inc(y_cols_done, 1)
                        u = unit(i, s + 1)
                        if u is not None:
                            for n in range(2 * k, min(2 * k + 2, FEATS)):
                                kind, m = TILE_OF[n]
                                src = ps_feat[(u + n) % 2]
                                if kind == KEY_TOK:
                                    dst = key_tok[:, u % 2, m, :]
                                    act.wait_ge(summed, upto(i, 12, 3 * (u - 1)))
                                elif kind == KEY_FEAT:
                                    dst = key_feat[:, ORDER[m], :]
                                    act.wait_ge(scored, upto(i, 32, HL * (u - 1) + m + 1))
                                else:
                                    dst = query_feat[:, u % 2, m, :]
                                    act.wait_ge(hist_done, upto(i, 4, u - 1))
                                act.wait_ge(feat_done, upto(i, 4 * FEATS, FEATS * u + n + 1))
                                act.activation(dst, src[:, :], ACT.Relu).then_inc(feat_out, 1)
                        b = batch(i, s + 3)
                        if k == 0 and b is not None:
                            act.wait_ge(xn_turned, upto(i, 2, b + 1))
                            act.wait_ge(v_done, upto(i, 2, b))
                            act.activation(xn_t[:, :], ps_build[:, :], ACT.Copy).then_inc(xn_t_done, 1)

                run(act, step)

            @block.vector
            def _(dve):
                def step(i, s):
                    for k in range(8):
                        u = unit(i, s)
                        if k in (4, 5, 6) and u is not None:
                            j = k - 4
                            dve.wait_ge(state_turned, upto(i, 12, 3 * u + j + 1))
                            dve.wait_ge(hist_done, upto(i, 4, u))
                            for r in range(2):
                                of_pairs = state[:, j, :].rearrange("p (q w) -> p q w", q=PU)
                                dve.tensor_tensor(of_pairs[:, :, 16 * r:16 * r + 16],
                                                  ps_turn[:, 128 * j:128 * j + 128].rearrange("p (q w) -> p q w", q=PU)
                                                  [:, :, 16 - 16 * r:32 - 16 * r],
                                                  g.pair_mask[:, 16 * r:16 * r + 16].unsqueeze(1)
                                                  .to_broadcast([128, PU, 16]), ALU.mult).then_inc(state_done, 1)
                        b = batch(i, s + 2)
                        if k == 4 and b is not None:
                            dve.wait_ge(v_done, upto(i, 2, b + 1))
                            dve.wait_ge(hist_done, upto(i, 4, 2 * (b - 1)))
                            src = ps_build[:, :].rearrange("p (j q r d) -> p j q r d", j=TILES, r=2, d=D)
                            bias = g.row_bias[:, 1, :].rearrange("p (q r d) -> p q r d", r=2, d=D)
                            for r in range(2):
                                at = 32 - 16 * r
                                dve.tensor_tensor(v_aug[b % 2][:, :, :, at:at + D], src[:, :, :, r, :],
                                                  bias[:, :, r, :].unsqueeze(1).to_broadcast([128, TILES, H // 2, D]),
                                                  ALU.add).then_inc(v_aug_done, 1)
                        v = unit(i, s - 2)
                        heads = ps_turn[:, :].rearrange("p (n w) -> p n w", w=16)
                        if k == 2 and v is not None:
                            dve.wait_ge(y_norm_done, upto(i, 4, v))
                            dve.wait_ge(y_recip_done, upto(i, 4, v + 1))
                            dve.wait_ge(y_norm_turned, upto(i, 2, v // 2))
                            f = v % 2
                            dve.tensor_tensor(y_norm[:, :, 64 * f:64 * f + 64].rearrange("p j (h d) -> p j h d", d=D),
                                              ps_turn[:, :].rearrange("p (j h w) -> p j h w", j=TILES, w=16)
                                              [:, :, :, 0:D],
                                              y_recip[:, :].rearrange("p (j h) -> p j h", j=TILES).unsqueeze(3)
                                              .to_broadcast([128, TILES, HL, D]), ALU.mult).then_inc(y_norm_done, 1)
                        if u is not None:
                            hl = ORDER[k]
                            dve.wait_ge(scored, upto(i, 32, HL * u + k + 1))
                            dve.wait_ge(within_done, upto(i, 8, 2 * (u - 1) + k // 4 + 1))
                            dve.tensor_tensor(attn[:, hl, :, :],
                                              ps_attn[k % 2][:, :].rearrange("p (j t) -> p j t", j=TILES),
                                              g.causal01[:, :].unsqueeze(1).to_broadcast([128, TILES, 128]),
                                              ALU.mult).then_inc(attn_done, 1)
                        if k == 0 and v is not None:
                            dve.wait_ge(y_turned, upto(i, 4, v + 1))
                            dve.tensor_scalar(y_sum[:, :], heads[:, :, D], DELTA, None, ALU.add).then_inc(y_sum_done, 1)
                        if k == 1 and v is not None:
                            dve.wait_ge(y_sum_done, upto(i, 4, v + 1))
                            dve.wait_ge(y_norm_done, upto(i, 4, v))
                            dve.reciprocal(y_recip[:, :], y_sum[:, :]).then_inc(y_recip_done, 1)
                        b = batch(i, s - 3)
                        if k == 7 and b is not None:
                            dve.wait_ge(projected, upto(i, 2, b + 1))
                            dve.wait_ge(x_added, upto(i, 2, b))
                            dve.tensor_tensor(y_out[:, :, :], ps_build[:, :].rearrange("p (j c) -> p j c", j=TILES),
                                              g.row_bias[:, 2, :].unsqueeze(1).to_broadcast([128, TILES, C]),
                                              ALU.add).then_inc(biased, 1)
                        b = batch(i, s + 3)
                        if k in (2, 3) and b is not None:
                            n = k - 2
                            dve.wait_ge(qk_full_done, upto(i, 4, 2 * b + n + 1))
                            for f in range(2):
                                dve.wait_ge(k_stacked[f], upto(i, 2 * 16 * STACK_DMAS, 16 * STACK_DMAS * (b - 1)))
                                dve.wait_ge(q_stacked[f], upto(i, 2 * 16 * STACK_DMAS, 16 * STACK_DMAS * (b - 1)))
                            dve.tensor_copy(parts[b % 2][:, n, 0, :], qk_full[:, n, :]).then_inc(top_done, 1)
                        if k in (3, 4) and b is not None:
                            n = k - 3
                            dve.wait_ge(left1_done, upto(i, 4, 2 * b + n + 1))
                            dve.tensor_copy(parts[b % 2][:, n, 1, :], qk_full[:, n, :]).then_inc(mid_done, 1)
                        b = batch(i, s + 4)
                        if k == 1 and b is not None:
                            emit_ln_stats(dve, g, i, b, ln_stats, ln_mv, stats_done, mv_done)
                        if k == 6 and b is not None:
                            dve.wait_ge(xn_turned, upto(i, 2, b))
                            emit_ln_apply(dve, g, i, b, xn, ln_mv, ln_rstd, rstd_done, xn_done)

                run(dve, step)

            @block.tensor
            def _(pe):
                def features(i, u, n):
                    bank, f = ps_feat[(u + n) % 2], u % 2
                    ks, qs = k_stack[u % 2], q_stack[u % 2]
                    if n == 0:
                        pe.wait_ge(k_stacked[f], upto(i, 2 * 16 * STACK_DMAS, 16 * STACK_DMAS * (u // 2 + 1)))
                    if n == TILE_OF.index((QUERY, 0)):
                        pe.wait_ge(q_stacked[f], upto(i, 2 * 16 * STACK_DMAS, 16 * STACK_DMAS * (u // 2 + 1)))
                    pe.wait_ge(feat_out, upto(i, 4 * FEATS, FEATS * u + n - 1))
                    kind, m = TILE_OF[n]
                    if kind == KEY_TOK:
                        for hl in range(HL):
                            last = pe.matmul(bank[:, M * hl:M * hl + M], ks[0:KROWS, hl, 128 * m:128 * m + 128],
                                             g.proj[:, HL * f + hl, M:2 * M], start=True, stop=True)
                    elif kind == KEY_FEAT:
                        hl = ORDER[m]
                        at = M * (1 - hl % 2)
                        last = pe.matmul(bank[:, :], g.proj[:, HL * f + hl, at:at + 2 * M], ks[0:KROWS, hl, :],
                                         start=True, stop=True)
                    else:
                        for r in range(2):
                            hl = 2 * m + r
                            last = pe.matmul(bank[M * r:M * r + M, :], g.proj[:, HL * f + hl, M:2 * M],
                                             qs[0:KROWS, hl, :], start=True, stop=True)
                    last.then_inc(feat_done, 1)

                def within(i, u, r):
                    f = u % 2
                    pe.wait_ge(attn_done, upto(i, 32, HL * u + 4 * r + 4))
                    if r == 0:
                        pe.wait_ge(y_cols_done, upto(i, 4, u))
                        pe.wait_ge(v_aug_done, upto(i, 4, 2 * (u // 2) + 2))
                    for j in range(TILES):
                        for c in range(PU):
                            last = pe.matmul(ps_pv[32 * c:32 * c + 32, 128 * j:128 * j + 128],
                                             v_aug[u // 2 % 2][:, j, PU * f + c, 32 - 32 * r:64 - 32 * r],
                                             attn[:, 2 * c + r, j, :],
                                             start=(r == 0 and j == 0), stop=False, skip_group_check=True)
                    last.then_inc(within_done, 1)

                def sums(i, u, j):
                    pe.wait_ge(state_cols_done, upto(i, 12, 3 * u + j))
                    if j == 0:
                        pe.wait_ge(v_aug_done, upto(i, 4, 2 * (u // 2) + 2))
                    for c in range(PU):
                        last = pe.matmul(ps_state[32 * c:32 * c + 32, 0:128],
                                         v_aug[u // 2 % 2][:, j, PU * (u % 2) + c, 16:48],
                                         key_tok[:, u % 2, j, 128 * c:128 * c + 128],
                                         start=(j == 0), stop=(j == TILES - 2), skip_group_check=True)
                    last.then_inc(summed, 1)

                def step(i, s):
                    for k in range(8):
                        b = batch(i, s + 3)
                        if k == 0 and b is not None:
                            pe.wait_ge(xn_done, upto(i, 2, b + 1))
                            pe.wait_ge(v_aug_done, upto(i, 4, 2 * b))
                            for j in range(TILES):
                                last = pe.transpose(ps_build[:, 128 * j:128 * j + 128], xn[:, j, :], g.ident[:, :])
                            last.then_inc(xn_turned, 1)
                        nxt = unit(i, s + 1)
                        u = unit(i, s)
                        if u is not None:
                            hl = ORDER[k]
                            tiles = max(TILE_OF.index((KEY_FEAT, k)), TILE_OF.index((QUERY, hl // 2))) + 1
                            pe.wait_ge(feat_out, upto(i, 4 * FEATS, FEATS * u + tiles))
                            pe.wait_ge(attn_done, upto(i, 32, HL * u + k - 1))
                            for j in range(TILES):
                                last = pe.matmul(ps_attn[k % 2][:, 128 * j:128 * j + 128],
                                                 key_feat[:, hl, 128 * j:128 * j + 128],
                                                 query_feat[:, u % 2, hl // 2, 128 * j:128 * j + 128],
                                                 start=True, stop=True)
                            last.then_inc(scored, 1)
                        v = unit(i, s - 1)
                        if k == 1 and v is not None:
                            within(i, v, 1)
                        if k == 2 and v is not None:
                            pe.wait_ge(state_done, upto(i, 24, 6 * v + 6))
                            for j in range(1, TILES):
                                for c in range(PU):
                                    last = pe.matmul(ps_pv[32 * c:32 * c + 32, 128 * j:128 * j + 128],
                                                     state[:, j - 1, 32 * c:32 * c + 32],
                                                     query_feat[:, v % 2, c, 128 * j:128 * j + 128],
                                                     start=False, stop=(j == TILES - 1), skip_group_check=True)
                            last.then_inc(hist_done, 1)
                        if k == 2 and u is not None:
                            sums(i, u, 0)
                        if nxt is not None:
                            for n in range(2 * k, min(2 * k + 2, FEATS)):
                                features(i, nxt, n)
                        if k in (3, 4, 5) and u is not None:
                            j = k - 3
                            if j < 2:
                                sums(i, u, j + 1)
                            pe.wait_ge(state_cols_done, upto(i, 12, 3 * u + j + 1))
                            pe.wait_ge(state_done, upto(i, 24, 2 * (3 * u + j)))
                            pe.wait_ge(y_norm_done, upto(i, 4, u - 1))
                            pe.transpose(ps_turn[:, 128 * j:128 * j + 128], state_cols[:, :], g.ident[:, :])\
                                .then_inc(state_turned, 1)
                        if k == 6 and u is not None:
                            within(i, u, 0)
                        if k == 7 and v is not None:
                            pe.wait_ge(y_cols_done, upto(i, 4, v + 1))
                            if u is not None:
                                pe.wait_ge(state_done, upto(i, 24, 6 * u + 6))
                            pe.wait_ge(y_norm_done, upto(i, 4, v))
                            for j in range(TILES):
                                last = pe.transpose(ps_turn[:, 128 * j:128 * j + 128], y_cols[:, 128 * j:128 * j + 128],
                                                    g.ident[:, :])
                            last.then_inc(y_turned, 1)
                        if k in (1, 2) and b is not None:
                            if k == 1:
                                pe.wait_ge(xn_t_done, upto(i, 2, b + 1))
                            else:
                                pe.wait_ge(qk_full_done, upto(i, 4, 2 * b + 1))
                            pe.matmul(ps_build[:, :], g.weights_t[:, 1 + k, :], xn_t[:, :], start=True, stop=True)\
                                .then_inc(qk_done, 1)
                        w = batch(i, s + 2)
                        if k == 3 and w is not None:
                            pe.wait_ge(qk_full_done, upto(i, 4, 2 * w + 2))
                            pe.wait_ge(biased, upto(i, 2, w - 2))
                            for j in range(TILES):
                                last = pe.matmul(ps_build[:, 128 * j:128 * j + 128], xn_t[:, 128 * j:128 * j + 128],
                                                 g.weights_t[:, 5, :], start=True, stop=True)
                            last.then_inc(v_done, 1)
                        o = batch(i, s - 3)
                        if k == 4 and o is not None:
                            pe.wait_ge(y_norm_done, upto(i, 4, 2 * o + 2))
                            if not (isinstance(i, int) and 2 * i + o + 3 >= NB):
                                pe.wait_ge(qk_full_done, upto(i, 4, 2 * (o + 3) + 2))
                            for j in range(TILES):
                                last = pe.transpose(ps_build[:, 128 * j:128 * j + 128], y_norm[:, j, :], g.ident[:, :])
                            last.then_inc(y_norm_turned, 1)
                        if k == 6 and o is not None:
                            pe.wait_ge(y_t_done, upto(i, 2, o + 1))
                            for j in range(TILES):
                                last = pe.matmul(ps_build[:, 128 * j:128 * j + 128], y_t[:, 128 * j:128 * j + 128],
                                                 g.weights_t[:, 6, :], start=True, stop=True)
                            last.then_inc(projected, 1)

                run(pe, step)


def x_slot(g, i, b):
    if isinstance(i, int):
        return g.x_all[:, 2 * i + b]
    return g.x_all[:, bass.ds(i * 2 + b, 1)].rearrange("p a j c -> p (a j) c")


def emit_ln_stats(dve, g, i, b, stats, mv, stats_done, mv_done):
    tile = x_slot(g, i, b)
    for j in range(TILES):
        last = dve.bn_stats(stats[:, j, :], tile[:, j, :])
    last.then_inc(stats_done, 1)
    dve.wait_ge(stats_done, upto(i, 2, b + 1))
    dve.sem_inc(g.passed_dve, 1)
    for j in range(TILES):
        last = dve.bn_aggr(mv[:, j, :], stats[:, j, :])
    last.then_inc(mv_done, 1)


def emit_ln_apply(dve, g, i, b, xn, mv, rstd, rstd_done, xn_done):
    tile = x_slot(g, i, b)
    dve.wait_ge(rstd_done, upto(i, 2, b + 1))
    for j in range(TILES):
        last = dve.tensor_scalar(xn[:, j, :], tile[:, j, :], mv[:, j, 0:1], rstd[:, j:j + 1],
                                 ALU.subtract, ALU.mult)
    last.then_inc(xn_done, 1)


def hybrid_kernel(nc, x, a_w, a_b, b_w, b_b, out_w, out_b, proj, router, gate, up, down, s_gate, s_up, s_down, out):
    src = Common()
    src.x_v = x.rearrange("b (j p) c -> p b j c", p=128)
    src.a_w, src.a_b, src.b_w, src.b_b, src.out_w, src.out_b = a_w, a_b, b_w, b_b, out_w, out_b
    src.proj, src.router, src.gate, src.up, src.down = proj, router, gate, up, down
    src.s_gate, src.s_up, src.s_down = s_gate, s_up, s_down
    with ExitStack() as ctx:
        g = allocate_common(nc, ctx)
        with ExitStack() as first:
            a = allocate_softmax_inputs(nc, first, g)
            emit_setup(nc, g, a, src)
            emit_softmax_attention(nc, g, a, src)
        with ExitStack() as third:
            values = allocate_linear_values(nc, third)
            emit_ffn(nc, g, 1, values=values)
            emit_linear_attention(nc, g, values)
        emit_ffn(nc, g, 3, out=out)


_INS = ['L0_attn_a_x', 'L0_attn_a_W', 'L0_attn_a_b', 'L0_attn_b_Wqkv', 'L0_attn_b_bqkv', 'L0_attn_b_Wout',
        'L0_attn_b_bout', 'L0_attn_b_proj', 'L0_ffn_router', 'L0_ffn_experts_gate', 'L0_ffn_experts_up',
        'L0_ffn_experts_down', 'L0_ffn_shared_gate', 'L0_ffn_shared_up', 'L0_ffn_shared_down']
_OUT_SHAPE = (NB, T, C)


def kernel(**inputs):
    import concourse.bacc as bacc
    from concourse.bass_utils import run_bass_kernel_spmd

    nc = bacc.Bacc("TRN2", target_bir_lowering=False, num_devices=1)
    arrays, args = {}, []
    for name in _INS:
        a = np.ascontiguousarray(inputs[name])
        arrays[f"in_{name}"] = a
        args.append(nc.dram_tensor(f"in_{name}", a.shape, mybir.dt.from_np(a.dtype), kind="ExternalInput").ap())
    args.append(nc.dram_tensor("out_x", _OUT_SHAPE, F32, kind="ExternalOutput").ap())
    hybrid_kernel(nc, *args)
    r = run_bass_kernel_spmd(nc, [arrays], core_ids=[0])
    return r.results[0]["out_x"]
```
